# Optimizing a Trainium2 kernel written in Bass

```python
import numpy as np
import jax
import jax.numpy as jnp

def _softmax(x, axis=-1):
    return jax.nn.softmax(x, axis=axis)

def _gelu(x):
    return jax.nn.gelu(x, approximate=True)

def _silu(x):
    return jax.nn.silu(x)

def _sigmoid(x):
    return jax.nn.sigmoid(x)

def _layernorm(x, axis=-1, eps=1e-05):
    m = jnp.mean(x, axis=axis, keepdims=True)
    v = jnp.var(x, axis=axis, keepdims=True)
    return (x - m) / jnp.sqrt(v + eps)

def _scatter_add(tgt, idx, src, axis=0):
    return tgt.at[idx].add(src)

def _segment_sum(src, seg, n):
    return jax.ops.segment_sum(src, seg, n)
kernel_name = 'mk_gnn_preln_d4_gnn_r8_b3effd'

def setup_inputs(seed: int=0):
    np.random.seed(seed)
    _w = jnp.asarray

    def _rec_inputs():
        import jax
        import jax.numpy as jnp
        _gk = jax.random.key(seed)
        x = -0.0005121 + 1.001 * jax.random.normal(jax.random.fold_in(_gk, 1), (12500, 32), jnp.float32)
        src = jax.random.randint(jax.random.fold_in(_gk, 2), (200000,), 0, 12500, jnp.int32)
        dst = jnp.minimum((12500 * jax.random.uniform(jax.random.fold_in(_gk, 3), (200000,)) ** 2.0).astype(jnp.int32), 99999)
        _o = jnp.argsort(dst, stable=True)
        src = src[_o]
        dst = dst[_o]
        edge_attr_10 = jax.random.uniform(jax.random.fold_in(_gk, 12), (200000, 10), jnp.float32, 0.0, 1)
        edge_attr_3 = 0.00109039 + 0.999626 * jax.random.normal(jax.random.fold_in(_gk, 13), (200000, 3), jnp.float32)
        edge_weight = jax.random.uniform(jax.random.fold_in(_gk, 15), (200000,), jnp.float32, 0.0, 0.999997)
        return (x, src, dst, edge_attr_10, edge_attr_3, edge_weight)
    x, src, dst, edge_attr_10, edge_attr_3, edge_weight = _rec_inputs()

    def _L0_gnn_setup():
        import jax, jax.numpy as jnp
        import numpy as np
        N_NODES = 12500
        N_EDGES = 200000
        DIM1 = 32
        LEAKY_SLOPE = 0.01
        key = jax.random.key(seed)
        k1, k2, k3, k4 = jax.random.split(key, 4)
        h = jax.random.normal(k1, (N_NODES, DIM1), dtype=jnp.float32)
        attn_w = jax.random.normal(k2, (2 * DIM1,), dtype=jnp.float32) * (1.0 / np.sqrt(2 * DIM1))
        src = jax.random.randint(k3, (N_EDGES,), 0, N_NODES, dtype=jnp.int32)
        dst = jax.random.randint(k4, (N_EDGES,), 0, N_NODES, dtype=jnp.int32)
        return {'h': h, 'attn_w': attn_w, 'src': src, 'dst': dst}
    _L0_gnn_all = _L0_gnn_setup()
    _L0_gnn_in = {k: v for k, v in _L0_gnn_all.items() if k in ('attn_w',)}
    del _L0_gnn_all

    def _L1_gnn_setup():
        import jax, jax.numpy as jnp
        import numpy as np
        N_NODES = 6250
        DEG = 16
        N_HEAD = 4
        F_IN = 32
        F_OUT = 32
        key = jax.random.key(seed)
        k_h, k_w, k_fw, k_fb = jax.random.split(key, 4)
        h = jax.random.normal(k_h, (N_NODES, F_IN), dtype=jnp.float32)
        src = jnp.repeat(jnp.arange(N_NODES, dtype=jnp.int64), DEG)
        offs = (jnp.arange(DEG, dtype=jnp.int64) + 1) * 97
        dst = (src.reshape(N_NODES, DEG) + offs[None, :]).reshape(-1) % N_NODES
        edge_index = jnp.stack([src, dst], axis=0)
        gain = 1.414
        bound_w = gain * np.sqrt(6.0 / (F_IN + F_OUT))
        w = jax.random.uniform(k_w, (N_HEAD, F_IN, F_OUT), jnp.float32, -bound_w, bound_w)
        bound_fc = np.sqrt(1.0 / (2 * F_OUT))
        fc_w = jax.random.uniform(k_fw, (1, 2 * F_OUT), jnp.float32, -bound_fc, bound_fc)
        fc_b = jax.random.uniform(k_fb, (1,), jnp.float32, -bound_fc, bound_fc)
        bias = jnp.zeros((F_OUT,), jnp.float32)
        return {'h': h, 'edge_index': edge_index, 'w': w, 'fc_w': fc_w, 'fc_b': fc_b, 'bias': bias}
    _L1_gnn_all = _L1_gnn_setup()
    _L1_gnn_in = {k: v for k, v in _L1_gnn_all.items() if k in ('w', 'fc_w', 'fc_b', 'bias')}
    del _L1_gnn_all

    def _L2_gnn_setup():
        import jax, jax.numpy as jnp
        import numpy as np
        MUL = 16
        MOUT = 8
        TANH_GAIN = 1.593
        INV_SQRT3 = 0.5773502691896258
        PW_S = 0.17677669529663687
        PW_V = 0.25

        def _w3j_121():
            s2, s6 = (2 ** 0.5, 6 ** 0.5)
            M = np.zeros((5, 3, 3))
            M[0, 0, 1] = M[0, 1, 0] = 1 / s2
            M[1, 1, 2] = M[1, 2, 1] = 1 / s2
            M[2] = np.diag([-1.0, -1.0, 2.0]) / s6
            M[3, 0, 2] = M[3, 2, 0] = 1 / s2
            M[4] = np.diag([1.0, -1.0, 0.0]) / s2
            return jnp.asarray(np.transpose(M, (1, 0, 2)) / 5 ** 0.5, jnp.float32)
        W3J121 = _w3j_121()

        def _sph(edge_vec):
            n = edge_vec / jnp.linalg.norm(edge_vec, axis=1, keepdims=True)
            x, y, z = (n[:, 0], n[:, 1], n[:, 2])
            y1 = 3.0 ** 0.5 * n
            s15 = 15.0 ** 0.5
            y2 = jnp.stack([s15 * x * y, s15 * y * z, 5.0 ** 0.5 / 2 * (3 * z * z - 1), s15 * x * z, s15 / 2 * (x * x - y * y)], axis=1)
            return (y1, y2)

        def _forward(x, edge_src, edge_dst, edge_vec, emb, norm, W1, W2):
            N, E = (x.shape[0], edge_src.shape[0])
            xs = jnp.concatenate([x[edge_src, :8], x[edge_dst, :8]], axis=1)
            xv = jnp.concatenate([x[edge_src, 8:].reshape(E, 8, 3), x[edge_dst, 8:].reshape(E, 8, 3)], axis=1)
            y1, y2 = _sph(edge_vec)
            h = 2.0 ** 0.5 * jax.nn.relu(emb @ W1 / 10.0 ** 0.5)
            w = (h @ W2 / 16.0 ** 0.5).reshape(E, 7, MUL, MOUT)
            wa_s, wb_s, wa_g, wb_g, wc, wd, we = [w[:, i] for i in range(7)]
            s_out = PW_S * (jnp.einsum('eu,euw->ew', xs, wa_s) + INV_SQRT3 * jnp.einsum('eui,ei,euw->ew', xv, y1, wb_s))
            g_out = PW_S * (jnp.einsum('eu,euw->ew', xs, wa_g) + INV_SQRT3 * jnp.einsum('eui,ei,euw->ew', xv, y1, wb_g))
            v_out = PW_V * (INV_SQRT3 * jnp.einsum('eu,ek,euw->ewk', xs, y1, wc) + INV_SQRT3 * jnp.einsum('eui,euw->ewi', xv, wd) + jnp.einsum('eui,ea,iak,euw->ewk', xv, y2, W3J121, we))
            s_act = TANH_GAIN * jnp.tanh(s_out)
            gates = TANH_GAIN * jnp.tanh(g_out)
            edge_ftr = jnp.concatenate([s_act, (gates[:, :, None] * v_out).reshape(E, 24)], axis=1) * norm[:, None]
            return jax.ops.segment_sum(edge_ftr, edge_dst, num_segments=N)
        key = jax.random.key(seed)
        ks = jax.random.split(key, 8)
        N, E = (6250, 37500)
        return {'x': jax.random.normal(ks[0], (N, 32), jnp.float32), 'edge_src': jax.random.randint(ks[1], (E,), 0, N), 'edge_dst': jax.random.randint(ks[2], (E,), 0, N), 'edge_vec': jax.random.normal(ks[3], (E, 3), jnp.float32), 'emb': jax.random.uniform(ks[4], (E, 10), jnp.float32), 'norm': jax.random.uniform(ks[5], (E,), jnp.float32), 'W1': jax.random.normal(ks[6], (10, 16), jnp.float32), 'W2': jax.random.normal(ks[7], (16, 896), jnp.float32)}
    _L2_gnn_all = _L2_gnn_setup()
    _L2_gnn_in = {k: v for k, v in _L2_gnn_all.items() if k in ('W1', 'W2')}
    del _L2_gnn_all

    def _L3_gnn_setup():
        import jax, jax.numpy as jnp
        import numpy as np
        N_NODES = 6250
        N_EDGES = 100000
        C_IN = 32
        C_OUT = 32
        BN_EPS = 1e-05

        def batch_norm(h, gamma, beta):
            mean = jnp.mean(h, axis=0)
            var = jnp.mean((h - mean) ** 2, axis=0)
            return (h - mean) * jax.lax.rsqrt(var + BN_EPS) * gamma + beta
        key = jax.random.key(seed)
        ks = jax.random.split(key, 8)
        x = jax.random.normal(ks[0], (N_NODES, C_IN), dtype=jnp.float32)
        edge_index = jax.random.randint(ks[1], (2, N_EDGES), 0, N_NODES, dtype=jnp.int64)
        s1 = 1.0 / np.sqrt(2 * C_IN)
        s2 = 1.0 / np.sqrt(C_OUT)
        W1 = jax.random.uniform(ks[2], (2 * C_IN, C_OUT), jnp.float32, -s1, s1)
        b1 = jax.random.uniform(ks[3], (C_OUT,), jnp.float32, -s1, s1)
        W2 = jax.random.uniform(ks[4], (C_OUT, C_OUT), jnp.float32, -s2, s2)
        b2 = jax.random.uniform(ks[5], (C_OUT,), jnp.float32, -s2, s2)
        gamma1 = jnp.ones((C_OUT,), jnp.float32)
        beta1 = jnp.zeros((C_OUT,), jnp.float32)
        gamma2 = jnp.ones((C_OUT,), jnp.float32)
        beta2 = jnp.zeros((C_OUT,), jnp.float32)
        return {'x': x, 'W1': W1, 'b1': b1, 'gamma1': gamma1, 'beta1': beta1, 'W2': W2, 'b2': b2, 'gamma2': gamma2, 'beta2': beta2, 'edge_index': edge_index}
    _L3_gnn_all = _L3_gnn_setup()
    _L3_gnn_in = {k: v for k, v in _L3_gnn_all.items() if k in ('W1', 'b1', 'gamma1', 'beta1', 'W2', 'b2', 'gamma2', 'beta2')}
    del _L3_gnn_all
    return {'x': x, 'src': src, 'dst': dst, 'edge_attr_10': edge_attr_10, 'edge_attr_3': edge_attr_3, 'edge_weight': edge_weight, 'L0_gnn_attn_w': _L0_gnn_in['attn_w'], 'L1_gnn_w': _L1_gnn_in['w'], 'L1_gnn_fc_w': _L1_gnn_in['fc_w'], 'L1_gnn_fc_b': _L1_gnn_in['fc_b'], 'L1_gnn_bias': _L1_gnn_in['bias'], 'L2_gnn_W1': _L2_gnn_in['W1'], 'L2_gnn_W2': _L2_gnn_in['W2'], 'L3_gnn_W1': _L3_gnn_in['W1'], 'L3_gnn_b1': _L3_gnn_in['b1'], 'L3_gnn_gamma1': _L3_gnn_in['gamma1'], 'L3_gnn_beta1': _L3_gnn_in['beta1'], 'L3_gnn_W2': _L3_gnn_in['W2'], 'L3_gnn_b2': _L3_gnn_in['b2'], 'L3_gnn_gamma2': _L3_gnn_in['gamma2'], 'L3_gnn_beta2': _L3_gnn_in['beta2']}

def reference(x, src, dst, edge_attr_10, edge_attr_3, edge_weight, L0_gnn_attn_w, L1_gnn_w, L1_gnn_fc_w, L1_gnn_fc_b, L1_gnn_bias, L2_gnn_W1, L2_gnn_W2, L3_gnn_W1, L3_gnn_b1, L3_gnn_gamma1, L3_gnn_beta1, L3_gnn_W2, L3_gnn_b2, L3_gnn_gamma2, L3_gnn_beta2):
    import jax
    import jax.numpy as jnp

    def _L0_gnn_ref(h, attn_w, src, dst):
        import jax, jax.numpy as jnp
        import numpy as np
        N_NODES = 12500
        N_EDGES = 200000
        DIM1 = 32
        LEAKY_SLOPE = 0.01
        N, d = h.shape
        s_src = h @ attn_w[:d]
        s_dst = h @ attn_w[d:]
        e = s_src[src] + s_dst[dst]
        e = jnp.where(e >= 0, e, LEAKY_SLOPE * e)
        m = jax.ops.segment_max(e, dst, num_segments=N)
        ex = jnp.exp(e - m[dst])
        denom = jax.ops.segment_sum(ex, dst, num_segments=N)
        alpha = ex / denom[dst]
        out = jax.ops.segment_sum(h[src] * alpha[:, None], dst, num_segments=N)
        return out

    def _L1_gnn_ref(h, edge_index, w, fc_w, fc_b, bias):
        import jax, jax.numpy as jnp
        import numpy as np
        N_NODES = 6250
        DEG = 16
        N_HEAD = 4
        F_IN = 32
        F_OUT = 32
        n_head, f_in, f_out = w.shape
        n = h.shape[0]
        src, dst = (edge_index[0], edge_index[1])
        hp = jnp.einsum('nf,hfo->hno', h, w)
        w_src = fc_w[0, :f_out]
        w_dst = fc_w[0, f_out:]
        a_src = jnp.einsum('hnf,f->hn', hp, w_src)
        a_dst = jnp.einsum('hnf,f->hn', hp, w_dst)
        e = a_src[:, src] + a_dst[:, dst] + fc_b[0]
        e = jax.nn.leaky_relu(e, negative_slope=0.2)
        seg_max = jax.ops.segment_max(e.T, src, num_segments=n)
        e = jnp.exp(e - seg_max.T[:, src])
        seg_sum = jax.ops.segment_sum(e.T, src, num_segments=n)
        att = e / seg_sum.T[:, src]
        msg = att[:, :, None] * hp[:, dst, :]
        agg = jax.vmap(lambda m: jax.ops.segment_sum(m, src, num_segments=n))(msg)
        out = agg.mean(axis=0) + bias
        return out

    def _L2_gnn_ref(x, edge_src, edge_dst, edge_vec, emb, norm, W1, W2):
        import jax, jax.numpy as jnp
        import numpy as np
        MUL = 16
        MOUT = 8
        TANH_GAIN = 1.593
        INV_SQRT3 = 0.5773502691896258
        PW_S = 0.17677669529663687
        PW_V = 0.25

        def _w3j_121():
            s2, s6 = (2 ** 0.5, 6 ** 0.5)
            M = np.zeros((5, 3, 3))
            M[0, 0, 1] = M[0, 1, 0] = 1 / s2
            M[1, 1, 2] = M[1, 2, 1] = 1 / s2
            M[2] = np.diag([-1.0, -1.0, 2.0]) / s6
            M[3, 0, 2] = M[3, 2, 0] = 1 / s2
            M[4] = np.diag([1.0, -1.0, 0.0]) / s2
            return jnp.asarray(np.transpose(M, (1, 0, 2)) / 5 ** 0.5, jnp.float32)
        W3J121 = _w3j_121()

        def _sph(edge_vec):
            n = edge_vec / jnp.linalg.norm(edge_vec, axis=1, keepdims=True)
            x, y, z = (n[:, 0], n[:, 1], n[:, 2])
            y1 = 3.0 ** 0.5 * n
            s15 = 15.0 ** 0.5
            y2 = jnp.stack([s15 * x * y, s15 * y * z, 5.0 ** 0.5 / 2 * (3 * z * z - 1), s15 * x * z, s15 / 2 * (x * x - y * y)], axis=1)
            return (y1, y2)

        def _forward(x, edge_src, edge_dst, edge_vec, emb, norm, W1, W2):
            N, E = (x.shape[0], edge_src.shape[0])
            xs = jnp.concatenate([x[edge_src, :8], x[edge_dst, :8]], axis=1)
            xv = jnp.concatenate([x[edge_src, 8:].reshape(E, 8, 3), x[edge_dst, 8:].reshape(E, 8, 3)], axis=1)
            y1, y2 = _sph(edge_vec)
            h = 2.0 ** 0.5 * jax.nn.relu(emb @ W1 / 10.0 ** 0.5)
            w = (h @ W2 / 16.0 ** 0.5).reshape(E, 7, MUL, MOUT)
            wa_s, wb_s, wa_g, wb_g, wc, wd, we = [w[:, i] for i in range(7)]
            s_out = PW_S * (jnp.einsum('eu,euw->ew', xs, wa_s) + INV_SQRT3 * jnp.einsum('eui,ei,euw->ew', xv, y1, wb_s))
            g_out = PW_S * (jnp.einsum('eu,euw->ew', xs, wa_g) + INV_SQRT3 * jnp.einsum('eui,ei,euw->ew', xv, y1, wb_g))
            v_out = PW_V * (INV_SQRT3 * jnp.einsum('eu,ek,euw->ewk', xs, y1, wc) + INV_SQRT3 * jnp.einsum('eui,euw->ewi', xv, wd) + jnp.einsum('eui,ea,iak,euw->ewk', xv, y2, W3J121, we))
            s_act = TANH_GAIN * jnp.tanh(s_out)
            gates = TANH_GAIN * jnp.tanh(g_out)
            edge_ftr = jnp.concatenate([s_act, (gates[:, :, None] * v_out).reshape(E, 24)], axis=1) * norm[:, None]
            return jax.ops.segment_sum(edge_ftr, edge_dst, num_segments=N)
        return _forward(x, edge_src, edge_dst, edge_vec, emb, norm, W1, W2)

    def _L3_gnn_ref(x, W1, b1, gamma1, beta1, W2, b2, gamma2, beta2, edge_index):
        import jax, jax.numpy as jnp
        import numpy as np
        N_NODES = 6250
        N_EDGES = 100000
        C_IN = 32
        C_OUT = 32
        BN_EPS = 1e-05

        def batch_norm(h, gamma, beta):
            mean = jnp.mean(h, axis=0)
            var = jnp.mean((h - mean) ** 2, axis=0)
            return (h - mean) * jax.lax.rsqrt(var + BN_EPS) * gamma + beta
        row, col = (edge_index[0], edge_index[1])
        ef = jnp.concatenate([x[row], x[col]], axis=-1)
        h = jax.nn.relu(batch_norm(ef @ W1 + b1, gamma1, beta1))
        h = jax.nn.relu(batch_norm(h @ W2 + b2, gamma2, beta2))
        out = jax.ops.segment_sum(h, row, num_segments=x.shape[0])
        return out
    edge_index = jnp.stack([src, dst])
    h = jnp.maximum(_layernorm(x, axis=-1), 0.0)
    x = x + _L0_gnn_ref(h, L0_gnn_attn_w, src, dst)
    h = jnp.maximum(_layernorm(x, axis=-1), 0.0)
    x = x + _L1_gnn_ref(h, edge_index, L1_gnn_w, L1_gnn_fc_w, L1_gnn_fc_b, L1_gnn_bias)
    h = jnp.maximum(_layernorm(x, axis=-1), 0.0)
    x = x + _L2_gnn_ref(h, src, dst, edge_attr_3, edge_attr_10, edge_weight, L2_gnn_W1, L2_gnn_W2)
    h = jnp.maximum(_layernorm(x, axis=-1), 0.0)
    x = x + _L3_gnn_ref(h, L3_gnn_W1, L3_gnn_b1, L3_gnn_gamma1, L3_gnn_beta1, L3_gnn_W2, L3_gnn_b2, L3_gnn_gamma2, L3_gnn_beta2, edge_index)
    return x

_drawn_inputs = setup_inputs


def setup_inputs(seed=0):
    import zlib

    import numpy as np

    out = dict(_drawn_inputs(seed))
    spreads = {'L1_gnn_bias': (0.0, 0.1),
     'L3_gnn_gamma1': (1.0, 0.2),
     'L3_gnn_beta1': (0.0, 0.1),
     'L3_gnn_gamma2': (1.0, 0.2),
     'L3_gnn_beta2': (0.0, 0.1)}
    factors = {'L0_gnn_attn_w': 4.259, 'L3_gnn_b1': 8.0, 'L3_gnn_b2': 8.0}
    for name, (base, spread) in spreads.items():
        noise = np.random.default_rng([zlib.crc32(name.encode()), seed]).standard_normal(out[name].shape)
        drawn = base * np.exp(spread * noise) if base else spread * noise
        out[name] = jnp.asarray(drawn.astype(out[name].dtype))
    for name, factor in factors.items():
        out[name] = (out[name] * factor).astype(out[name].dtype)
    return out
```

```python
import math
from contextlib import ExitStack

import concourse.bass as bass
from concourse import mybir

ALU = mybir.AluOpType
ACT = mybir.ActivationFunctionType
AX = mybir.AxisListType
F32 = mybir.dt.float32
BF16 = mybir.dt.bfloat16
I32 = mybir.dt.int32

P = 128
N, E, D = 12500, 200000, 32
EC = 1568
EP = P * EC
NPAD = EP - E
NC_ = 98
NN = P * NC_
NB = -(-NC_ // 4)
HI = NN // P
SG = 28
STAGES = EC // SG
RT = 16
NEG = -3.0e38
HEADS = 4
LN_EPS = 1e-5


class Kit:
    pass


def phase(nc, name):
    return Phase(nc, name)


class Phase:

    def __init__(self, nc, name):
        self.nc, self.name, self.stack, self.sems = nc, name, ExitStack(), []

    def __enter__(self):
        self.stack.__enter__()
        return self

    def sb(self, name, shape, dt=F32):
        return self.stack.enter_context(self.nc.sbuf_tensor(f"{self.name}_{name}", shape, dt))

    def ps(self, name, shape, dt=F32):
        return self.stack.enter_context(self.nc.psum_tensor(f"{self.name}_{name}", shape, dt))

    def sem(self, name):
        s = self.nc.alloc_semaphore(f"{self.name}_{name}")
        self.sems.append(s)
        return s

    def __exit__(self, *a):
        if a[0] is None:
            self.nc.clear_and_free_semaphores(self.sems)
            self.nc.all_engine_barrier()
        return self.stack.__exit__(*a)


class Steps:

    def __init__(self, eng, sem):
        self.eng, self.sem, self.n, self.base = eng, sem, 0, 0

    def did(self, ins):
        ins.then_inc(self.sem, 1)
        self.n += 1

    def settle(self):
        self.eng.wait_ge(self.sem, self.base + self.n)

    def step(self, ins):
        self.did(ins)
        self.settle()

    def loop(self, i, per):
        self.outer, self.per = self.n, per
        self.base = i * per

    def end_loop(self, times):
        assert self.n - self.outer == self.per, (self.n - self.outer, self.per)
        self.n, self.base = self.outer + self.per * times, 0



def setup(nc, K):
    with phase(nc, "setup") as ph:
        padi = ph.sb("padi", [64, NPAD // 64], I32)
        padf = ph.sb("padf", [64, NPAD // 64 * 10])
        s_const, s_copy, s_x, s_sel = ph.sem("const"), ph.sem("copy"), ph.sem("x"), ph.sem("sel")
        with nc.Block() as block:

            @block.vector
            def _(v):
                v.memset(padi[:], N).then_inc(s_const, 1)
                v.memset(padf[:], 1.0).then_inc(s_const, 1)
                v.memset(K.X[:], 0.0).then_inc(s_const, 1)
                v.memset(K.H[:], 0.0).then_inc(s_const, 1)

            @block.gpsimd
            def _(g):
                g.memset(K.ident[:], 0.0).then_inc(s_sel, 1)
                g.memset(K.tri[:], 1.0).then_inc(s_sel, 1)
                g.iota(K.pcol_i[:], [[0, 1]], 0, 1).then_inc(s_sel, 1)
                g.iota(K.lane_i[:], [[1, P]], 0, 0).then_inc(s_sel, 1)
                g.wait_ge(s_sel, 4)
                g.affine_select(out=K.ident[:], in_=K.ident[:], compare_op=ALU.not_equal, fill=1.0,
                                base=0, pattern=[[-1, P]], channel_multiplier=1).then_inc(s_sel, 1)
                g.affine_select(out=K.tri[:], in_=K.tri[:], compare_op=ALU.is_gt, fill=0.0,
                                base=0, pattern=[[-1, P]], channel_multiplier=1).then_inc(s_sel, 1)
                g.tensor_copy(K.pcol[:], K.pcol_i[:]).then_inc(s_sel, 1)
                g.tensor_copy(K.lane[:], K.lane_i[:]).then_inc(s_sel, 1)
                g.tensor_copy(K.lane_b[:], K.lane_i[:]).then_inc(s_sel, 1)
                g.wait_ge(s_sel, 9)

            @block.sync
            def _(sp):
                n = 0

                def copy(dst, src):
                    nonlocal n
                    sp.dma_start(dst, src).then_inc(s_copy, 16)
                    n += 16

                copy(K.src[0:E].rearrange("(a b) -> a b", a=64), K.in_src.rearrange("(a b) -> a b", a=64))
                copy(K.dst[0:E].rearrange("(a b) -> a b", a=64), K.in_dst.rearrange("(a b) -> a b", a=64))
                copy(K.emb[0:E * 10].rearrange("(a b) -> a b", a=128), K.in_emb.rearrange("e w -> (e w)").rearrange("(a b) -> a b", a=128))
                copy(K.vec[0:E * 3].rearrange("(a b) -> a b", a=64), K.in_vec.rearrange("e w -> (e w)").rearrange("(a b) -> a b", a=64))
                copy(K.nrm[0:E].rearrange("(a b) -> a b", a=64), K.in_nrm.rearrange("(a b) -> a b", a=64))
                sp.wait_ge(s_const, 2)
                c = NPAD // 64
                copy(K.src[E:EP].rearrange("(a b) -> a b", a=64), padi[:])
                copy(K.dst[E:EP].rearrange("(a b) -> a b", a=64), padi[:])
                copy(K.emb[E * 10:EP * 10].rearrange("(a b) -> a b", a=64), padf[:])
                copy(K.vec[E * 3:EP * 3].rearrange("(a b) -> a b", a=64), padf[:, 0:3 * c])
                copy(K.nrm[E:EP].rearrange("(a b) -> a b", a=64), padf[:, 0:c])
                sp.wait_ge(s_copy, n)

            @block.scalar
            def _(act):
                act.wait_ge(s_const, 4)
                n = 0
                rows = N // NC_
                xf = K.in_x.rearrange("n d -> (n d)")
                for a, b in ((0, 112), (112, rows)):
                    act.dma_start(K.X[a:b, :], xf[a * NC_ * D:b * NC_ * D].rearrange("(p f) -> p f", p=b - a)).then_inc(s_x, 16)
                    n += 16
                left = (N - rows * NC_) * D
                act.dma_start(K.X[rows:rows + 1, 0:left], xf[rows * NC_ * D:N * D].rearrange("(p f) -> p f", p=1)).then_inc(s_x, 16)
                act.wait_ge(s_x, n + 16)


def load_keys(nc, K):
    with phase(nc, "keys") as ph:
        ki = ph.sb("ki", [P, 2, EC], I32)
        t = ph.sb("t", [P, EC], I32)
        lo = ph.sb("lo", [P, EC], I32)
        hi_f = ph.sb("hi_f", [P, EC])
        prev = ph.sb("prev", [P, 1], I32)
        prev_f = ph.sb("prev_f", [P, 1])
        kT = ph.sb("kT", [112, 14, P])
        hT = ph.sb("hT", [112, 14, P], BF16)
        pt = [ph.ps(f"pt{i}", [112, 2, P]) for i in range(2)]
        s_in, s_own, s_tr, s_ev, s_out, s_m = (ph.sem(x) for x in ("in", "own", "tr", "ev", "out", "m"))
        with nc.Block() as block:

            @block.sync
            def _(sp):
                sp.dma_start(ki[:, 0, :], K.src.rearrange("(p c) -> p c", p=P)).then_inc(s_in, 16)
                sp.dma_start(ki[:, 1, :], K.dst.rearrange("(p c) -> p c", p=P)).then_inc(s_in, 16)
                sp.wait_ge(s_m, 1)
                sp.dma_start(prev[1:P, :], K.dst.rearrange("(p c) -> p c", p=P)[0:P - 1, EC - 1:EC],
                             allow_slow_non_contiguous=True).then_inc(s_in, 16)
                sp.wait_ge(s_ev, 28)
                sp.dma_start(K.key_rows.rearrange("(b c p) -> c b p", c=112, p=P), kT[:]).then_inc(s_out, 16)
                sp.dma_start(K.hi_rows.rearrange("(b c p) -> c b p", c=112, p=P), hT[:]).then_inc(s_out, 16)
                sp.wait_ge(s_out, 32)

            @block.vector
            def _(v):
                st = Steps(v, s_own)
                v.memset(prev[:], -1).then_inc(s_m, 1)
                v.wait_ge(s_in, 48)
                st.did(v.tensor_copy(K.src_f[:], ki[:, 0, :]))
                st.did(v.tensor_copy(K.dst_f[:], ki[:, 1, :]))
                st.did(v.tensor_copy(prev_f[:], prev[:]))
                st.did(v.tensor_copy(K.o_d.first_i[:], ki[:, 1, 0:1]))
                for n, (hb, lb) in enumerate(((K.src_hi, K.src_lo), (K.dst_hi, K.dst_lo))):
                    st.step(v.tensor_scalar(t[:], ki[:, n, :], 7, None, ALU.logical_shift_right))
                    st.step(v.tensor_scalar(lo[:], ki[:, n, :], P - 1, None, ALU.bitwise_and))
                    st.did(v.tensor_copy(hb[:], t[:]))
                    if n == 0:
                        st.did(v.tensor_copy(hi_f[:], t[:]))
                    st.step(v.tensor_copy(lb[:], lo[:]))
                st.did(v.tensor_tensor(K.keep_d[:, 1:EC], K.dst_f[:, 1:EC], K.dst_f[:, 0:EC - 1], ALU.is_equal))
                st.did(v.tensor_tensor(K.keep_d[:, 0:1], K.dst_f[:, 0:1], prev_f[:], ALU.is_equal))
                st.settle()
                for b in range(14):
                    v.wait_ge(s_tr, b + 1)
                    v.tensor_copy(kT[:, b, :], pt[b % 2][:, 0, :]).then_inc(s_ev, 1)
                    v.tensor_copy(hT[:, b, :], pt[b % 2][:, 1, :]).then_inc(s_ev, 1)

            @block.tensor
            def _(pe):
                pe.wait_ge(s_own, 11)
                for b in range(14):
                    if b >= 2:
                        pe.wait_ge(s_ev, 2 * (b - 1))
                    pe.transpose(pt[b % 2][:, 0, :], K.src_f[:, 112 * b:112 * b + 112], K.ident[:])
                    pe.transpose(pt[b % 2][:, 1, :], hi_f[:, 112 * b:112 * b + 112], K.ident[:]).then_inc(s_tr, 1)



def one_hots(v, K, out_lo, out_hi, lo, hi, col):
    v_lo = lo[:, bass.ds(col, RT)].unsqueeze(2).to_broadcast([P, RT, P])
    v_hi = hi[:, bass.ds(col, RT)].unsqueeze(2).to_broadcast([P, RT, HI])
    lane = K.lane_b[:].unsqueeze(1).to_broadcast([P, RT, P])
    a = v.tensor_tensor(out_lo, v_lo, lane, ALU.is_equal)
    b = v.tensor_tensor(out_hi, v_hi, lane[:, :, 0:HI], ALU.is_equal)
    return a, b


class Histogram:

    def __init__(self, nc, K, ph, name, lo, hi, start_out, end_out, start_sb):
        self.nc, self.K, self.ph, self.name, self.lo, self.hi, self.start_out, self.end_out, self.start_sb = nc, K, ph, name, lo, hi, start_out, end_out, start_sb
        self.oh_lo = [ph.sb(f"{name}_oh_lo{k}", [P, RT, P], BF16) for k in range(2)]
        self.oh_hi = [ph.sb(f"{name}_oh_hi{k}", [P, RT, HI], BF16) for k in range(2)]
        self.cnt = ph.ps(f"{name}_cnt", [HI, P])
        self.off = ph.ps(f"{name}_off", [HI, 1])
        self.cnt_sb = ph.sb(f"{name}_cnt_sb", [HI, P])
        self.incl = ph.sb(f"{name}_incl", [HI, P])
        self.end_sb = ph.sb(f"{name}_end_sb", [HI, P])
        self.ones = ph.sb(f"{name}_ones", [HI, P])
        self.tri_t = ph.sb(f"{name}_tri_t", [HI, HI])
        self.s_oh = [ph.sem(f"{name}_oh{k}") for k in range(2)]
        self.s_used = [ph.sem(f"{name}_used{k}") for k in range(2)]
        self.s_zero, self.s_cnt, self.s_own, self.s_tot, self.s_off, self.s_done, self.s_out = (
            ph.sem(f"{name}_{x}") for x in ("zero", "cnt", "own", "tot", "off", "done", "out"))

    def vector(self, v):
        S = self
        for k in range(2):
            v.sem_inc(S.s_used[k], 1)
        st = Steps(v, S.s_own)
        v.memset(S.end_sb[:], 0.0).then_inc(S.s_zero, 1)
        st.did(v.memset(S.ones[:], 1.0))
        st.did(v.tensor_scalar(S.tri_t[:], S.K.lane[0:HI, 0:HI], S.K.pcol[0:HI, :], None, ALU.is_gt))
        with v.Fori(0, EC // RT // 2) as i:
            for k in range(2):
                v.wait_ge(S.s_used[k], i + 1)
                a, b = one_hots(v, S.K, S.oh_lo[k][:], S.oh_hi[k][:], S.lo, S.hi, (i * 2 + k) * RT)
                a.then_inc(S.s_oh[k], 1)
                b.then_inc(S.s_oh[k], 1)
        v.wait_ge(S.s_cnt, 1)
        st.step(v.tensor_copy(S.cnt_sb[:], S.cnt[:]))
        st.step(v.tensor_tensor_scan(S.incl[:], S.ones[:], S.cnt_sb[:], 0.0, ALU.mult, ALU.add))
        v.sem_inc(S.s_tot, 1)
        v.wait_ge(S.s_off, 1)
        st.step(v.tensor_scalar(S.end_sb[:], S.incl[:], S.off[:, 0:1], None, ALU.add))
        v.tensor_tensor(S.start_sb[:], S.end_sb[:], S.cnt_sb[:], ALU.subtract).then_inc(S.s_done, 1)

    def tensor(self, pe):
        S = self
        pe.wait_ge(S.s_zero, 1)
        pe.matmul(S.cnt[:], S.end_sb[:, 0:HI], S.end_sb[:], start=True, stop=False, skip_group_check=True)
        with pe.Fori(0, EC // RT // 2) as i:
            for k in range(2):
                pe.wait_ge(S.s_oh[k], i * 2 + 2)
                for j in range(RT):
                    mm = pe.matmul(S.cnt[:], S.oh_hi[k][:, j, :], S.oh_lo[k][:, j, :], start=False, stop=False,
                                   skip_group_check=True)
                mm.then_inc(S.s_used[k], 1)
        pe.matmul(S.cnt[:], S.ones[:, 0:HI], S.end_sb[:], start=False, stop=True, skip_group_check=True).then_inc(S.s_cnt, 1)
        pe.wait_ge(S.s_tot, 1)
        pe.matmul(S.off[:], S.tri_t[:], S.incl[:, P - 1:P], start=True, stop=True).then_inc(S.s_off, 1)

    def store(self, q):
        S = self
        q.wait_ge(S.s_done, 1)
        q.dma_start(S.start_out.rearrange("(h l) -> h l", l=P), S.start_sb[:]).then_inc(S.s_out, 16)
        q.dma_start(S.end_out.rearrange("(h l) -> h l", l=P), S.end_sb[:]).then_inc(S.s_out, 16)
        q.wait_ge(S.s_out, 32)


class Ranks:

    def __init__(self, nc, K, ph, hist):
        self.nc, self.K, self.ph, self.hist = nc, K, ph, hist
        self.oh_lo, self.oh_hi = hist.oh_lo, hist.oh_hi
        self.oh_hi_t = [ph.sb(f"rk_oh_hi_t{k}", [HI, RT * P]) for k in range(2)]
        self.krow = [ph.sb(f"rk_krow{k}", [P, RT * P]) for k in range(2)]
        self.hrow = [ph.sb(f"rk_hrow{k}", [HI, RT * P], BF16) for k in range(2)]
        self.junk = [ph.sb(f"rk_junk{k}", [P, P]) for k in range(4)]
        self.before = ph.sb("rk_before", [P, 2 * RT])
        self.own = ph.sb("rk_own", [P, 2 * RT])
        self.run_sb = [ph.sb(f"rk_run_sb{k}", [HI, P]) for k in range(2)]
        self.run = ph.ps("rk_run", [HI, P])
        self.look = [ph.ps(f"rk_look{k}", [P, P]) for k in range(2)]
        names = ("oh", "used", "rows", "rows_used")
        self.s_oh, self.s_used, self.s_rows, self.s_rows_used = ([ph.sem(f"rk_{x}{k}") for k in range(2)] for x in names)
        self.s_run, self.s_copied, self.s_look, self.s_read, self.s_own, self.s_junk = (
            ph.sem(f"rk_{x}") for x in ("run", "copied", "look", "read", "own", "junk"))

    def vector(self, v):
        S, K = self, self.K
        for k in range(2):
            v.sem_inc(S.s_used[k], 1)
        v.sem_inc(S.s_read, 2)
        v.sem_inc(S.s_junk, 2)
        st = Steps(v, S.s_own)
        with v.Fori(0, EC // RT // 2) as i:
            st.loop(i, 2)
            for k in range(2):
                v.wait_ge(S.s_used[k], i + 1)
                v.wait_ge(S.s_rows[k], 32 * i + 32)
                col = (i * 2 + k) * RT
                a, b = one_hots(v, K, S.oh_lo[k][:], S.oh_hi[k][:], K.src_lo, K.src_hi, col)
                a.then_inc(S.s_oh[k], 1)
                b.then_inc(S.s_oh[k], 1)
                v.tensor_scalar(S.oh_hi_t[k][:], S.hrow[k][:], K.pcol[0:HI, :], None, ALU.is_equal).then_inc(S.s_oh[k], 1)
                for j in range(RT):
                    c = k * RT + j
                    v.wait_ge(S.s_junk, i * (2 * RT) + c + 1)
                    v.scalar_tensor_tensor(out=S.junk[j % 2][:], in0=S.krow[k][:, j * P:(j + 1) * P],
                                           scalar=K.src_f[:, bass.ds(col + j, 1)], in1=K.tri[:],
                                           op0=ALU.is_equal, op1=ALU.mult,
                                           accum_out=S.own[:, c:c + 1]).then_inc(S.s_junk, 1)
                    v.wait_ge(S.s_look, i * (2 * RT) + c + 1)
                    v.tensor_tensor_reduce(out=S.junk[2 + j % 2][:], in0=S.look[j % 2][:], in1=S.oh_lo[k][:, j, :],
                                           scale=1.0, scalar=0.0, op0=ALU.mult, op1=ALU.add,
                                           accum_out=S.before[:, c:c + 1]).then_inc(S.s_read, 1)
                v.wait_ge(S.s_junk, i * (2 * RT) + k * RT + RT + 2)
                v.wait_ge(S.s_read, i * (2 * RT) + k * RT + RT + 2)
                st.step(v.tensor_tensor(K.pos[:, bass.ds(col, RT)], S.before[:, k * RT:k * RT + RT],
                                        S.own[:, k * RT:k * RT + RT], ALU.add))
                v.sem_inc(S.s_rows_used[k], 1)
            st.end_loop(EC // RT // 2)

    def tensor(self, pe):
        S, K = self, self.K
        pe.wait_ge(S.hist.s_done, 1)
        pe.matmul(S.run[:], K.ident[0:HI, 0:HI], S.hist.start_sb[:], start=True, stop=False,
                  skip_group_check=True).then_inc(S.s_run, 1)
        with pe.Fori(0, EC // RT // 2) as i:
            for k in range(2):
                pe.wait_ge(S.s_oh[k], i * 3 + 3)
                for j in range(RT):
                    c = k * RT + j
                    pe.wait_ge(S.s_copied, i * (2 * RT) + c + 1)
                    pe.matmul(S.run[:], S.oh_hi[k][:, j, :], S.oh_lo[k][:, j, :], start=False, stop=False,
                              skip_group_check=True).then_inc(S.s_run, 1)
                    pe.wait_ge(S.s_read, i * (2 * RT) + c + 1)
                    mm = pe.matmul(S.look[j % 2][:], S.oh_hi_t[k][:, j * P:(j + 1) * P], S.run_sb[j % 2][:],
                                   start=True, stop=True)
                    mm.then_inc(S.s_look, 1)
                pe.wait_ge(S.s_look, i * (2 * RT) + (k + 1) * RT)
                pe.sem_inc(S.s_used[k], 1)



class Gather:

    def __init__(self, nc, K, ph, table, width, idx):
        self.nc, self.K, self.ph, self.table, self.width, self.idx = nc, K, ph, table, width, idx
        self.ix = [ph.sb(f"g_ix{k}", [P, SG], I32) for k in range(2)]
        self.st = [ph.sb(f"g_st{k}", [P, SG, width]) for k in range(2)]
        names = ("ix_in", "rows", "out", "free")
        self.s_ix, self.s_rows, self.s_out, self.s_free = ([ph.sem(f"g_{x}{k}") for k in range(2)] for x in names)

    def gpsimd(self, g):
        S = self
        with g.Fori(0, STAGES // 2) as i:
            for k in range(2):
                g.wait_ge(S.s_ix[k], 16 * i + 16)
                g.wait_ge(S.s_free[k], i + 1)
                g.nop(nofuse=True)
                for j in range(SG):
                    g.indirect_dma_start(S.st[k][:, j, :], None, S.table,
                                         bass.IndirectOffsetOnAxis(ap=S.ix[k][:, j:j + 1], axis=0)).then_inc(S.s_rows[k], 16)

    def load_index(self, sp, k, t):
        sp.dma_start(self.ix[k][:], self.idx.rearrange("(p c) -> p c", p=P)[:, bass.ds(t * SG, SG)]).then_inc(self.s_ix[k], 16)


def store_gathered(G, sp, out, attn):
    w = G.width
    for k in range(2):
        G.load_index(sp, k, k)
        sp.sem_inc(G.s_free[k], 1)

    def turn(i, last):
        for k in range(2):
            t = i * 2 + k
            sp.wait_ge(G.s_rows[k], (16 * SG) * i + 16 * SG)
            sp.dma_start(out.rearrange("(p c) -> p c", p=P)[:, bass.ds(t * (SG * w), SG * w)],
                         G.st[k][:].rearrange("p j w -> p (j w)")).then_inc(G.s_out[k], 16)
            sp.dma_start(attn[:, bass.ds(t * SG, SG)].unsqueeze(2), G.st[k][:, :, w - 1:w],
                         allow_slow_non_contiguous=True).then_inc(G.s_out[k], 16)
            if not last:
                G.load_index(sp, k, t + 2)
            sp.wait_ge(G.s_out[k], 32 * i + 32)
            if not last:
                sp.sem_inc(G.s_free[k], 1)

    with sp.Fori(0, STAGES // 2 - 1) as i:
        turn(i, False)
    turn(STAGES // 2 - 1, True)


def sort_and_gather(nc, K):
    with phase(nc, "sort") as ph:
        G = Gather(nc, K, ph, K.table0, 33, K.src)
        hs = Histogram(nc, K, ph, "hs", K.src_lo, K.src_hi, K.start_s, K.end_s, K.start_s_sb)
        hd = Histogram(nc, K, ph, "hd", K.dst_lo, K.dst_hi, K.start_d, K.end_d, ph.sb("start_d_sb", [HI, P]))
        rk = Ranks(nc, K, ph, hs)
        ZW = 6272
        zero = ph.sb("zero", [P, ZW])
        s_z, s_zero = ph.sem("z"), ph.sem("zeroed")
        with nc.Block() as block:

            @block.gpsimd
            def _(g):
                G.gpsimd(g)

            @block.sync
            def _(sp):
                store_gathered(G, sp, K.rows0, K.a0)

            @block.vector
            def _(v):
                v.memset(zero[:], 0.0).then_inc(s_z, 1)
                hs.vector(v)
                rk.vector(v)
                hd.vector(v)

            @block.tensor
            def _(pe):
                hs.tensor(pe)
                rk.tensor(pe)
                hd.tensor(pe)

            @block.scalar
            def _(act):
                act.wait_ge(s_z, 1)
                k = 0
                for arr in K.zeroed:
                    at, total = 0, arr.shape[0]
                    while at < total:
                        w = min(ZW * P, total - at)
                        assert w % P == 0
                        act.dma_start(arr[at:at + w].rearrange("(p f) -> p f", p=P), zero[:, 0:w // P]).then_inc(s_zero, 16)
                        at += w
                        k += 16
                hs.store(act)
                rank_rows_and_counts(rk, act)
                hd.store(act)
                act.wait_ge(s_zero, k)


def rank_rows_and_counts(rk, act):
    S = rk

    def load(k, t):
        at = t * (RT * P)
        act.dma_start(S.krow[k][:], S.K.key_rows[bass.ds(at, RT * P)].partition_broadcast(P)).then_inc(S.s_rows[k], 16)
        act.dma_start(S.hrow[k][:], S.K.hi_rows[bass.ds(at, RT * P)].partition_broadcast(HI)).then_inc(S.s_rows[k], 16)

    def turn(i, last):
        for k in range(2):
            for j in range(RT):
                c = k * RT + j
                act.wait_ge(S.s_run, i * (2 * RT) + c + 1)
                act.copy(S.run_sb[j % 2][:], S.run[:]).then_inc(S.s_copied, 1)
            if not last:
                act.wait_ge(S.s_rows_used[k], i + 1)
                load(k, i * 2 + k + 2)

    load(0, 0)
    load(1, 1)
    steps = EC // RT // 2
    with act.Fori(0, steps - 1) as i:
        turn(i, False)
    turn(steps - 1, True)



def layernorm(v, act, ph, K, sems):
    s_own, s_var, s_std = sems
    mean, sq = ph.sb("mean", [P, NC_]), ph.sb("sq", [P, NC_, D])
    var, std, rstd, eps = (ph.sb(x, [P, NC_ if x != "eps" else 1]) for x in ("var", "std", "rstd", "eps"))
    X = K.X[:].rearrange("p (c d) -> p c d", d=D)
    H = K.H[:, 0:NC_, :]

    def wide(a):
        return a[:].unsqueeze(2).to_broadcast([P, NC_, D])

    def vector(v, st):
        st.did(v.memset(eps[:], LN_EPS))
        st.step(v.tensor_reduce(mean[:], X, AX.X, ALU.add))
        st.step(v.tensor_scalar(mean[:], mean[:], 1.0 / D, None, ALU.mult))
        st.step(v.tensor_tensor(H, X, wide(mean), ALU.subtract))
        st.step(v.tensor_tensor(sq[:], H, H, ALU.mult))
        st.step(v.tensor_reduce(var[:], sq[:], AX.X, ALU.add))
        v.sem_inc(s_var, 1)
        v.wait_ge(s_std, 1)
        st.step(v.reciprocal(rstd[:], std[:]))
        st.step(v.tensor_tensor(H, H, wide(rstd), ALU.mult))
        st.step(v.tensor_scalar(H, H, 0.0, None, ALU.max))

    def scalar(act):
        act.wait_ge(s_var, 1)
        act.activation(std[:], var[:], ACT.Sqrt, bias=eps[:, 0:1], scale=1.0 / D).then_inc(s_std, 1)

    return vector, scalar


def table0(nc, K):
    with phase(nc, "t0") as ph:
        aw = ph.sb("aw", [P, 2 * D])
        prod = ph.sb("prod", [P, NC_, D])
        tab = ph.sb("tab", [P, NC_, D + 1])
        s_w, s_tab, s_out = ph.sem("w"), ph.sem("tab"), ph.sem("out")
        sems = ph.sem("own"), ph.sem("var"), ph.sem("std")
        vec, sca = layernorm(None, None, ph, K, sems)
        with nc.Block() as block:

            @block.sync
            def _(sp):
                sp.dma_start(aw[:], K.in_aw.partition_broadcast(P)).then_inc(s_w, 16)
                sp.wait_ge(s_tab, 1)
                sp.dma_start(K.table0.rearrange("(p c) w -> p (c w)", p=P), tab[:].rearrange("p c w -> p (c w)")).then_inc(s_out, 16)
                sp.wait_ge(s_out, 16)

            @block.vector
            def _(v):
                st = Steps(v, sems[0])
                vec(v, st)
                v.wait_ge(s_w, 16)
                H = K.H[:, 0:NC_, :]
                st.did(v.tensor_copy(tab[:, :, 0:D], H))
                for s, out in ((0, tab[:, :, D]), (1, K.b0[:])):
                    w = aw[:, s * D:(s + 1) * D].unsqueeze(1).to_broadcast([P, NC_, D])
                    st.step(v.tensor_tensor(prod[:], H, w, ALU.mult))
                    st.step(v.tensor_reduce(out, prod[:], AX.X, ALU.add))
                v.sem_inc(s_tab, 1)

            @block.scalar
            def _(act):
                sca(act)




class Order:

    def __init__(self, sb, name, keep):
        self.name, self.keep = name, keep
        self.fill_i = sb(f"{name}_fill_i", [P, NC_], I32)
        self.last_i = sb(f"{name}_last_i", [P, NC_], I32)
        self.has = sb(f"{name}_has", [P, NC_])
        self.mend_i = sb(f"{name}_mend_i", [P, 1], I32)
        self.span = sb(f"{name}_span", [P, P])
        self.span_neg = sb(f"{name}_span_neg", [P, P])
        self.first_i = sb(f"{name}_first_i", [P, 1], I32)


def places(nc, K, O, start, end):
    with phase(nc, f"pl_{O.name}") as ph:
        a, b, t, spare = (ph.sb(x, [P, NC_]) for x in "abts")
        spare_i = ph.sb("spare_i", [P, NC_], I32)
        s_in, s_own, s_io = ph.sem("in"), ph.sem("own"), ph.sem("io")
        with nc.Block() as block:

            @block.gpsimd
            def _(g):
                g.iota(spare_i[:], [[1, NC_]], EP, NC_).then_inc(s_io, 1)

            @block.sync
            def _(sp):
                sp.dma_start(a[:], start.rearrange("(p c) -> p c", p=P)).then_inc(s_in, 16)
                sp.dma_start(b[:], end.rearrange("(p c) -> p c", p=P)).then_inc(s_in, 16)

            @block.vector
            def _(v):
                st = Steps(v, s_own)
                v.wait_ge(s_in, 32)
                v.wait_ge(s_io, 1)
                st.did(v.tensor_copy(spare[:], spare_i[:]))
                st.did(v.tensor_tensor(O.has[:], b[:], a[:], ALU.is_gt))
                st.step(v.tensor_scalar(t[:], b[:], -1.0, 0.0, ALU.add, ALU.max))
                st.step(v.tensor_copy(O.last_i[:], t[:]))
                st.step(v.tensor_tensor(a[:], a[:], spare[:], ALU.subtract))
                st.step(v.tensor_tensor(a[:], a[:], O.has[:], ALU.mult))
                st.step(v.tensor_tensor(a[:], a[:], spare[:], ALU.add))
                st.step(v.tensor_copy(O.fill_i[:], a[:]))


def carries(nc, K, O):
    with phase(nc, f"ca_{O.name}") as ph:
        lead = ph.sb("lead", [P, EC])
        f, m, base, spare, r = (ph.sb(x, [P, 1]) for x in ("f", "m", "base", "spare", "r"))
        wide = ph.sb("wide", [P, P])
        pt = ph.ps("pt", [P, P])
        s_own, s_wide, s_t = ph.sem("own"), ph.sem("wide"), ph.sem("t")
        with nc.Block() as block:

            @block.vector
            def _(v):
                st = Steps(v, s_own)
                st.step(v.tensor_tensor_scan(lead[:], O.keep[:], O.keep[:], 1.0, ALU.mult, ALU.mult))
                st.step(v.tensor_reduce(f[:], lead[:], AX.X, ALU.add))
                st.did(v.tensor_scalar(m[:], f[:], 0.5, None, ALU.is_gt))
                st.did(v.tensor_scalar(base[:], K.pcol[:], float(EC), -1.0, ALU.mult, ALU.add))
                st.step(v.tensor_scalar(spare[:], K.pcol[:], float(EP), None, ALU.add))
                st.step(v.tensor_tensor(r[:], f[:], base[:], ALU.add))
                st.step(v.tensor_tensor(r[:], r[:], spare[:], ALU.subtract))
                st.step(v.tensor_tensor(r[:], r[:], m[:], ALU.mult))
                st.step(v.tensor_tensor(r[:], r[:], spare[:], ALU.add))
                st.did(v.tensor_copy(O.mend_i[:], r[:]))
                v.tensor_copy(wide[:], lead[:, EC - 1:EC].to_broadcast([P, P])).then_inc(s_wide, 1)
                v.wait_ge(s_t, 1)
                st.step(v.tensor_copy(O.span[:], pt[:]))
                st.did(v.tensor_scalar(O.span_neg[:], O.span[:], 1.0, -NEG, ALU.subtract, ALU.mult))
                st.settle()

            @block.tensor
            def _(pe):
                pe.wait_ge(s_wide, 1)
                pe.transpose(pt[:], wide[:], K.ident[:]).then_inc(s_t, 1)


def mend_and_read(nc, K, name, O, rows, W, ends, op, out):
    pieces = [(a, min(a + 64, W)) for a in range(0, W, 64)]
    with phase(nc, name) as ph:
        full = [ph.sb(f"full{a}", [b - a, P + 1]) for a, b in pieces]
        carry, row = ph.sb("carry", [P, W]), ph.sb("row", [P, W])
        pt = ph.ps("pt", [64, P])
        pc = ph.ps("pc", [P, W])
        s_t, s_own, s_full, s_c, s_row, s_mended, s_back, s_out = (
            ph.sem(x) for x in ("t", "own", "full", "c", "row", "mended", "back", "out"))
        with nc.Block() as block:

            @block.tensor
            def _(pe):
                for n, (a, b) in enumerate(pieces):
                    if n:
                        pe.wait_ge(s_full, n)
                    pe.transpose(pt[0:b - a, :], ends[:, a:b], K.ident[:]).then_inc(s_t, 1)
                for n, (a, b) in enumerate(pieces):
                    pe.wait_ge(s_full, n + 1)
                    mm = pe.matmul(pc[:, a:b], full[n][:, 0:P], K.ident[0:b - a, 0:b - a], start=True, stop=True)
                    mm.then_inc(s_c, 1)

            @block.vector
            def _(v):
                st = Steps(v, s_own)
                for n, (a, b) in enumerate(pieces):
                    st.step(v.memset(full[n][:, 0:1], 0.0))
                    v.wait_ge(s_t, n + 1)
                    if op == ALU.add:
                        ins = v.tensor_tensor_scan(full[n][:, 1:P + 1], O.span[0:b - a, :], pt[0:b - a, :], 0.0, ALU.mult, ALU.add)
                    else:
                        ins = v.tensor_tensor_scan(full[n][:, 1:P + 1], O.span_neg[0:b - a, :], pt[0:b - a, :], NEG, ALU.add, ALU.max)
                    ins.then_inc(s_full, 1)
                v.wait_ge(s_c, len(pieces))
                st.step(v.tensor_copy(carry[:], pc[:]))
                v.wait_ge(s_row, 16)
                v.tensor_tensor(row[:], row[:], carry[:], op).then_inc(s_mended, 1)

            @block.gpsimd
            def _(g):
                g.indirect_dma_start(row[:], None, rows, bass.IndirectOffsetOnAxis(ap=O.mend_i[:], axis=0)).then_inc(s_row, 16)
                g.wait_ge(s_mended, 1)
                g.indirect_dma_start(rows, bass.IndirectOffsetOnAxis(ap=O.mend_i[:], axis=0), row[:], None).then_inc(s_back, 16)
                g.wait_ge(s_back, 16)
                for c in range(NC_):
                    g.indirect_dma_start(out[:, c, :], None, rows,
                                         bass.IndirectOffsetOnAxis(ap=O.last_i[:, c:c + 1], axis=0)).then_inc(s_out, 16)
                g.wait_ge(s_out, 16 * NC_)


def put_starts(nc, K, name, O, tile, W, fill, table, init):
    with phase(nc, name) as ph:
        s_put, s_tab, s_init = ph.sem("put"), ph.sem("tab"), ph.sem("init")
        with nc.Block() as block:

            @block.sync
            def _(sp):
                sp.dma_start(table.rearrange("(p c) w -> p (c w)", p=P), tile.rearrange("p c w -> p (c w)")).then_inc(s_tab, 16)
                sp.wait_ge(s_tab, 16)

            @block.gpsimd
            def _(g):
                for c in range(NC_):
                    g.indirect_dma_start(fill, bass.IndirectOffsetOnAxis(ap=O.fill_i[:, c:c + 1], axis=0),
                                         tile[:, c, :], None).then_inc(s_put, 16)
                g.wait_ge(s_tab, 16)
                g.indirect_dma_start(init, None, table, bass.IndirectOffsetOnAxis(ap=O.first_i[:], axis=0)).then_inc(s_init, 16)
                g.wait_ge(s_put, 16 * NC_)
                g.wait_ge(s_init, 16)


def max_scan(nc, K, name, O, vals, rows, W, ends):
    with phase(nc, name) as ph:
        neg = ph.sb("neg", [P, EC])
        m = ph.sb("m", [P, EC, W])
        s_own, s_m, s_out = ph.sem("own"), ph.sem("m"), ph.sem("out")
        with nc.Block() as block:

            @block.vector
            def _(v):
                st = Steps(v, s_own)
                st.step(v.tensor_scalar(neg[:], O.keep[:], 1.0, -NEG, ALU.subtract, ALU.mult))
                for w in range(W):
                    st.did(v.tensor_tensor_scan(m[:, :, w], neg[:], vals[:, w, :], NEG, ALU.add, ALU.max))
                st.settle()
                v.tensor_copy(ends, m[:, EC - 1, :]).then_inc(s_m, 1)
                v.wait_ge(s_m, 1)

            @block.sync
            def _(sp):
                sp.wait_ge(s_m, 1)
                sp.dma_start(rows[0:EP, :].rearrange("(p c) w -> p (c w)", p=P), m[:].rearrange("p c w -> p (c w)")).then_inc(s_out, 16)
                sp.wait_ge(s_out, 16)


def bound(nc, K, name, b, top, out, W, slope):
    with phase(nc, name) as ph:
        t = ph.sb("t", [P, NC_, W])
        s_own = ph.sem("own")
        with nc.Block() as block:

            @block.vector
            def _(v):
                st = Steps(v, s_own)
                st.did(v.tensor_copy(out[:, :, 0:W], b))
                st.step(v.tensor_tensor(t[:], top, b, ALU.add))
                st.step(v.scalar_tensor_tensor(out=out[:, :, W:2 * W], in0=t[:], scalar=slope, in1=t[:],
                                               op0=ALU.mult, op1=ALU.max))


def exponentials(nc, K, name, O, vals, fill, init, W, slope, ex):
    HC = EC // 2
    with phase(nc, name) as ph:
        f = ph.sb("f", [P, HC, 2 * W])
        last = ph.sb("last", [P, 2 * W])
        e = [ph.sb(f"e{k}", [P, HC]) for k in range(2)]
        s_in, s_own, s_e, s_ex, s_f = (ph.sem(x) for x in ("in", "own", "e", "ex", "f"))
        with nc.Block() as block:

            @block.sync
            def _(sp):
                for half in range(2):
                    if half:
                        sp.wait_ge(s_f, 1)
                    sp.dma_start(f[:].rearrange("p c w -> p (c w)"),
                                 fill[0:EP, :].rearrange("(p c) w -> p (c w)", p=P)[:, half * HC * 2 * W:(half + 1) * HC * 2 * W]).then_inc(s_in, 16)

            @block.vector
            def _(v):
                st = Steps(v, s_own)
                st.step(v.tensor_copy(last[:], init))
                for half in range(2):
                    c = slice(half * HC, (half + 1) * HC)
                    v.wait_ge(s_in, 16 * half + 16)
                    for w in range(2 * W):
                        st.did(v.tensor_tensor_scan(f[:, :, w], O.keep[:, c], f[:, :, w], last[:, w:w + 1], ALU.mult, ALU.add))
                    st.settle()
                    st.did(v.tensor_copy(last[:], f[:, HC - 1, :]))
                    for w in range(W):
                        n = half * W + w
                        if n >= 2:
                            v.wait_ge(s_ex, n - 1)
                        b = e[n % 2]
                        st.step(v.tensor_tensor(b[:], vals[:, w, c], f[:, :, w], ALU.add))
                        st.step(v.scalar_tensor_tensor(out=b[:], in0=b[:], scalar=slope, in1=b[:], op0=ALU.mult, op1=ALU.max))
                        v.tensor_tensor(b[:], b[:], f[:, :, W + w], ALU.subtract).then_inc(s_e, 1)
                    v.wait_ge(s_e, (half + 1) * W)
                    v.sem_inc(s_f, 1)
                    st.settle()

            @block.scalar
            def _(act):
                for half in range(2):
                    for w in range(W):
                        n = half * W + w
                        act.wait_ge(s_e, n + 1)
                        act.activation(ex[:, w, half * HC:(half + 1) * HC], e[n % 2][:], ACT.Exp).then_inc(s_ex, 1)
                act.wait_ge(s_ex, 2 * W)


def weighted_sums(nc, K, name, O, rows, Win, ex, W, out, CH):
    WO = W * (D + 1)
    with phase(nc, name) as ph:
        inp = [ph.sb(f"in{k}", [P, CH, Win]) for k in range(2)]
        acc = [ph.sb(f"acc{k}", [P, CH, WO]) for k in range(2)]
        s_in, s_used, s_acc, s_out, s_free = ([ph.sem(f"{x}{k}") for k in range(2)] for x in ("in", "used", "acc", "out", "free"))
        s_own = ph.sem("own")
        pairs = EC // CH // 2
        with nc.Block() as block:

            @block.sync
            def _(sp):
                with sp.Fori(0, pairs) as i:
                    for k in range(2):
                        sp.wait_ge(s_used[k], i + 1)
                        sp.dma_start(inp[k][:].rearrange("p c w -> p (c w)"),
                                     rows.rearrange("(p c) -> p c", p=P)[:, bass.ds((i * 2 + k) * (CH * Win), CH * Win)]).then_inc(s_in[k], 16)

            @block.vector
            def _(v):
                st = Steps(v, s_own)
                for k in range(2):
                    v.sem_inc(s_used[k], 1)
                st.step(v.memset(acc[1][:, CH - 1, :], 0.0))
                with v.Fori(0, pairs) as i:
                    st.loop(i, 4 * W + 2 * WO)
                    for k in range(2):
                        col = (i * 2 + k) * CH
                        v.wait_ge(s_in[k], 16 * i + 16)
                        v.wait_ge(s_free[k], i + 1)
                        for h in range(W):
                            x = ex[:, h, bass.ds(col, CH)]
                            st.did(v.tensor_tensor(acc[k][:, :, h * D:(h + 1) * D], inp[k][:, :, 0:D],
                                                   x.unsqueeze(2).to_broadcast([P, CH, D]), ALU.mult))
                            st.did(v.tensor_copy(acc[k][:, :, W * D + h], x))
                        st.settle()
                        v.sem_inc(s_used[k], 1)
                        for c in range(WO):
                            st.did(v.tensor_tensor_scan(acc[k][:, :, c], O.keep[:, bass.ds(col, CH)], acc[k][:, :, c],
                                                        acc[1 - k][:, CH - 1, c:c + 1], ALU.mult, ALU.add))
                        st.settle()
                        v.sem_inc(s_acc[k], 1)
                    st.end_loop(pairs)
                st.step(v.tensor_copy(K.ends[:, 0:WO], acc[1][:, CH - 1, :]))

            @block.scalar
            def _(act):
                for k in range(2):
                    act.sem_inc(s_free[k], 1)
                with act.Fori(0, pairs) as i:
                    for k in range(2):
                        act.wait_ge(s_acc[k], i + 1)
                        act.dma_start(out[0:EP, :].rearrange("(p c) w -> p (c w)", p=P)[:, bass.ds((i * 2 + k) * (CH * WO), CH * WO)],
                                      acc[k][:].rearrange("p c w -> p (c w)")).then_inc(s_out[k], 16)
                        act.wait_ge(s_out[k], 16 * i + 16)
                        act.sem_inc(s_free[k], 1)


def permute(nc, K, name, O, fill, init, W, WO, out):
    with phase(nc, name) as ph:
        inp = [ph.sb(f"in{k}", [P, SG, W]) for k in range(2)]
        buf = [ph.sb(f"buf{k}", [P, SG, WO]) for k in range(2)]
        ix = [ph.sb(f"ix{k}", [P, SG], I32) for k in range(2)]
        s_in, s_used, s_buf, s_put, s_free = ([ph.sem(f"{x}{k}") for k in range(2)] for x in ("in", "used", "buf", "put", "free"))
        s_own = ph.sem("own")
        pairs = STAGES // 2
        keyed = WO > W
        with nc.Block() as block:

            @block.sync
            def _(sp):
                with sp.Fori(0, pairs) as i:
                    for k in range(2):
                        t = i * 2 + k
                        sp.wait_ge(s_used[k], i + 1)
                        sp.wait_ge(s_free[k], i + 1)
                        sp.dma_start(inp[k][:].rearrange("p c w -> p (c w)"),
                                     fill[0:EP, :].rearrange("(p c) w -> p (c w)", p=P)[:, bass.ds(t * (SG * W), SG * W)]).then_inc(s_in[k], 16)
                        sp.dma_start(ix[k][:], K.pos_i.rearrange("(p c) -> p c", p=P)[:, bass.ds(t * SG, SG)]).then_inc(s_in[k], 16)

            @block.vector
            def _(v):
                st = Steps(v, s_own)
                for k in range(2):
                    v.sem_inc(s_used[k], 1)
                st.step(v.tensor_copy(buf[1][:, SG - 1, 0:W], init))
                with v.Fori(0, pairs) as i:
                    st.loop(i, 2 * WO)
                    for k in range(2):
                        col = (i * 2 + k) * SG
                        v.wait_ge(s_in[k], 32 * i + 32)
                        for c in range(W):
                            st.did(v.tensor_tensor_scan(buf[k][:, :, c], O.keep[:, bass.ds(col, SG)], inp[k][:, :, c],
                                                        buf[1 - k][:, SG - 1, c:c + 1], ALU.mult, ALU.add))
                        if keyed:
                            st.did(v.tensor_copy(buf[k][:, :, W], K.src_f[:, bass.ds(col, SG)]))
                        st.settle()
                        v.sem_inc(s_used[k], 1)
                        v.sem_inc(s_buf[k], 1)
                    st.end_loop(pairs)

            @block.gpsimd
            def _(g):
                with g.Fori(0, pairs) as i:
                    for k in range(2):
                        g.wait_ge(s_buf[k], i + 1)
                        g.wait_ge(s_in[k], 32 * i + 32)
                        g.nop(nofuse=True)
                        for j in range(SG):
                            g.indirect_dma_start(out, bass.IndirectOffsetOnAxis(ap=ix[k][:, j:j + 1], axis=0),
                                                 buf[k][:, j, :], None).then_inc(s_put[k], 16)

            @block.scalar
            def _(act):
                for k in range(2):
                    act.sem_inc(s_free[k], 1)
                with act.Fori(0, pairs) as i:
                    for k in range(2):
                        act.wait_ge(s_put[k], (16 * SG) * i + 16 * SG)
                        act.sem_inc(s_free[k], 1)


def store_pos(nc, K):
    with phase(nc, "pos") as ph:
        t = ph.sb("t", [P, EC], I32)
        s_t, s_out = ph.sem("t"), ph.sem("out")
        with nc.Block() as block:

            @block.vector
            def _(v):
                v.tensor_copy(t[:], K.pos[:]).then_inc(s_t, 1)

            @block.sync
            def _(sp):
                sp.wait_ge(s_t, 1)
                sp.dma_start(K.pos_i.rearrange("(p c) -> p c", p=P), t[:]).then_inc(s_out, 16)
                sp.wait_ge(s_out, 16)


def unpack(nc, K, rows, W, vals):
    CH = 196
    with phase(nc, "unpack") as ph:
        inp = [ph.sb(f"in{k}", [P, CH, W]) for k in range(2)]
        key = ph.sb("key", [P, EC])
        prev = ph.sb("prev", [P, 1])
        s_in, s_a, s_v = ([ph.sem(f"{x}{k}") for k in range(2)] for x in ("in", "a", "v"))
        s_own, s_prev, s_key = ph.sem("own"), ph.sem("prev"), ph.sem("key")
        pairs = EC // CH // 2
        with nc.Block() as block:

            @block.sync
            def _(sp):
                with sp.Fori(0, pairs) as i:
                    for k in range(2):
                        sp.wait_ge(s_a[k], i + 1)
                        sp.wait_ge(s_v[k], i + 1)
                        sp.dma_start(inp[k][:].rearrange("p c w -> p (c w)"),
                                     rows.rearrange("(p c) w -> p (c w)", p=P)[:, bass.ds((i * 2 + k) * (CH * W), CH * W)]).then_inc(s_in[k], 16)
                sp.wait_ge(s_key, 1)
                sp.dma_start(prev[1:P, :], key[0:P - 1, EC - 1:EC]).then_inc(s_prev, 16)

            @block.scalar
            def _(act):
                for k in range(2):
                    act.sem_inc(s_a[k], 1)
                with act.Fori(0, pairs) as i:
                    for k in range(2):
                        col = (i * 2 + k) * CH
                        act.wait_ge(s_in[k], 16 * i + 16)
                        for h in range(HEADS):
                            last = act.copy(vals[:, h, bass.ds(col, CH)], inp[k][:, :, D + h])
                        last.then_inc(s_a[k], 1)

            @block.vector
            def _(v):
                st = Steps(v, s_own)
                for k in range(2):
                    v.sem_inc(s_v[k], 1)
                st.step(v.memset(prev[:], -1.0))
                with v.Fori(0, pairs) as i:
                    for k in range(2):
                        v.wait_ge(s_in[k], 16 * i + 16)
                        v.tensor_copy(key[:, bass.ds((i * 2 + k) * CH, CH)], inp[k][:, :, W - 1]).then_inc(s_v[k], 1)
                v.wait_ge(s_v[1], pairs + 1)
                v.wait_ge(s_v[0], pairs + 1)
                v.sem_inc(s_key, 1)
                st.did(v.tensor_copy(K.o_s.first_i[:], key[:, 0:1]))
                st.did(v.tensor_tensor(K.keep_s[:, 1:EC], key[:, 1:EC], key[:, 0:EC - 1], ALU.is_equal))
                v.wait_ge(s_prev, 16)
                st.did(v.tensor_tensor(K.keep_s[:, 0:1], key[:, 0:1], prev[:], ALU.is_equal))
                st.settle()



MUL, MOUT, KH = 16, 8, 16
FW = 96
NOUT = 48
TANH_GAIN = 1.593
INV_SQRT3 = 0.5773502691896258
PW_S, PW_V = 0.17677669529663687, 0.25


def edge_weights(nc, K, wall):
    c0 = math.sqrt(2.0) / math.sqrt(10.0) / 4.0
    r32 = math.sqrt(1.5)
    with phase(nc, "wall") as ph:
        a = ph.sb("a", [32, 3, KH, MOUT])
        b = ph.sb("b", [48, 2, KH, MOUT])
        ao = ph.sb("ao", [32, 3, MOUT, KH])
        bo = ph.sb("bo", [48, MOUT, KH])
        cc = ph.sb("cc", [32, 1])
        s_z, s_in, s_own, s_done, s_out = (ph.sem(x) for x in ("z", "in", "own", "done", "out"))
        W2 = K.in_W2.rearrange("k (i u w) -> i u k w", i=7, u=MUL)
        with nc.Block() as block:

            @block.sync
            def _(sp):
                for r, parts in enumerate(((0, 2, 4), (1, 3, 6))):
                    for n, i in enumerate(parts):
                        sp.dma_start(a[16 * r:16 * r + 16, n, :, :], W2[i]).then_inc(s_in, 16)
                for r in range(3):
                    for n, i in enumerate((5, 6)):
                        sp.dma_start(b[16 * r:16 * r + 16, n, :, :], W2[i]).then_inc(s_in, 16)
                sp.wait_ge(s_z, 1)
                sp.wait_ge(s_done, 1)
                out = wall[:, 0:NOUT * KH].rearrange("p (o k) -> p o k", k=KH)
                sp.dma_start(out[0:32, 0:24, :], ao[:].rearrange("p n w k -> p (n w) k")).then_inc(s_out, 16)
                v = out[:, 24:48, :].rearrange("p (w i) k -> p w i k", i=3)
                for i in range(3):
                    sp.dma_start(v[32 + 16 * i:48 + 16 * i, :, i, :], bo[16 * i:16 * i + 16, :, :]).then_inc(s_out, 16)
                sp.dma_start(wall[80:90, NOUT * KH:], K.in_W1).then_inc(s_out, 16)
                sp.wait_ge(s_out, 80)

            @block.vector
            def _(v):
                st = Steps(v, s_own)
                v.memset(wall[:], 0.0).then_inc(s_z, 1)
                st.step(v.memset(cc[:], r32 * PW_V * c0))
                st.step(v.memset(cc[0:16, :], PW_V * c0))
                v.wait_ge(s_in, 16 * 12)
                st.did(v.tensor_scalar(ao[:, 0:2, :, :], a[:, 0:2, :, :].rearrange("p n k w -> p n w k"), PW_S * c0, None, ALU.mult))
                st.did(v.tensor_scalar(ao[:, 2, :, :], a[:, 2, :, :].rearrange("p k w -> p w k"), cc[:, 0:1], None, ALU.mult))
                st.did(v.tensor_scalar(b[:, 0, :, :], b[:, 0, :, :], INV_SQRT3 * PW_V * c0, None, ALU.mult))
                st.step(v.tensor_scalar(b[:, 1, :, :], b[:, 1, :, :], r32 / 3 * PW_V * c0, None, ALU.mult))
                st.step(v.tensor_tensor(bo[:], b[:, 0, :, :].rearrange("p k w -> p w k"), b[:, 1, :, :].rearrange("p k w -> p w k"), ALU.subtract))
                v.sem_inc(s_done, 1)


def unit_vectors(nc, K, n, gain):
    with phase(nc, "unit") as ph:
        sq = ph.sb("sq", [P, EC, 3])
        ln, zero = ph.sb("ln", [P, EC]), ph.sb("zero", [P, 1])
        s_in, s_own, s_a, s_b = (ph.sem(x) for x in ("in", "own", "a", "b"))
        with nc.Block() as block:

            @block.sync
            def _(sp):
                sp.dma_start(n.rearrange("p c w -> p (c w)"), K.vec.rearrange("(p c) -> p c", p=P)).then_inc(s_in, 16)
                sp.dma_start(gain, K.nrm.rearrange("(p c) -> p c", p=P)).then_inc(s_in, 16)

            @block.vector
            def _(v):
                st = Steps(v, s_own)
                st.did(v.memset(zero[:], 0.0))
                v.wait_ge(s_in, 32)
                st.step(v.tensor_tensor(sq[:], n, n, ALU.mult))
                st.step(v.tensor_reduce(ln[:], sq[:], AX.X, ALU.add))
                v.sem_inc(s_a, 1)
                st.did(v.tensor_scalar(gain, gain, TANH_GAIN, None, ALU.mult))
                v.wait_ge(s_b, 1)
                st.step(v.reciprocal(ln[:], ln[:]))
                st.step(v.tensor_tensor(n, n, ln[:].unsqueeze(2).to_broadcast([P, EC, 3]), ALU.mult))

            @block.scalar
            def _(act):
                act.wait_ge(s_a, 1)
                act.activation(ln[:], ln[:], ACT.Sqrt, bias=zero[:, 0:1]).then_inc(s_b, 1)


def edge_network(nc, K, O, table, fill, init, wall, n, gain, out):
    with phase(nc, "net") as ph:
        G = Gather(nc, K, ph, table, D, K.src)
        hd = [ph.sb(f"hd{k}", [P, SG, D]) for k in range(2)]
        F = [ph.sb(f"F{k}", [P, SG, FW]) for k in range(2)]
        t3 = ph.sb("t3", [P, SG, 16, 3])
        fT = [ph.sb(f"fT{k}", [FW, P]) for k in range(2)]
        hk = [ph.sb(f"hk{k}", [P, KH]) for k in range(2)]
        pr = [ph.sb(f"pr{k}", [P, 2, NOUT, KH]) for k in range(2)]
        o = ph.sb("o", [P, SG, NOUT])
        u3 = ph.sb("u3", [P, SG, MOUT, 3])
        res = [ph.sb(f"res{k}", [P, SG, D]) for k in range(2)]
        last = ph.sb("last", [P, D])
        pf = [ph.ps(f"pf{k}", [FW, P]) for k in range(2)]
        pp = [ph.ps(f"pp{k}", [P, 1024]) for k in range(2)]
        names = ("in", "xs", "cp", "emb", "F", "Fused", "res", "out", "free")
        s_in, s_xs, s_cp, s_emb, s_F, s_Fu, s_res, s_out, s_free = ([ph.sem(f"{x}{k}") for k in range(2)] for x in names)
        (s_own, s_tr, s_fT, s_P, s_h, s_pr, s_red, s_tanh_in, s_tanh, s_z) = (
            ph.sem(x) for x in ("own", "tr", "fT", "P", "h", "pr", "red", "tanh_in", "tanh", "z"))
        pairs = STAGES // 2
        per = 2 * SG

        def turns(eng, turn):
            with eng.Fori(0, pairs - 1) as i:
                turn(i, 0, True)
                turn(i, 1, True)
            turn(pairs - 1, 0, True)
            turn(pairs - 1, 1, False)

        def following(i, k):
            return (i, 1) if k == 0 else (i + 1, 0)

        with nc.Block() as block:

            @block.gpsimd
            def _(g):
                G.gpsimd(g)

            @block.sync
            def _(sp):
                def load(i, k):
                    t = i * 2 + k
                    sp.wait_ge(s_cp[k], i + 1)
                    sp.dma_start(hd[k][:].rearrange("p c w -> p (c w)"),
                                 fill[0:EP, :].rearrange("(p c) w -> p (c w)", p=P)[:, bass.ds(t * (SG * D), SG * D)]).then_inc(s_in[k], 16)
                    G.load_index(sp, k, t)
                    sp.sem_inc(G.s_free[k], 1)
                    sp.wait_ge(s_Fu[k], i + 1)
                    sp.dma_start(F[k][:, :, 80:90], K.emb.rearrange("(p c w) -> p c w", p=P, w=10)[:, bass.ds(t * SG, SG), :]).then_inc(s_emb[k], 16)

                def store(i, k):
                    sp.wait_ge(s_res[k], i + 1)
                    sp.dma_start(out[0:EP, :].rearrange("(p c) w -> p (c w)", p=P)[:, bass.ds((i * 2 + k) * (SG * D), SG * D)],
                                 res[k][:].rearrange("p c w -> p (c w)")).then_inc(s_out[k], 16)
                    sp.wait_ge(s_out[k], 16 * i + 16)
                    sp.sem_inc(s_free[k], 1)

                sp.wait_ge(s_z, 1)
                for k in range(2):
                    load(0, k)
                with sp.Fori(0, pairs - 1) as i:
                    for k in range(2):
                        load(i + 1, k)
                        store(i, k)
                for k in range(2):
                    store(pairs - 1, k)

            @block.vector
            def _(v):
                st = Steps(v, s_own)
                for k in range(2):
                    st.did(v.memset(F[k][:], 0.0))
                st.step(v.tensor_copy(last[:], init))
                v.sem_inc(s_z, 1)
                st.step(v.memset(res[1][:, SG - 1, :], 0.0))

                def hold(i, k):
                    col = (i * 2 + k) * SG
                    v.wait_ge(s_in[k], 16 * i + 16)
                    for c in range(D):
                        st.did(v.tensor_tensor_scan(hd[k][:, :, c], O.keep[:, bass.ds(col, SG)], hd[k][:, :, c],
                                                    last[:, c:c + 1], ALU.mult, ALU.add))
                    st.settle()
                    st.step(v.tensor_copy(last[:], hd[k][:, SG - 1, :]))
                    v.sem_inc(s_xs[k], 1)

                def dots(i, k):
                    col = (i * 2 + k) * SG
                    v.wait_ge(s_cp[k], i + 2)
                    nn = n[:, bass.ds(col, SG), :].unsqueeze(2).to_broadcast([P, SG, 16, 3])
                    st.step(v.tensor_tensor(t3[:], F[k][:, :, 32:80].rearrange("p c (i u) -> p c u i", i=3), nn, ALU.mult))
                    st.step(v.tensor_reduce(F[k][:, :, 16:32], t3[:], AX.X, ALU.add))
                    v.sem_inc(s_F[k], 1)

                def columns(i, k):
                    for j in range(0, SG + 2, 2):
                        b = (j // 2) % 2
                        if j < SG:
                            q2 = i * SG + k * (SG // 2) + j // 2
                            v.wait_ge(s_red, q2 + 1)
                            for c in range(2):
                                q = i * per + k * SG + j + c
                                v.wait_ge(s_h, q + 1)
                                v.tensor_tensor(pr[b][:, c, :, :], pp[c][:, 0:NOUT * KH].rearrange("p (o k) -> p o k", k=KH),
                                                hk[c][:].unsqueeze(1).to_broadcast([P, NOUT, KH]), ALU.mult).then_inc(s_pr, 1)
                        if j >= 2:
                            q = i * per + k * SG + j - 2
                            v.wait_ge(s_pr, q + 4)
                            v.tensor_reduce(o[:, j - 2:j, :], pr[1 - b][:], AX.X, ALU.add).then_inc(s_red, 1)
                    v.wait_ge(s_red, i * SG + (k + 1) * (SG // 2) + 2)
                    v.sem_inc(s_tanh_in, 1)

                def outputs(i, k):
                    t = i * 2 + k
                    col = t * SG
                    nn = n[:, bass.ds(col, SG), :].unsqueeze(2).to_broadcast([P, SG, MOUT, 3])
                    cw = o[:, :, 16:24].unsqueeze(3).to_broadcast([P, SG, MOUT, 3])
                    vv = o[:, :, 24:48].rearrange("p c (w i) -> p c w i", i=3)
                    st.step(v.tensor_tensor(u3[:], cw, nn, ALU.mult))
                    st.step(v.tensor_tensor(vv, vv, u3[:], ALU.add))
                    gg = gain[:, bass.ds(col, SG)].unsqueeze(2)
                    v.wait_ge(s_tanh, t + 1)
                    v.wait_ge(s_free[k], i + 1)
                    gt = o[:, :, 8:16].unsqueeze(3).to_broadcast([P, SG, MOUT, 3])
                    st.did(v.tensor_tensor(res[k][:, :, 0:8], o[:, :, 0:8], gg.to_broadcast([P, SG, 8]), ALU.mult))
                    st.step(v.tensor_tensor(o[:, :, 8:16], o[:, :, 8:16], gg.to_broadcast([P, SG, 8]), ALU.mult))
                    st.step(v.tensor_tensor(res[k][:, :, 8:32].rearrange("p c (w i) -> p c w i", i=3), vv, gt, ALU.mult))
                    for c in range(D):
                        st.did(v.tensor_tensor_scan(res[k][:, :, c], O.keep[:, bass.ds(col, SG)], res[k][:, :, c],
                                                    res[1 - k][:, SG - 1, c:c + 1], ALU.mult, ALU.add))
                    st.settle()
                    v.sem_inc(s_res[k], 1)

                def turn(i, k, more):
                    if more:
                        hold(*following(i, k))
                    columns(i, k)
                    if more:
                        dots(*following(i, k))
                    outputs(i, k)

                hold(0, 0)
                dots(0, 0)
                with v.Fori(0, pairs - 1) as i:
                    st.loop(i, 2 * (D + 1 + 2 + 5 + D))
                    turn(i, 0, True)
                    turn(i, 1, True)
                st.end_loop(pairs - 1)
                turn(pairs - 1, 0, True)
                turn(pairs - 1, 1, False)
                st.step(v.tensor_copy(K.ends[:, 0:D], res[1][:, SG - 1, :]))

            @block.tensor
            def _(pe):
                pe.sem_inc(s_Fu[0], 1)
                pe.sem_inc(s_Fu[1], 1)
                pe.sem_inc(s_pr, 2)
                with pe.Fori(0, pairs) as i:
                    for k in range(2):
                        pe.wait_ge(s_F[k], i + 1)
                        pe.wait_ge(s_emb[k], 16 * i + 16)
                        for j in range(SG + 1):
                            b = (j - 1) % 2
                            if j < SG:
                                q = i * per + k * SG + j
                                pe.wait_ge(s_fT, q + 1)
                                pe.transpose(pf[j % 2][:], F[k][:, j, :], K.ident[:]).then_inc(s_tr, 1)
                            if j >= 1:
                                q = i * per + k * SG + j - 1
                                pe.wait_ge(s_fT, q + 3)
                                pe.wait_ge(s_pr, q + 1)
                                pe.matmul(pp[b][:, 512:NOUT * KH + KH], fT[b][:], wall[:, 512:], start=True, stop=True)
                                pe.matmul(pp[b][:, 0:512], fT[b][:], wall[:, 0:512], start=True, stop=True).then_inc(s_P, 1)
                        pe.sem_inc(s_Fu[k], 1)

            @block.scalar
            def _(act):
                act.sem_inc(s_fT, 2)
                act.sem_inc(s_red, 2)
                for k in range(2):
                    act.sem_inc(s_free[k], 1)
                    act.sem_inc(s_cp[k], 1)

                def place(i, k, part):
                    e, c = part // 4, part % 4
                    x = (G.st[k], hd[k])[e]
                    if part == 0:
                        act.wait_ge(G.s_rows[k], (16 * SG) * i + 16 * SG)
                        act.wait_ge(s_emb[k], 16 * i + 16)
                    if part == 4:
                        act.wait_ge(s_xs[k], i + 1)
                    if c == 0:
                        act.copy(F[k][:, :, 8 * e:8 * e + 8], x[:, :, 0:8])
                    else:
                        ins = act.copy(F[k][:, :, 16 + 16 * c + 8 * e:24 + 16 * c + 8 * e],
                                       x[:, :, 8:32].rearrange("p c (u i) -> p c u i", i=3)[:, :, :, c - 1])
                        if part == 7:
                            ins.then_inc(s_cp[k], 1)

                def turn(i, k, more):
                    t = i * 2 + k
                    for j in range(SG + 1):
                        if j < SG:
                            q = i * per + k * SG + j
                            act.wait_ge(s_tr, q + 1)
                            act.copy(fT[j % 2][:], pf[j % 2][:]).then_inc(s_fT, 1)
                        if j >= 1:
                            q = i * per + k * SG + j - 1
                            act.wait_ge(s_P, q + 1)
                            act.activation(hk[(j - 1) % 2][:], pp[(j - 1) % 2][:, NOUT * KH:NOUT * KH + KH], ACT.Relu).then_inc(s_h, 1)
                        if more and 16 <= j < 24:
                            place(*following(i, k), j - 16)
                    act.wait_ge(s_tanh_in, t + 1)
                    act.activation(o[:, :, 0:16], o[:, :, 0:16], ACT.Tanh).then_inc(s_tanh, 1)

                for part in range(8):
                    place(0, 0, part)
                turns(act, turn)



BN_EPS = 1e-5
CB = 112


def first_sums(nc, K, O, fill, init, rows, out, stats):
    CH = CB
    with phase(nc, "z") as ph:
        a = [ph.sb(f"a{k}", [P, CH, D]) for k in range(2)]
        b = [ph.sb(f"b{k}", [P, CH, D]) for k in range(2)]
        sq = ph.sb("sq", [P, CH, D])
        last = ph.sb("last", [P, D])
        one = ph.sb("one", [P, 1])
        zz = ph.sb("zz", [P, 448])
        p1, p2 = ph.ps("p1", [1, 448]), ph.ps("p2", [1, 448])
        s_in, s_z, s_out, s_free = ([ph.sem(f"{x}{k}") for k in range(2)] for x in ("in", "z", "out", "free"))
        s_own, s_sq, s_pe, s_one, s_fin = (ph.sem(x) for x in ("own", "sq", "pe", "one", "fin"))
        pairs = EC // CH // 2
        with nc.Block() as block:

            @block.sync
            def _(sp):
                with sp.Fori(0, pairs) as i:
                    for k in range(2):
                        t = i * 2 + k
                        sp.wait_ge(s_free[k], i + 1)
                        for x, src in ((a, fill[0:EP, :]), (b, rows)):
                            sp.dma_start(x[k][:].rearrange("p c w -> p (c w)"),
                                         src.rearrange("(p c) w -> p (c w)", p=P)[:, bass.ds(t * (CH * D), CH * D)]).then_inc(s_in[k], 16)

            @block.vector
            def _(v):
                st = Steps(v, s_own)
                st.did(v.memset(one[:], 1.0))
                st.did(v.memset(zz[:], 0.0))
                st.step(v.tensor_copy(last[:], init))
                v.sem_inc(s_one, 1)
                with v.Fori(0, pairs) as i:
                    st.loop(i, 2 * (D + 2))
                    for k in range(2):
                        col = (i * 2 + k) * CH
                        v.wait_ge(s_in[k], 32 * i + 32)
                        for c in range(D):
                            st.did(v.tensor_tensor_scan(a[k][:, :, c], O.keep[:, bass.ds(col, CH)], a[k][:, :, c],
                                                        last[:, c:c + 1], ALU.mult, ALU.add))
                        st.settle()
                        st.did(v.tensor_copy(last[:], a[k][:, CH - 1, :]))
                        st.step(v.tensor_tensor(b[k][:], a[k][:], b[k][:], ALU.add))
                        v.sem_inc(s_z[k], 1)
                    st.end_loop(pairs)
                v.wait_ge(s_fin, 1)
                st.did(v.tensor_copy(stats[:, 0, :], p1[:]))
                st.did(v.tensor_copy(stats[:, 1, :], p2[:]))
                st.settle()

            @block.scalar
            def _(act):
                for k in range(2):
                    act.sem_inc(s_free[k], 1)
                act.sem_inc(s_pe, 1)
                with act.Fori(0, pairs) as i:
                    for k in range(2):
                        t = i * 2 + k
                        act.wait_ge(s_z[k], i + 1)
                        act.dma_start(out.rearrange("(p c) w -> p (c w)", p=P)[:, bass.ds(t * (CH * D), CH * D)],
                                      b[k][:].rearrange("p c w -> p (c w)")).then_inc(s_out[k], 16)
                        act.wait_ge(s_pe, t + 1)
                        act.activation(sq[:], b[k][:], ACT.Square).then_inc(s_sq, 1)
                        act.wait_ge(s_pe, t + 2)
                        act.wait_ge(s_out[k], 16 * i + 16)
                        act.sem_inc(s_free[k], 1)

            @block.tensor
            def _(pe):
                pe.wait_ge(s_one, 1)
                pe.matmul(p1[:], one[:], zz[:], start=True, stop=False, skip_group_check=True)
                pe.matmul(p2[:], one[:], zz[:], start=True, stop=False, skip_group_check=True)
                with pe.Fori(0, pairs) as i:
                    for k in range(2):
                        t = i * 2 + k
                        pe.wait_ge(s_z[k], i + 1)
                        bf, sf = b[k][:].rearrange("p c w -> p (c w)"), sq[:].rearrange("p c w -> p (c w)")
                        for m in range(CH * D // 448):
                            pe.matmul(p1[:], one[:], bf[:, 448 * m:448 * m + 448], start=False, stop=False, skip_group_check=True)
                        pe.wait_ge(s_sq, t + 1)
                        for m in range(CH * D // 448):
                            mm = pe.matmul(p2[:], one[:], sf[:, 448 * m:448 * m + 448], start=False, stop=False, skip_group_check=True)
                        mm.then_inc(s_pe, 1)
                pe.matmul(p1[:], one[:], zz[:], start=False, stop=True, skip_group_check=True)
                pe.matmul(p2[:], one[:], zz[:], start=False, stop=True, skip_group_check=True).then_inc(s_fin, 1)


def bn_coefficients(v, st, s_a, s_b, total, total_sq, pad, gamma, beta, scale, shift, t, eps):
    st.step(v.tensor_tensor(t, pad, pad, ALU.mult))
    st.step(v.scalar_tensor_tensor(out=total, in0=pad, scalar=-float(NPAD), in1=total, op0=ALU.mult, op1=ALU.add))
    st.step(v.scalar_tensor_tensor(out=total_sq, in0=t, scalar=-float(NPAD), in1=total_sq, op0=ALU.mult, op1=ALU.add))
    st.did(v.tensor_scalar(total, total, 1.0 / E, None, ALU.mult))
    st.step(v.tensor_scalar(total_sq, total_sq, 1.0 / E, None, ALU.mult))
    st.step(v.tensor_tensor(t, total, total, ALU.mult))
    st.step(v.tensor_tensor(t, total_sq, t, ALU.subtract))
    st.step(v.tensor_scalar(t, t, 0.0, None, ALU.max))
    v.sem_inc(s_a, 1)
    v.wait_ge(s_b, 1)
    st.step(v.reciprocal(t, t))
    st.step(v.tensor_tensor(scale, t, gamma, ALU.mult))
    st.step(v.tensor_tensor(t, total, scale, ALU.mult))
    st.step(v.tensor_tensor(shift, beta, t, ALU.subtract))


def norm1(nc, K, stats, z, coef):
    with phase(nc, "bn1") as ph:
        r = ph.sb("r", [1, 8, D])
        eps = ph.sb("eps", [1, 1])
        row = ph.sb("row", [1, 2, 4, D])
        pt = ph.ps("pt", [P, 2])
        s_in, s_own, s_a, s_b, s_row, s_t = (ph.sem(x) for x in ("in", "own", "a", "b", "row", "t"))
        with nc.Block() as block:

            @block.sync
            def _(sp):
                for n, x in enumerate((K.in_g1, K.in_be1)):
                    sp.dma_start(r[:, n, :], x.unsqueeze(0)).then_inc(s_in, 16)
                sp.dma_start(r[:, 2, :], z[EP - 1:EP, :]).then_inc(s_in, 16)

            @block.vector
            def _(v):
                st = Steps(v, s_own)
                st.step(v.memset(eps[:], BN_EPS))
                for n in range(2):
                    st.step(v.tensor_reduce(r[:, 3 + n, :], stats[:, n, :].rearrange("p (j d) -> p d j", d=D), AX.X, ALU.add))
                v.wait_ge(s_in, 48)
                bn_coefficients(v, st, s_a, s_b, r[:, 3, :], r[:, 4, :], r[:, 2, :], r[:, 0, :], r[:, 1, :], r[:, 5, :], r[:, 6, :], r[:, 7, :], eps)
                for n in range(2):
                    st.step(v.tensor_copy(row[:, n, :, :], r[:, 5 + n, :].unsqueeze(1).to_broadcast([1, 4, D])))
                v.sem_inc(s_row, 1)
                v.wait_ge(s_t, 1)
                st.step(v.tensor_copy(coef, pt[:]))

            @block.scalar
            def _(act):
                act.wait_ge(s_a, 1)
                act.activation(r[:, 7, :], r[:, 7, :], ACT.Sqrt, bias=eps[:, 0:1]).then_inc(s_b, 1)

            @block.tensor
            def _(pe):
                pe.wait_ge(s_row, 1)
                for n in range(2):
                    mm = pe.matmul(pt[:, n:n + 1], row[:, n, :, :].rearrange("p c d -> p (c d)"), K.ident[0:1, 0:1], start=True, stop=True)
                mm.then_inc(s_t, 1)


def second_product(nc, K, z, coef, out, sums):
    G7, NCH = CB // 16, EC // CB
    with phase(nc, "y") as ph:
        zi = [ph.sb(f"zi{k}", [P, CB, D]) for k in range(2)]
        rT = [ph.sb(f"rT{k}", [P, 512]) for k in range(2)]
        yT = [ph.sb(f"yT{k}", [P, 28 * P]) for k in range(2)]
        junk = [ph.sb(f"junk{k}", [P, 512]) for k in range(2)]
        m2 = ph.sb("m2", [P, P])
        b2 = ph.sb("b2", [P, 1])
        part = ph.sb("part", [P, 2, 2 * G7])
        pt = [ph.ps(f"pt{k}", [P, 512]) for k in range(2)]
        py = [ph.ps(f"py{k}", [P, 512]) for k in range(2)]
        s_in, s_used, s_y, s_out, s_free = ([ph.sem(f"{x}{k}") for k in range(2)] for x in ("in", "used", "y", "out", "free"))
        s_z, s_w, s_t, s_r, s_p, s_e, s_q, s_own, s_sum = (ph.sem(x) for x in ("z", "w", "t", "r", "p", "e", "q", "own", "sum"))
        pairs = NCH // 2
        with nc.Block() as block:

            @block.sync
            def _(sp):
                sp.wait_ge(s_z, 1)
                for c in range(4):
                    sp.dma_start(m2[c * D:(c + 1) * D, c * D:(c + 1) * D], K.in_M2).then_inc(s_w, 16)
                    sp.dma_start(b2[c * D:(c + 1) * D, :], K.in_b2.unsqueeze(1)).then_inc(s_w, 16)
                with sp.Fori(0, pairs) as i:
                    for k in range(2):
                        t = i * 2 + k
                        sp.wait_ge(s_used[k], i + 1)
                        sp.dma_start(zi[k][:].rearrange("p c w -> p (c w)"),
                                     z.rearrange("(p c) w -> p (c w)", p=P)[:, bass.ds(t * (CB * D), CB * D)]).then_inc(s_in[k], 16)

            @block.tensor
            def _(pe):
                pe.wait_ge(s_w, 128)
                for k in range(2):
                    pe.sem_inc(s_used[k], 1)
                with pe.Fori(0, pairs) as i:
                    for k in range(2):
                        zf = zi[k][:].rearrange("p c w -> p (c w)")
                        pe.wait_ge(s_in[k], 16 * i + 16)
                        for g in range(G7 + 1):
                            if g < G7:
                                n = i * (2 * G7) + k * G7 + g
                                b = (k * G7 + g) % 2
                                pe.wait_ge(s_r, n + 1)
                                for m in range(4):
                                    mm = pe.transpose(pt[b][:, m * P:(m + 1) * P], zf[:, (4 * g + m) * P:(4 * g + m + 1) * P], K.ident[:])
                                mm.then_inc(s_t, 1)
                            if g >= 1:
                                n = i * (2 * G7) + k * G7 + g - 1
                                b = (k * G7 + g - 1) % 2
                                pe.wait_ge(s_r, n + 3)
                                pe.wait_ge(s_e, n + 1)
                                pe.matmul(py[b][:], m2[:], rT[b][:], start=True, stop=True).then_inc(s_p, 1)
                        pe.sem_inc(s_used[k], 1)

            @block.scalar
            def _(act):
                act.sem_inc(s_r, 2)
                with act.Fori(0, pairs) as i:
                    for k in range(2):
                        for g in range(G7):
                            n = i * (2 * G7) + k * G7 + g
                            b = (k * G7 + g) % 2
                            act.wait_ge(s_t, n + 1)
                            act.activation(rT[b][:], pt[b][:], ACT.Relu, bias=coef[:, 1:2], scale=coef[:, 0:1]).then_inc(s_r, 1)
                            act.wait_ge(s_q, n + 1)
                            act.wait_ge(s_e, n + 3)
                            act.activation(junk[b][:], yT[k][:, g * 512:(g + 1) * 512], ACT.Square,
                                           accum_out=part[:, 1, k * G7 + g:k * G7 + g + 1]).then_inc(s_q, 1)
                        act.wait_ge(s_q, i * (2 * G7) + (k + 1) * G7 + 2)
                        act.sem_inc(s_y[k], 1)

            @block.vector
            def _(v):
                st = Steps(v, s_own)
                v.memset(m2[:], 0.0).then_inc(s_z, 1)
                v.sem_inc(s_e, 2)
                v.sem_inc(s_q, 2)
                v.wait_ge(s_w, 128)
                with v.Fori(0, pairs) as i:
                    st.loop(i, 2 + 2)
                    for k in range(2):
                        v.wait_ge(s_free[k], i + 1)
                        for g in range(G7):
                            n = i * (2 * G7) + k * G7 + g
                            b = (k * G7 + g) % 2
                            v.wait_ge(s_p, n + 1)
                            v.tensor_scalar(yT[k][:, g * 512:(g + 1) * 512], py[b][:], b2[:, 0:1], None, ALU.add).then_inc(s_e, 1)
                        v.wait_ge(s_e, i * (2 * G7) + (k + 1) * G7 + 2)
                        st.step(v.tensor_reduce(sums[:, 0, bass.ds((i * 2 + k) * G7, 1)], yT[k][:], AX.X, ALU.add))
                        v.wait_ge(s_q, i * (2 * G7) + (k + 1) * G7 + 2)
                        st.step(v.tensor_reduce(sums[:, 1, bass.ds((i * 2 + k) * G7, 1)], part[:, 1, k * G7:(k + 1) * G7], AX.X, ALU.add))
                        v.sem_inc(s_y[k], 1)
                    st.end_loop(pairs)

            @block.gpsimd
            def _(g_):
                for k in range(2):
                    g_.sem_inc(s_free[k], 1)
                with g_.Fori(0, pairs) as i:
                    for k in range(2):
                        t = i * 2 + k
                        g_.wait_ge(s_y[k], 2 * i + 2)
                        g_.nop(nofuse=True)
                        g_.dma_start(out[bass.ds(t * P, P), :], yT[k][:]).then_inc(s_out[k], 16)
                        g_.wait_ge(s_out[k], 16 * i + 16)
                        g_.sem_inc(s_free[k], 1)


def norm2(nc, K, sums, yT, coef):
    NCH, G7 = EC // CB, CB // 16
    with phase(nc, "bn2") as ph:
        c = ph.sb("c", [P, 10])
        eps = ph.sb("eps", [P, 1])
        gath = ph.sb("gath", [P, P])
        row, col = ph.sb("row", [P, 2]), ph.sb("col", [P, 2])
        ps = ph.ps("ps", [P, 2])
        s_in, s_own, s_a, s_b, s_g, s_t = (ph.sem(x) for x in ("in", "own", "a", "b", "g", "t"))
        with nc.Block() as block:

            @block.sync
            def _(sp):
                for q in range(4):
                    sp.dma_start(c[q * D:(q + 1) * D, 0:1], K.in_g2.unsqueeze(1)).then_inc(s_in, 16)
                    sp.dma_start(c[q * D:(q + 1) * D, 1:2], K.in_be2.unsqueeze(1)).then_inc(s_in, 16)
                    sp.dma_start(c[q * D:(q + 1) * D, 2:3],
                                 yT[(NCH - 1) * P + 96:(NCH - 1) * P + P, 28 * P - 1:28 * P], allow_slow_non_contiguous=True).then_inc(s_in, 16)

            @block.vector
            def _(v):
                st = Steps(v, s_own)
                st.did(v.memset(eps[:], BN_EPS))
                for a in range(4):
                    for b in range(4):
                        st.did(v.tensor_copy(gath[a * D:(a + 1) * D, b * D:(b + 1) * D], K.ident[a * D:(a + 1) * D, a * D:(a + 1) * D]))
                for n in range(2):
                    st.did(v.tensor_reduce(row[:, n:n + 1], sums[:, n, :].rearrange("p (t g) -> p g t", g=G7)[:, 0, :], AX.X, ALU.add))
                st.settle()
                v.sem_inc(s_g, 1)
                v.wait_ge(s_t, 1)
                st.step(v.tensor_copy(col[:], ps[:]))
                v.wait_ge(s_in, 192)
                bn_coefficients(v, st, s_a, s_b, col[:, 0:1], col[:, 1:2], c[:, 2:3], c[:, 0:1], c[:, 1:2], coef[:, 0:1], coef[:, 1:2], c[:, 3:4], eps)

            @block.tensor
            def _(pe):
                pe.wait_ge(s_g, 1)
                pe.matmul(ps[:], gath[:], row[:], start=True, stop=True).then_inc(s_t, 1)

            @block.scalar
            def _(act):
                act.wait_ge(s_a, 1)
                act.activation(c[:, 3:4], c[:, 3:4], ACT.Sqrt, bias=eps[:, 0:1]).then_inc(s_b, 1)


def last_sums(nc, K, O, yT, coef, out):
    G7, NCH = CB // 16, EC // CB
    with phase(nc, "r") as ph:
        yi = [ph.sb(f"yi{k}", [P, 28 * P]) for k in range(2)]
        acc = [ph.sb(f"acc{k}", [P, CB, D]) for k in range(2)]
        pt = [ph.ps(f"pt{k}", [P, 512]) for k in range(2)]
        s_in, s_used, s_r, s_acc, s_out, s_free = ([ph.sem(f"{x}{k}") for k in range(2)] for x in ("in", "used", "r", "acc", "out", "free"))
        s_t, s_c, s_own = ph.sem("t"), ph.sem("c"), ph.sem("own")
        pairs = NCH // 2
        with nc.Block() as block:

            @block.sync
            def _(sp):
                with sp.Fori(0, pairs) as i:
                    for k in range(2):
                        sp.wait_ge(s_used[k], i + 1)
                        sp.dma_start(yi[k][:], yT[bass.ds((i * 2 + k) * P, P), :]).then_inc(s_in[k], 16)

            @block.scalar
            def _(act):
                with act.Fori(0, pairs) as i:
                    for k in range(2):
                        act.wait_ge(s_in[k], 16 * i + 16)
                        act.activation(yi[k][:], yi[k][:], ACT.Relu, bias=coef[:, 1:2], scale=coef[:, 0:1]).then_inc(s_r[k], 1)

            @block.tensor
            def _(pe):
                for k in range(2):
                    pe.sem_inc(s_used[k], 1)
                with pe.Fori(0, pairs) as i:
                    for k in range(2):
                        pe.wait_ge(s_r[k], i + 1)
                        for g in range(G7):
                            n = i * (2 * G7) + k * G7 + g
                            b = (k * G7 + g) % 2
                            pe.wait_ge(s_c, n + 1)
                            for m in range(4):
                                mm = pe.transpose(pt[b][:, m * P:(m + 1) * P], yi[k][:, (4 * g + m) * P:(4 * g + m + 1) * P], K.ident[:])
                            mm.then_inc(s_t, 1)
                        pe.wait_ge(s_t, i * (2 * G7) + (k + 1) * G7)
                        pe.sem_inc(s_used[k], 1)

            @block.vector
            def _(v):
                st = Steps(v, s_own)
                v.sem_inc(s_c, 2)
                st.step(v.memset(acc[1][:, CB - 1, :], 0.0))
                with v.Fori(0, pairs) as i:
                    st.loop(i, 2 * D)
                    for k in range(2):
                        v.wait_ge(s_free[k], i + 1)
                        af = acc[k][:].rearrange("p c w -> p (c w)")
                        for g in range(G7):
                            v.wait_ge(s_t, i * (2 * G7) + k * G7 + g + 1)
                            v.tensor_copy(af[:, g * 512:(g + 1) * 512], pt[(k * G7 + g) % 2][:]).then_inc(s_c, 1)
                        v.wait_ge(s_c, i * (2 * G7) + (k + 1) * G7 + 2)
                        for c in range(D):
                            st.did(v.tensor_tensor_scan(acc[k][:, :, c], O.keep[:, bass.ds((i * 2 + k) * CB, CB)], acc[k][:, :, c],
                                                        acc[1 - k][:, CB - 1, c:c + 1], ALU.mult, ALU.add))
                        st.settle()
                        v.sem_inc(s_acc[k], 1)
                    st.end_loop(pairs)
                st.step(v.tensor_copy(K.ends[:, 0:D], acc[1][:, CB - 1, :]))

            @block.gpsimd
            def _(g_):
                for k in range(2):
                    g_.sem_inc(s_free[k], 1)
                with g_.Fori(0, pairs) as i:
                    for k in range(2):
                        g_.wait_ge(s_acc[k], i + 1)
                        g_.nop(nofuse=True)
                        g_.dma_start(out[0:EP, :].rearrange("(p c) w -> p (c w)", p=P)[:, bass.ds((i * 2 + k) * (CB * D), CB * D)],
                                     acc[k][:].rearrange("p c w -> p (c w)")).then_inc(s_out[k], 16)
                        g_.wait_ge(s_out[k], 16 * i + 16)
                        g_.sem_inc(s_free[k], 1)



def safe_reciprocal(v, st, O, den, out, W):
    has = O.has[:].unsqueeze(2).to_broadcast([P, NC_, W])
    st.step(v.tensor_tensor(out, den, has, ALU.mult))
    st.step(v.tensor_tensor(out, out, has, ALU.subtract))
    st.step(v.tensor_scalar(out, out, 1.0, None, ALU.add))
    st.step(v.reciprocal(out, out))
    st.step(v.tensor_tensor(out, out, has, ALU.mult))


class BlockProduct:

    def __init__(self, ph, K, wide, M, out_fn):
        self.ph, self.K, self.wide, self.M, self.out_fn = ph, K, wide, M, out_fn
        self.pt = [ph.ps(f"bp_pt{k}", [P, P]) for k in range(2)]
        self.po = [ph.ps(f"bp_po{k}", [P, 4 * M]) for k in range(2)]
        self.hT = [ph.sb(f"bp_hT{k}", [P, P]) for k in range(2)]
        self.s_t, self.s_c, self.s_o, self.s_e = (ph.sem(f"bp_{x}") for x in "tcoe")

    def tensor(self, pe):
        S = self
        H = S.K.H[:].rearrange("p c d -> p (c d)")
        for b in range(NB + 1):
            if b < NB:
                if b >= 2:
                    pe.wait_ge(S.s_c, b - 1)
                pe.transpose(S.pt[b % 2][:], H[:, b * P:(b + 1) * P], S.K.ident[:]).then_inc(S.s_t, 1)
            if b >= 1:
                pe.wait_ge(S.s_c, b)
                if b >= 3:
                    pe.wait_ge(S.s_e, b - 2)
                pe.matmul(S.po[(b - 1) % 2][:], S.hT[(b - 1) % 2][:], S.wide[:], start=True, stop=True).then_inc(S.s_o, 1)

    def scalar(self, act):
        S = self
        for b in range(NB):
            act.wait_ge(S.s_t, b + 1)
            if b >= 2:
                act.wait_ge(S.s_o, b - 1)
            act.copy(S.hT[b % 2][:], S.pt[b % 2][:]).then_inc(S.s_c, 1)

    def vector(self, v):
        S = self
        for b in range(NB):
            v.wait_ge(S.s_o, b + 1)
            n = min(4, NC_ - 4 * b)
            S.out_fn(v, b, n, S.po[b % 2][:].rearrange("p (c m) -> p c m", m=S.M)[:, 0:n, :]).then_inc(S.s_e, 1)
        v.wait_ge(S.s_e, NB)


def node1(nc, K, R):
    with phase(nc, "n1") as ph:
        rec = ph.sb("rec", [P, NC_, 1])
        w = ph.sb("w", [P, HEADS, D])
        fw, fb = ph.sb("fw", [P, 2 * D]), ph.sb("fb", [P, 1])
        prod = ph.sb("prod", [P, HEADS, D])
        V = ph.sb("V", [P, 2, HEADS])
        wide = ph.sb("wide", [P, 4 * 8])
        s_w, s_h, s_wide = ph.sem("w"), ph.sem("h"), ph.sem("wide")
        sems = ph.sem("own"), ph.sem("var"), ph.sem("std")
        vec, sca = layernorm(None, None, ph, K, sems)

        def out_fn(v, b, n, po):
            v.tensor_scalar(K.b1[:, 4 * b:4 * b + n, :], po[:, :, 0:HEADS], fb[:, 0:1], None, ALU.add).then_inc(s_h, 1)
            return v.tensor_copy(K.t1[:, 4 * b:4 * b + n, D:D + HEADS], po[:, :, HEADS:8])

        bp = BlockProduct(ph, K, wide, 8, out_fn)
        with nc.Block() as block:

            @block.sync
            def _(sp):
                for c in range(4):
                    sp.dma_start(w[c * D:(c + 1) * D, :, :], K.in_w.rearrange("h f o -> f h o")).then_inc(s_w, 16)
                sp.dma_start(fw[:], K.in_fw.rearrange("a b -> (a b)").partition_broadcast(P)).then_inc(s_w, 16)
                sp.dma_start(fb[:], K.in_fb.partition_broadcast(P)).then_inc(s_w, 16)

            @block.vector
            def _(v):
                st = Steps(v, sems[0])
                st.did(v.memset(wide[:], 0.0))
                v.wait_ge(s_w, 96)
                for s in range(2):
                    f = fw[:, s * D:(s + 1) * D].unsqueeze(1).to_broadcast([P, HEADS, D])
                    st.step(v.tensor_tensor(prod[:], w[:], f, ALU.mult))
                    st.step(v.tensor_reduce(V[:, s, :], prod[:], AX.X, ALU.add))
                for c in range(4):
                    st.step(v.tensor_copy(wide[c * D:(c + 1) * D, c * 8:(c + 1) * 8], V[c * D:(c + 1) * D, :, :].rearrange("p s h -> p (s h)")))
                safe_reciprocal(v, st, K.o_d, R[:, :, D:D + 1], rec[:], 1)
                st.step(v.tensor_tensor(R[:, :, 0:D], R[:, :, 0:D], rec[:].to_broadcast([P, NC_, D]), ALU.mult))
                X = K.X[:].rearrange("p (c d) -> p c d", d=D)
                st.step(v.tensor_tensor(X, X, R[:, :, 0:D], ALU.add))
                vec(v, st)
                v.sem_inc(s_wide, 1)
                st.did(v.tensor_copy(K.t1[:, :, 0:D], K.H[:, 0:NC_, :]))
                bp.vector(v)
                v.wait_ge(s_h, NB)
                st.settle()

            @block.scalar
            def _(act):
                sca(act)
                bp.scalar(act)

            @block.tensor
            def _(pe):
                pe.wait_ge(s_wide, 1)
                bp.tensor(pe)


def node2(nc, K, R):
    with phase(nc, "n2") as ph:
        rec = ph.sb("rec", [P, NC_, HEADS])
        w = ph.sb("w", [P, D])
        bias = ph.sb("bias", [P, D])
        nq = -(-NC_ // 4)
        sT = [ph.sb(f"sT{k}", [P, 4, P]) for k in range(2)]
        pt = [ph.ps(f"pt{k}", [P, 4, P]) for k in range(2)]
        po = [ph.ps(f"po{k}", [P, 4, D]) for k in range(2)]
        s_w, s_r, s_t, s_c, s_o, s_x = (ph.sem(x) for x in ("w", "r", "t", "c", "o", "x"))
        sems = ph.sem("own"), ph.sem("var"), ph.sem("std")
        vec, sca = layernorm(None, None, ph, K, sems)
        with nc.Block() as block:

            @block.sync
            def _(sp):
                sp.dma_start(w[:], K.in_w.rearrange("h f o -> (h f) o")).then_inc(s_w, 16)
                sp.dma_start(bias[:], K.in_bias.partition_broadcast(P)).then_inc(s_w, 16)

            @block.vector
            def _(v):
                st = Steps(v, sems[0])
                safe_reciprocal(v, st, K.o_s, R[:, :, HEADS * D:], rec[:], HEADS)
                st.step(v.tensor_scalar(rec[:], rec[:], 1.0 / HEADS, None, ALU.mult))
                for h in range(HEADS):
                    st.did(v.tensor_tensor(R[:, :, h * D:(h + 1) * D], R[:, :, h * D:(h + 1) * D],
                                           rec[:, :, h:h + 1].to_broadcast([P, NC_, D]), ALU.mult))
                v.wait_ge(s_w, 32)
                X = K.X[:].rearrange("p (c d) -> p c d", d=D)
                st.did(v.tensor_tensor(X, X, bias[:].unsqueeze(1).to_broadcast([P, NC_, D]), ALU.add))
                st.settle()
                v.sem_inc(s_r, 1)
                for q in range(nq):
                    n = min(4, NC_ - 4 * q)
                    v.wait_ge(s_o, q + 1)
                    v.tensor_tensor(X[:, 4 * q:4 * q + n, :], X[:, 4 * q:4 * q + n, :], po[q % 2][:, 0:n, :], ALU.add).then_inc(s_x, 1)
                v.wait_ge(s_x, nq)
                vec(v, st)

            @block.tensor
            def _(pe):
                pe.wait_ge(s_r, 1)
                pe.wait_ge(s_w, 32)
                for q in range(nq + 1):
                    if q < nq:
                        if q >= 2:
                            pe.wait_ge(s_c, q - 1)
                        for c in range(min(4, NC_ - 4 * q)):
                            t = pe.transpose(pt[q % 2][:, c, :], R[:, 4 * q + c, 0:P], K.ident[:])
                        t.then_inc(s_t, 1)
                    if q >= 1:
                        pe.wait_ge(s_c, q)
                        if q >= 3:
                            pe.wait_ge(s_x, q - 2)
                        for c in range(min(4, NC_ - 4 * (q - 1))):
                            t = pe.matmul(po[(q - 1) % 2][:, c, :], sT[(q - 1) % 2][:, c, :], w[:], start=True, stop=True)
                        t.then_inc(s_o, 1)

            @block.scalar
            def _(act):
                for q in range(nq):
                    n = min(4, NC_ - 4 * q)
                    act.wait_ge(s_t, q + 1)
                    if q >= 2:
                        act.wait_ge(s_o, q - 1)
                    act.copy(sT[q % 2][:, 0:n, :], pt[q % 2][:, 0:n, :]).then_inc(s_c, 1)
                sca(act)


def add_sums(v, st, K, O, R):
    X = K.X[:].rearrange("p (c d) -> p c d", d=D)
    st.step(v.tensor_tensor(R, R, O.has[:].unsqueeze(2).to_broadcast([P, NC_, D]), ALU.mult))
    st.step(v.tensor_tensor(X, X, R, ALU.add))


def node3(nc, K, R):
    with phase(nc, "n3") as ph:
        b1 = ph.sb("b1", [P, D])
        wide = ph.sb("wide", [P, 4 * 2 * D])
        s_w, s_h, s_wide, s_z = ph.sem("w"), ph.sem("h"), ph.sem("wide"), ph.sem("z")
        sems = ph.sem("own"), ph.sem("var"), ph.sem("std")
        vec, sca = layernorm(None, None, ph, K, sems)

        def out_fn(v, b, n, po):
            v.tensor_copy(K.tA[:, 4 * b:4 * b + n, :], po[:, :, 0:D]).then_inc(s_h, 1)
            return v.tensor_tensor(K.tB[:, 4 * b:4 * b + n, :], po[:, :, D:2 * D],
                                   b1[:].unsqueeze(1).to_broadcast([P, n, D]), ALU.add)

        bp = BlockProduct(ph, K, wide, 2 * D, out_fn)
        with nc.Block() as block:

            @block.sync
            def _(sp):
                sp.wait_ge(s_z, 1)
                for c in range(4):
                    for s in range(2):
                        sp.dma_start(wide[c * D:(c + 1) * D, (2 * c + s) * D:(2 * c + s + 1) * D],
                                     K.in_M1[s * D:(s + 1) * D, :]).then_inc(s_w, 16)
                sp.dma_start(b1[:], K.in_b1.partition_broadcast(P)).then_inc(s_w, 16)

            @block.vector
            def _(v):
                st = Steps(v, sems[0])
                v.memset(wide[:], 0.0).then_inc(s_z, 1)
                add_sums(v, st, K, K.o_d, R)
                vec(v, st)
                v.sem_inc(s_wide, 1)
                v.wait_ge(s_w, 144)
                bp.vector(v)
                v.wait_ge(s_h, NB)

            @block.scalar
            def _(act):
                sca(act)
                bp.scalar(act)

            @block.tensor
            def _(pe):
                pe.wait_ge(s_wide, 1)
                pe.wait_ge(s_w, 144)
                bp.tensor(pe)


def finish(nc, K, R):
    with phase(nc, "fin") as ph:
        s_own, s_x, s_out = ph.sem("own"), ph.sem("x"), ph.sem("out")
        with nc.Block() as block:

            @block.vector
            def _(v):
                st = Steps(v, s_own)
                add_sums(v, st, K, K.o_s, R)
                v.sem_inc(s_x, 1)

            @block.sync
            def _(sp):
                sp.wait_ge(s_x, 1)
                rows = N // NC_
                of = K.out.rearrange("n d -> (n d)")
                for a, b in ((0, 112), (112, rows)):
                    sp.dma_start(of[a * NC_ * D:b * NC_ * D].rearrange("(p f) -> p f", p=b - a), K.X[a:b, :]).then_inc(s_out, 16)
                sp.dma_start(of[rows * NC_ * D:N * D].rearrange("(p f) -> p f", p=1),
                             K.X[rows:rows + 1, 0:(N - rows * NC_) * D]).then_inc(s_out, 16)
                sp.wait_ge(s_out, 48)


def program(nc, args, out, stop=99):
    K = Kit()
    (K.in_x, K.in_src, K.in_dst, K.in_emb, K.in_vec, K.in_nrm, K.in_aw, K.in_w, K.in_fw, K.in_fb, K.in_bias,
     K.in_W1, K.in_W2, K.in_M1, K.in_b1, K.in_g1, K.in_be1, K.in_M2, K.in_b2, K.in_g2, K.in_be2) = args
    K.out = out

    def dram(name, shape, dt=F32):
        return nc.dram_tensor(name, shape, dt).ap()

    K.src, K.dst = dram("src_pad", (EP,), I32), dram("dst_pad", (EP,), I32)
    K.emb, K.vec, K.nrm = dram("emb_pad", (EP * 10,)), dram("vec_pad", (EP * 3,)), dram("nrm_pad", (EP,))
    K.key_rows, K.hi_rows = dram("key_rows", (EP,)), dram("hi_rows", (EP,), BF16)
    K.start_s, K.end_s, K.start_d, K.end_d = (dram(x, (NN,)) for x in ("start_s", "end_s", "start_d", "end_d"))
    K.table0 = dram("table0_rows", (NN, 33))
    K.rows0 = dram("rows0", (EP * 33,))
    K.zeroed = []
    with ExitStack() as res:
        def sb(name, shape, dt=F32):
            return res.enter_context(nc.sbuf_tensor(name, shape, dt))

        K.ident, K.tri, K.lane = sb("ident", [P, P]), sb("tri", [P, P]), sb("lane", [P, P])
        K.lane_b, K.lane_i = sb("lane_b", [P, P], BF16), sb("lane_i", [P, P], I32)
        K.pcol, K.pcol_i = sb("pcol", [P, 1]), sb("pcol_i", [P, 1], I32)
        K.X, K.H = sb("X", [P, NC_ * D]), sb("H", [P, 4 * NB, D])
        K.b0 = sb("b0", [P, NC_])
        K.b1 = sb("b1", [P, NC_, HEADS])
        K.keep_d, K.keep_s = sb("keep_d", [P, EC]), sb("keep_s", [P, EC])
        K.src_f = sb("src_f", [P, EC])
        K.ends = sb("ends", [P, 33 * HEADS])
        K.init = sb("init", [P, 36])
        K.o_d, K.o_s = Order(sb, "od", K.keep_d), Order(sb, "os", K.keep_s)
        rowsM1, rowsM4 = dram("rowsM1", (EP + P, 1)), dram("rowsM4", (EP + P, HEADS))
        rowsS1, rowsS4 = dram("rowsS1", (EP + P, 33)), dram("rowsS4", (EP + P, 33 * HEADS))
        rowsS2 = dram("rowsS2", (EP + P, D))
        fill_d2, fill_d36, fill_d32 = dram("fill_d2", (EP + NN, 2)), dram("fill_d36", (EP + NN, D + HEADS)), dram("fill_d32", (EP + NN, D))
        fill_s8, fill_s32 = dram("fill_s8", (EP + NN, 2 * HEADS)), dram("fill_s32", (EP + NN, D))
        tab2, tab36, tab32, tab8 = dram("tab2", (NN, 2)), dram("tab36", (NN, D + HEADS)), dram("tab32", (NN, D)), dram("tab8", (NN, 2 * HEADS))
        tabA = dram("tabA", (NN, D))
        perm1, perm3 = dram("perm1", (EP, D + HEADS + 1)), dram("perm3", (EP, D))
        K.pos_i = dram("pos_i", (EP,), I32)
        tabB, zrows, yrows = dram("tabB", (NN, D)), dram("zrows", (EP, D)), dram("yrows", (EC // CB * P, 28 * P))
        rowsS3 = dram("rowsS3", (EP + P, D))
        flat = lambda a: a.rearrange("a b -> (a b)")
        K.zeroed = [flat(a) for a in (fill_d2, fill_d36, fill_d32, fill_s8, fill_s32)]
        K.zeroed += [flat(a[EP:EP + P, :]) for a in (rowsM1, rowsM4, rowsS1, rowsS4, rowsS2, rowsS3)]

        with ExitStack() as lay:
            def lsb(name, shape, dt=F32):
                return lay.enter_context(nc.sbuf_tensor(name, shape, dt))

            K.a0 = lsb("a0", [P, EC])
            with ExitStack() as srt:
                def ssb(name, shape, dt=F32):
                    return srt.enter_context(nc.sbuf_tensor(name, shape, dt))

                K.pos, K.dst_f, K.start_s_sb = ssb("pos", [P, EC]), ssb("dst_f", [P, EC]), ssb("start_s_sb", [HI, P])
                K.src_hi, K.src_lo, K.dst_hi, K.dst_lo = (ssb(x, [P, EC], BF16) for x in ("src_hi", "src_lo", "dst_hi", "dst_lo"))
                setup(nc, K)
                load_keys(nc, K)
                table0(nc, K)
                sort_and_gather(nc, K)
                store_pos(nc, K)
            places(nc, K, K.o_d, K.start_d, K.end_d)
            places(nc, K, K.o_s, K.start_s, K.end_s)
            carries(nc, K, K.o_d)

            ex, top, f2, R = lsb("l0_ex", [P, 1, EC]), lsb("l0_top", [P, NC_, 1]), lsb("l0_f2", [P, NC_, 2]), lsb("l0_R", [P, NC_, 33])
            a0 = K.a0[:].unsqueeze(1)
            max_scan(nc, K, "mx0", K.o_d, a0, rowsM1, 1, K.ends[:, 0:1])
            mend_and_read(nc, K, "mr0", K.o_d, rowsM1, 1, K.ends[:, 0:1], ALU.max, top[:])
            bound(nc, K, "bd0", K.b0[:].unsqueeze(2), top[:], f2[:], 1, 0.01)
            put_starts(nc, K, "ps0", K.o_d, f2[:], 2, fill_d2, tab2, K.init[:, 0:2])
            exponentials(nc, K, "ex0", K.o_d, a0, fill_d2, K.init[:, 0:2], 1, 0.01, ex[:])
            weighted_sums(nc, K, "ws0", K.o_d, K.rows0, 33, ex[:], 1, rowsS1, 196)
            mend_and_read(nc, K, "ms0", K.o_d, rowsS1, 33, K.ends[:, 0:33], ALU.add, R[:])
            with ExitStack() as two:
                K.t1 = two.enter_context(nc.sbuf_tensor("t1", [P, NC_, D + HEADS], F32))
                node1(nc, K, R)
                put_starts(nc, K, "ps1", K.o_d, K.t1[:], D + HEADS, fill_d36, tab36, K.init[:])
        if stop < 1:
            return K
        permute(nc, K, "pm1", K.o_d, fill_d36, K.init[:], D + HEADS, D + HEADS + 1, perm1)
        with ExitStack() as lay:
            def lsb(name, shape, dt=F32):
                return lay.enter_context(nc.sbuf_tensor(name, shape, dt))
            vals = lsb("l1_vals", [P, HEADS, EC])
            unpack(nc, K, perm1, D + HEADS + 1, vals[:])
            carries(nc, K, K.o_s)
            with ExitStack() as two:
                top = two.enter_context(nc.sbuf_tensor("l1_top", [P, NC_, HEADS], F32))
                f8 = two.enter_context(nc.sbuf_tensor("l1_f8", [P, NC_, 2 * HEADS], F32))
                max_scan(nc, K, "mx1", K.o_s, vals[:], rowsM4, HEADS, K.ends[:, 0:HEADS])
                mend_and_read(nc, K, "mr1", K.o_s, rowsM4, HEADS, K.ends[:, 0:HEADS], ALU.max, top[:])
                bound(nc, K, "bd1", K.b1[:], top[:], f8[:], HEADS, 0.2)
                put_starts(nc, K, "ps1b", K.o_s, f8[:], 2 * HEADS, fill_s8, tab8, K.init[:, 0:2 * HEADS])
            exponentials(nc, K, "ex1", K.o_s, vals[:], fill_s8, K.init[:, 0:2 * HEADS], HEADS, 0.2, vals[:])
            weighted_sums(nc, K, "ws1", K.o_s, flat(perm1), D + HEADS + 1, vals[:], HEADS, rowsS4, 98)
        with ExitStack() as lay:
            R = lay.enter_context(nc.sbuf_tensor("l1_R", [P, NC_, 33 * HEADS], F32))
            mend_and_read(nc, K, "ms1", K.o_s, rowsS4, 33 * HEADS, K.ends[:], ALU.add, R[:])
            node2(nc, K, R)
        if stop < 2:
            return K
        with ExitStack() as lay:
            def lsb(name, shape, dt=F32):
                return lay.enter_context(nc.sbuf_tensor(name, shape, dt))
            put_starts(nc, K, "ps2", K.o_d, K.H[:, 0:NC_, :], D, fill_d32, tab32, K.init[:, 0:D])
            wall, nv, gain = lsb("wall", [FW, NOUT * KH + KH]), lsb("nv", [P, EC, 3]), lsb("gain", [P, EC])
            edge_weights(nc, K, wall)
            unit_vectors(nc, K, nv[:], gain[:])
            edge_network(nc, K, K.o_d, tab32, fill_d32, K.init[:, 0:D], wall, nv[:], gain[:], rowsS2)
        with ExitStack() as lay:
            def lsb(name, shape, dt=F32):
                return lay.enter_context(nc.sbuf_tensor(name, shape, dt))
            R = lsb("l2_R", [P, NC_, D])
            mend_and_read(nc, K, "ms2", K.o_d, rowsS2, D, K.ends[:, 0:D], ALU.add, R[:])
            K.tA, K.tB = lsb("tA", [P, NC_, D]), lsb("tB", [P, NC_, D])
            node3(nc, K, R[:])
            put_starts(nc, K, "psB", K.o_d, K.tB[:], D, fill_d32, tabB, K.init[:, 0:D])
            permute(nc, K, "pm3", K.o_d, fill_d32, K.init[:, 0:D], D, D, perm3)
            put_starts(nc, K, "psA", K.o_s, K.tA[:], D, fill_s32, tabA, K.init[:, 0:D])
        if stop < 3:
            return K
        with ExitStack() as lay:
            def lsb(name, shape, dt=F32):
                return lay.enter_context(nc.sbuf_tensor(name, shape, dt))
            stats, coef, sums = lsb("stats", [1, 2, 448]), lsb("coef", [P, 4]), lsb("sums", [P, 2, EC // 16])
            first_sums(nc, K, K.o_s, fill_s32, K.init[:, 0:D], perm3, zrows, stats[:])
            norm1(nc, K, stats[:], zrows, coef[:, 0:2])
            second_product(nc, K, zrows, coef[:, 0:2], yrows, sums[:])
            norm2(nc, K, sums[:], yrows, coef[:, 2:4])
            last_sums(nc, K, K.o_s, yrows, coef[:, 2:4], rowsS3)
            R = lsb("l3_R", [P, NC_, D])
            mend_and_read(nc, K, "ms3", K.o_s, rowsS3, D, K.ends[:, 0:D], ALU.add, R[:])
            finish(nc, K, R[:])
    return K


_INS = ["x", "src", "dst", "edge_attr_10", "edge_attr_3", "edge_weight", "L0_gnn_attn_w", "L1_gnn_w", "L1_gnn_fc_w",
        "L1_gnn_fc_b", "L1_gnn_bias", "L2_gnn_W1", "L2_gnn_W2", "L3_gnn_W1", "L3_gnn_b1", "L3_gnn_gamma1",
        "L3_gnn_beta1", "L3_gnn_W2", "L3_gnn_b2", "L3_gnn_gamma2", "L3_gnn_beta2"]


def kernel(**inputs):
    import numpy as _np
    import concourse.bacc as _bacc
    from concourse import mybir as _mybir
    from concourse.bass_utils import run_bass_kernel_spmd as _run

    nc = _bacc.Bacc("TRN2", target_bir_lowering=False, num_devices=1)
    arrays, args = {}, []
    for name in _INS:
        a = _np.ascontiguousarray(inputs[name])
        arrays[f"in_{name}_dram"] = a
        args.append(nc.dram_tensor(f"in_{name}_dram", a.shape, _mybir.dt.from_np(a.dtype), kind="ExternalInput").ap())
    out = nc.dram_tensor("out_0_dram", (N, D), F32, kind="ExternalOutput").ap()
    program(nc, args, out)
    r = _run(nc, [arrays], core_ids=[0])
    return r.results[0]["out_0_dram"]
```

```python
import math
from contextlib import ExitStack

import concourse.bass as bass
from concourse import mybir

ALU = mybir.AluOpType
ACT = mybir.ActivationFunctionType
AX = mybir.AxisListType
F32 = mybir.dt.float32
BF16 = mybir.dt.bfloat16
I32 = mybir.dt.int32

P = 128
N, E, D = 12500, 200000, 32
EC = 1568
EP = P * EC
NPAD = EP - E
NC_ = 98
NN = P * NC_
NB = -(-NC_ // 4)
HI = NN // P
SG = 28
STAGES = EC // SG
RT = 16
NEG = -3.0e38
HEADS = 4
LN_EPS = 1e-5


class Kit:
    pass


def phase(nc, name):
    return Phase(nc, name)


class Phase:

    def __init__(self, nc, name):
        self.nc, self.name, self.stack, self.sems = nc, name, ExitStack(), []

    def __enter__(self):
        self.stack.__enter__()
        return self

    def sb(self, name, shape, dt=F32):
        return self.stack.enter_context(self.nc.sbuf_tensor(f"{self.name}_{name}", shape, dt))

    def ps(self, name, shape, dt=F32):
        return self.stack.enter_context(self.nc.psum_tensor(f"{self.name}_{name}", shape, dt))

    def sem(self, name):
        s = self.nc.alloc_semaphore(f"{self.name}_{name}")
        self.sems.append(s)
        return s

    def __exit__(self, *a):
        if a[0] is None:
            self.nc.clear_and_free_semaphores(self.sems)
            self.nc.all_engine_barrier()
        return self.stack.__exit__(*a)


class Steps:

    def __init__(self, eng, sem):
        self.eng, self.sem, self.n, self.base = eng, sem, 0, 0

    def did(self, ins):
        ins.then_inc(self.sem, 1)
        self.n += 1

    def settle(self):
        self.eng.wait_ge(self.sem, self.base + self.n)

    def step(self, ins):
        self.did(ins)
        self.settle()

    def loop(self, i, per):
        self.outer, self.per = self.n, per
        self.base = i * per

    def end_loop(self, times):
        assert self.n - self.outer == self.per, (self.n - self.outer, self.per)
        self.n, self.base = self.outer + self.per * times, 0



def setup(nc, K):
    with phase(nc, "setup") as ph:
        padi = ph.sb("padi", [64, NPAD // 64], I32)
        padf = ph.sb("padf", [64, NPAD // 64 * 10])
        s_const, s_copy, s_x, s_sel = ph.sem("const"), ph.sem("copy"), ph.sem("x"), ph.sem("sel")
        with nc.Block() as block:

            @block.vector
            def _(v):
                v.memset(padi[:], N).then_inc(s_const, 1)
                v.memset(padf[:], 1.0).then_inc(s_const, 1)
                v.memset(K.X[:], 0.0).then_inc(s_const, 1)
                v.memset(K.H[:], 0.0).then_inc(s_const, 1)

            @block.gpsimd
            def _(g):
                g.memset(K.ident[:], 0.0).then_inc(s_sel, 1)
                g.memset(K.tri[:], 1.0).then_inc(s_sel, 1)
                g.iota(K.pcol_i[:], [[0, 1]], 0, 1).then_inc(s_sel, 1)
                g.iota(K.lane_i[:], [[1, P]], 0, 0).then_inc(s_sel, 1)
                g.wait_ge(s_sel, 4)
                g.affine_select(out=K.ident[:], in_=K.ident[:], compare_op=ALU.not_equal, fill=1.0,
                                base=0, pattern=[[-1, P]], channel_multiplier=1).then_inc(s_sel, 1)
                g.affine_select(out=K.tri[:], in_=K.tri[:], compare_op=ALU.is_gt, fill=0.0,
                                base=0, pattern=[[-1, P]], channel_multiplier=1).then_inc(s_sel, 1)
                g.tensor_copy(K.pcol[:], K.pcol_i[:]).then_inc(s_sel, 1)
                g.tensor_copy(K.lane[:], K.lane_i[:]).then_inc(s_sel, 1)
                g.tensor_copy(K.lane_b[:], K.lane_i[:]).then_inc(s_sel, 1)
                g.wait_ge(s_sel, 9)

            @block.sync
            def _(sp):
                n = 0

                def copy(dst, src):
                    nonlocal n
                    sp.dma_start(dst, src).then_inc(s_copy, 16)
                    n += 16

                copy(K.src[0:E].rearrange("(a b) -> a b", a=64), K.in_src.rearrange("(a b) -> a b", a=64))
                copy(K.dst[0:E].rearrange("(a b) -> a b", a=64), K.in_dst.rearrange("(a b) -> a b", a=64))
                copy(K.emb[0:E * 10].rearrange("(a b) -> a b", a=128), K.in_emb.rearrange("e w -> (e w)").rearrange("(a b) -> a b", a=128))
                copy(K.vec[0:E * 3].rearrange("(a b) -> a b", a=64), K.in_vec.rearrange("e w -> (e w)").rearrange("(a b) -> a b", a=64))
                copy(K.nrm[0:E].rearrange("(a b) -> a b", a=64), K.in_nrm.rearrange("(a b) -> a b", a=64))
                sp.wait_ge(s_const, 2)
                c = NPAD // 64
                copy(K.src[E:EP].rearrange("(a b) -> a b", a=64), padi[:])
                copy(K.dst[E:EP].rearrange("(a b) -> a b", a=64), padi[:])
                copy(K.emb[E * 10:EP * 10].rearrange("(a b) -> a b", a=64), padf[:])
                copy(K.vec[E * 3:EP * 3].rearrange("(a b) -> a b", a=64), padf[:, 0:3 * c])
                copy(K.nrm[E:EP].rearrange("(a b) -> a b", a=64), padf[:, 0:c])
                sp.wait_ge(s_copy, n)

            @block.scalar
            def _(act):
                act.wait_ge(s_const, 4)
                n = 0
                rows = N // NC_
                xf = K.in_x.rearrange("n d -> (n d)")
                for a, b in ((0, 112), (112, rows)):
                    act.dma_start(K.X[a:b, :], xf[a * NC_ * D:b * NC_ * D].rearrange("(p f) -> p f", p=b - a)).then_inc(s_x, 16)
                    n += 16
                left = (N - rows * NC_) * D
                act.dma_start(K.X[rows:rows + 1, 0:left], xf[rows * NC_ * D:N * D].rearrange("(p f) -> p f", p=1)).then_inc(s_x, 16)
                act.wait_ge(s_x, n + 16)


def load_keys(nc, K):
    with phase(nc, "keys") as ph:
        ki = ph.sb("ki", [P, 2, EC], I32)
        t = ph.sb("t", [P, EC], I32)
        lo = ph.sb("lo", [P, EC], I32)
        hi_f = ph.sb("hi_f", [P, EC])
        prev = ph.sb("prev", [P, 1], I32)
        prev_f = ph.sb("prev_f", [P, 1])
        kT = ph.sb("kT", [112, 14, P])
        hT = ph.sb("hT", [112, 14, P], BF16)
        pt = [ph.ps(f"pt{i}", [112, 2, P]) for i in range(2)]
        s_in, s_own, s_tr, s_ev, s_out, s_m = (ph.sem(x) for x in ("in", "own", "tr", "ev", "out", "m"))
        with nc.Block() as block:

            @block.sync
            def _(sp):
                sp.dma_start(ki[:, 0, :], K.src.rearrange("(p c) -> p c", p=P)).then_inc(s_in, 16)
                sp.dma_start(ki[:, 1, :], K.dst.rearrange("(p c) -> p c", p=P)).then_inc(s_in, 16)
                sp.wait_ge(s_m, 1)
                sp.dma_start(prev[1:P, :], K.dst.rearrange("(p c) -> p c", p=P)[0:P - 1, EC - 1:EC],
                             allow_slow_non_contiguous=True).then_inc(s_in, 16)
                sp.wait_ge(s_ev, 28)
                sp.dma_start(K.key_rows.rearrange("(b c p) -> c b p", c=112, p=P), kT[:]).then_inc(s_out, 16)
                sp.dma_start(K.hi_rows.rearrange("(b c p) -> c b p", c=112, p=P), hT[:]).then_inc(s_out, 16)
                sp.wait_ge(s_out, 32)

            @block.vector
            def _(v):
                st = Steps(v, s_own)
                v.memset(prev[:], -1).then_inc(s_m, 1)
                v.wait_ge(s_in, 48)
                st.did(v.tensor_copy(K.src_f[:], ki[:, 0, :]))
                st.did(v.tensor_copy(K.dst_f[:], ki[:, 1, :]))
                st.did(v.tensor_copy(prev_f[:], prev[:]))
                st.did(v.tensor_copy(K.o_d.first_i[:], ki[:, 1, 0:1]))
                for n, (hb, lb) in enumerate(((K.src_hi, K.src_lo), (K.dst_hi, K.dst_lo))):
                    st.step(v.tensor_scalar(t[:], ki[:, n, :], 7, None, ALU.logical_shift_right))
                    st.step(v.tensor_scalar(lo[:], ki[:, n, :], P - 1, None, ALU.bitwise_and))
                    st.did(v.tensor_copy(hb[:], t[:]))
                    if n == 0:
                        st.did(v.tensor_copy(hi_f[:], t[:]))
                    st.step(v.tensor_copy(lb[:], lo[:]))
                st.did(v.tensor_tensor(K.keep_d[:, 1:EC], K.dst_f[:, 1:EC], K.dst_f[:, 0:EC - 1], ALU.is_equal))
                st.did(v.tensor_tensor(K.keep_d[:, 0:1], K.dst_f[:, 0:1], prev_f[:], ALU.is_equal))
                st.settle()
                for b in range(14):
                    v.wait_ge(s_tr, b + 1)
                    v.tensor_copy(kT[:, b, :], pt[b % 2][:, 0, :]).then_inc(s_ev, 1)
                    v.tensor_copy(hT[:, b, :], pt[b % 2][:, 1, :]).then_inc(s_ev, 1)

            @block.tensor
            def _(pe):
                pe.wait_ge(s_own, 11)
                for b in range(14):
                    if b >= 2:
                        pe.wait_ge(s_ev, 2 * (b - 1))
                    pe.transpose(pt[b % 2][:, 0, :], K.src_f[:, 112 * b:112 * b + 112], K.ident[:])
                    pe.transpose(pt[b % 2][:, 1, :], hi_f[:, 112 * b:112 * b + 112], K.ident[:]).then_inc(s_tr, 1)



def one_hots(v, K, out_lo, out_hi, lo, hi, col):
    v_lo = lo[:, bass.ds(col, RT)].unsqueeze(2).to_broadcast([P, RT, P])
    v_hi = hi[:, bass.ds(col, RT)].unsqueeze(2).to_broadcast([P, RT, HI])
    lane = K.lane_b[:].unsqueeze(1).to_broadcast([P, RT, P])
    a = v.tensor_tensor(out_lo, v_lo, lane, ALU.is_equal)
    b = v.tensor_tensor(out_hi, v_hi, lane[:, :, 0:HI], ALU.is_equal)
    return a, b


def half_one_hot(v, K, out, values, t, h):
    W, w = RT // 2, out.shape[2]
    x = values[:, bass.ds(t * RT + h * W, W)].unsqueeze(2).to_broadcast([P, W, w])
    return v.tensor_tensor(out[:, h * W:(h + 1) * W, :], x, K.lane_b[:, 0:w].unsqueeze(1).to_broadcast([P, W, w]), ALU.is_equal)


class Histogram:

    def __init__(self, nc, K, ph, name, lo, hi, start_out, end_out, start_sb):
        self.nc, self.K, self.ph, self.name, self.lo, self.hi, self.start_out, self.end_out, self.start_sb = nc, K, ph, name, lo, hi, start_out, end_out, start_sb
        self.oh_lo = [ph.sb(f"{name}_oh_lo{k}", [P, RT, P], BF16) for k in range(2)]
        self.oh_hi = [ph.sb(f"{name}_oh_hi{k}", [P, RT, HI], BF16) for k in range(2)]
        self.cnt = ph.ps(f"{name}_cnt", [HI, P])
        self.off = ph.ps(f"{name}_off", [HI, 1])
        self.cnt_sb = ph.sb(f"{name}_cnt_sb", [HI, P])
        self.incl = ph.sb(f"{name}_incl", [HI, P])
        self.end_sb = ph.sb(f"{name}_end_sb", [HI, P])
        self.ones = ph.sb(f"{name}_ones", [HI, P])
        self.tri_t = ph.sb(f"{name}_tri_t", [HI, HI])
        self.s_oh = [ph.sem(f"{name}_oh{k}") for k in range(2)]
        self.s_used = [ph.sem(f"{name}_used{k}") for k in range(2)]
        self.s_zero, self.s_cnt, self.s_own, self.s_tot, self.s_off, self.s_done, self.s_out = (
            ph.sem(f"{name}_{x}") for x in ("zero", "cnt", "own", "tot", "off", "done", "out"))

    def vector_start(self, v):
        S = self
        for k in range(2):
            v.sem_inc(S.s_used[k], 1)
        self.st = Steps(v, S.s_own)
        v.memset(S.end_sb[:], 0.0).then_inc(S.s_zero, 1)
        self.st.did(v.memset(S.ones[:], 1.0))
        self.st.did(v.tensor_scalar(S.tri_t[:], S.K.lane[0:HI, 0:HI], S.K.pcol[0:HI, :], None, ALU.is_gt))

    def vector_rows(self, v):
        S = self
        with v.Fori(0, EC // RT // 2) as i:
            for k in range(2):
                v.wait_ge(S.s_used[k], i + 1)
                a, b = one_hots(v, S.K, S.oh_lo[k][:], S.oh_hi[k][:], S.lo, S.hi, (i * 2 + k) * RT)
                a.then_inc(S.s_oh[k], 1)
                b.then_inc(S.s_oh[k], 1)

    def vector_end(self, v):
        S, st = self, self.st
        v.wait_ge(S.s_cnt, 1)
        st.step(v.tensor_copy(S.cnt_sb[:], S.cnt[:]))
        st.step(v.tensor_tensor_scan(S.incl[:], S.ones[:], S.cnt_sb[:], 0.0, ALU.mult, ALU.add))
        v.sem_inc(S.s_tot, 1)
        v.wait_ge(S.s_off, 1)
        st.step(v.tensor_scalar(S.end_sb[:], S.incl[:], S.off[:, 0:1], None, ALU.add))
        v.tensor_tensor(S.start_sb[:], S.end_sb[:], S.cnt_sb[:], ALU.subtract).then_inc(S.s_done, 1)

    def tensor_start(self, pe):
        S = self
        pe.wait_ge(S.s_zero, 1)
        pe.matmul(S.cnt[:], S.end_sb[:, 0:HI], S.end_sb[:], start=True, stop=False, skip_group_check=True)

    def count(self, pe, k, j):
        S = self
        return pe.matmul(S.cnt[:], S.oh_hi[k][:, j, :], S.oh_lo[k][:, j, :], start=False, stop=False, skip_group_check=True)

    def tensor_rows(self, pe):
        S = self
        with pe.Fori(0, EC // RT // 2) as i:
            for k in range(2):
                pe.wait_ge(S.s_oh[k], i * 2 + 2)
                for j in range(RT):
                    mm = S.count(pe, k, j)
                mm.then_inc(S.s_used[k], 1)

    def tensor_end(self, pe):
        S = self
        pe.matmul(S.cnt[:], S.ones[:, 0:HI], S.end_sb[:], start=False, stop=True, skip_group_check=True).then_inc(S.s_cnt, 1)
        pe.wait_ge(S.s_tot, 1)
        pe.matmul(S.off[:], S.tri_t[:], S.incl[:, P - 1:P], start=True, stop=True).then_inc(S.s_off, 1)

    def store(self, q):
        S = self
        q.wait_ge(S.s_done, 1)
        q.dma_start(S.start_out.rearrange("(h l) -> h l", l=P), S.start_sb[:]).then_inc(S.s_out, 16)
        q.dma_start(S.end_out.rearrange("(h l) -> h l", l=P), S.end_sb[:]).then_inc(S.s_out, 16)
        q.wait_ge(S.s_out, 32)


class Ranks:

    def __init__(self, nc, K, ph, hist, other):
        self.nc, self.K, self.ph, self.hist, self.other = nc, K, ph, hist, other
        self.oh_lo, self.oh_hi = hist.oh_lo, hist.oh_hi
        self.oh_hi_t = [ph.sb(f"rk_oh_hi_t{k}", [HI, RT * P]) for k in range(2)]
        self.krow = [ph.sb(f"rk_krow{k}", [P, RT * P]) for k in range(2)]
        self.hrow = [ph.sb(f"rk_hrow{k}", [HI, RT * P], BF16) for k in range(2)]
        self.junk = [ph.sb(f"rk_junk{k}", [P, P]) for k in range(4)]
        self.before = ph.sb("rk_before", [P, 2 * RT])
        self.own = ph.sb("rk_own", [P, 2 * RT])
        self.run_sb = [ph.sb(f"rk_run_sb{k}", [HI, P]) for k in range(2)]
        self.run = ph.ps("rk_run", [HI, P])
        self.look = [ph.ps(f"rk_look{k}", [P, P]) for k in range(2)]
        names = ("oh", "used", "rows", "rows_used")
        self.s_oh, self.s_used, self.s_rows, self.s_rows_used = ([ph.sem(f"rk_{x}{k}") for k in range(2)] for x in names)
        self.s_run, self.s_copied, self.s_look, self.s_read, self.s_own, self.s_junk = (
            ph.sem(f"rk_{x}") for x in ("run", "copied", "look", "read", "own", "junk"))

    def vector(self, v):
        S, K = self, self.K
        for k in range(2):
            v.sem_inc(S.s_used[k], 1)
        v.sem_inc(S.s_read, 2)
        v.sem_inc(S.s_junk, 2)
        st = Steps(v, S.s_own)
        X = S.other
        half = RT * P // 2

        def build(i, k, part):
            kind, h = part // 2, part % 2
            t = i * 2 + k
            if part == 0:
                v.wait_ge(S.s_used[k], i + 1)
            if kind == 0:
                half_one_hot(v, K, S.oh_lo[k][:], K.src_lo, t, h).then_inc(S.s_oh[k], 1)
            elif kind == 1:
                half_one_hot(v, K, S.oh_hi[k][:], K.src_hi, t, h).then_inc(S.s_oh[k], 1)
            elif kind == 2:
                if h == 0:
                    v.wait_ge(X.s_used[k], i + 1)
                half_one_hot(v, K, X.oh_lo[k][:], X.lo, t, h).then_inc(X.s_oh[k], 1)
            elif kind == 3:
                half_one_hot(v, K, X.oh_hi[k][:], X.hi, t, h).then_inc(X.s_oh[k], 1)
            else:
                v.wait_ge(S.s_rows[k], 32 * i + 32)
                v.tensor_scalar(S.oh_hi_t[k][:, h * half:(h + 1) * half], S.hrow[k][:, h * half:(h + 1) * half],
                                K.pcol[0:HI, :], None, ALU.is_equal).then_inc(S.s_oh[k], 1)

        def turn(i, k, to):
            col = (i * 2 + k) * RT
            for j in range(RT):
                c = k * RT + j
                v.wait_ge(S.s_junk, i * (2 * RT) + c + 1)
                v.scalar_tensor_tensor(out=S.junk[j % 2][:], in0=S.krow[k][:, j * P:(j + 1) * P],
                                       scalar=K.src_f[:, bass.ds(col + j, 1)], in1=K.tri[:],
                                       op0=ALU.is_equal, op1=ALU.mult,
                                       accum_out=S.own[:, c:c + 1]).then_inc(S.s_junk, 1)
                v.wait_ge(S.s_look, i * (2 * RT) + c + 1)
                v.tensor_tensor_reduce(out=S.junk[2 + j % 2][:], in0=S.look[j % 2][:], in1=S.oh_lo[k][:, j, :],
                                       scale=1.0, scalar=0.0, op0=ALU.mult, op1=ALU.add,
                                       accum_out=S.before[:, c:c + 1]).then_inc(S.s_read, 1)
                if to is not None and j % 3 != 2 and j < 15:
                    build(*to, j // 3 * 2 + j % 3)
            v.wait_ge(S.s_junk, i * (2 * RT) + k * RT + RT + 2)
            v.wait_ge(S.s_read, i * (2 * RT) + k * RT + RT + 2)
            st.step(v.tensor_tensor(K.pos[:, bass.ds(col, RT)], S.before[:, k * RT:k * RT + RT],
                                    S.own[:, k * RT:k * RT + RT], ALU.add))
            v.sem_inc(S.s_rows_used[k], 1)

        steps = EC // RT // 2
        for part in range(10):
            build(0, 0, part)
        with v.Fori(0, steps - 1) as i:
            st.loop(i, 2)
            turn(i, 0, (i, 1))
            turn(i, 1, (i + 1, 0))
        st.end_loop(steps - 1)
        turn(steps - 1, 0, (steps - 1, 1))
        turn(steps - 1, 1, None)

    def tensor(self, pe):
        S, K = self, self.K
        X = S.other
        pe.wait_ge(S.hist.s_done, 1)
        pe.matmul(S.run[:], K.ident[0:HI, 0:HI], S.hist.start_sb[:], start=True, stop=False,
                  skip_group_check=True).then_inc(S.s_run, 1)
        with pe.Fori(0, EC // RT // 2) as i:
            for k in range(2):
                pe.wait_ge(S.s_oh[k], i * 6 + 6)
                for j in range(RT):
                    c = k * RT + j
                    pe.wait_ge(S.s_copied, i * (2 * RT) + c + 1)
                    pe.matmul(S.run[:], S.oh_hi[k][:, j, :], S.oh_lo[k][:, j, :], start=False, stop=False,
                              skip_group_check=True).then_inc(S.s_run, 1)
                    pe.wait_ge(S.s_read, i * (2 * RT) + c + 1)
                    mm = pe.matmul(S.look[j % 2][:], S.oh_hi_t[k][:, j * P:(j + 1) * P], S.run_sb[j % 2][:],
                                   start=True, stop=True)
                    mm.then_inc(S.s_look, 1)
                    if j == 0:
                        pe.wait_ge(X.s_oh[k], i * 4 + 4)
                    mm = X.count(pe, k, j)
                mm.then_inc(X.s_used[k], 1)
                pe.wait_ge(S.s_look, i * (2 * RT) + (k + 1) * RT)
                pe.sem_inc(S.s_used[k], 1)



class Gather:

    def __init__(self, nc, K, ph, table, width, idx):
        self.nc, self.K, self.ph, self.table, self.width, self.idx = nc, K, ph, table, width, idx
        self.ix = [ph.sb(f"g_ix{k}", [P, SG], I32) for k in range(2)]
        self.st = [ph.sb(f"g_st{k}", [P, SG, width]) for k in range(2)]
        names = ("ix_in", "rows", "out", "free")
        self.s_ix, self.s_rows, self.s_out, self.s_free = ([ph.sem(f"g_{x}{k}") for k in range(2)] for x in names)

    def gpsimd(self, g):
        S = self
        with g.Fori(0, STAGES // 2) as i:
            for k in range(2):
                g.wait_ge(S.s_ix[k], 16 * i + 16)
                g.wait_ge(S.s_free[k], i + 1)
                g.nop(nofuse=True)
                for j in range(SG):
                    g.indirect_dma_start(S.st[k][:, j, :], None, S.table,
                                         bass.IndirectOffsetOnAxis(ap=S.ix[k][:, j:j + 1], axis=0)).then_inc(S.s_rows[k], 16)

    def load_index(self, sp, k, t):
        sp.dma_start(self.ix[k][:], self.idx.rearrange("(p c) -> p c", p=P)[:, bass.ds(t * SG, SG)]).then_inc(self.s_ix[k], 16)


def store_gathered(G, sp, out, attn):
    w = G.width
    for k in range(2):
        G.load_index(sp, k, k)
        sp.sem_inc(G.s_free[k], 1)

    def turn(i, last):
        for k in range(2):
            t = i * 2 + k
            sp.wait_ge(G.s_rows[k], (16 * SG) * i + 16 * SG)
            sp.dma_start(out.rearrange("(p c) -> p c", p=P)[:, bass.ds(t * (SG * w), SG * w)],
                         G.st[k][:].rearrange("p j w -> p (j w)")).then_inc(G.s_out[k], 16)
            sp.dma_start(attn[:, bass.ds(t * SG, SG)].unsqueeze(2), G.st[k][:, :, w - 1:w],
                         allow_slow_non_contiguous=True).then_inc(G.s_out[k], 16)
            if not last:
                G.load_index(sp, k, t + 2)
            sp.wait_ge(G.s_out[k], 32 * i + 32)
            if not last:
                sp.sem_inc(G.s_free[k], 1)

    with sp.Fori(0, STAGES // 2 - 1) as i:
        turn(i, False)
    turn(STAGES // 2 - 1, True)


def sort_and_gather(nc, K):
    with phase(nc, "sort") as ph:
        G = Gather(nc, K, ph, K.table0, 33, K.src)
        hs = Histogram(nc, K, ph, "hs", K.src_lo, K.src_hi, K.start_s, K.end_s, K.start_s_sb)
        hd = Histogram(nc, K, ph, "hd", K.dst_lo, K.dst_hi, K.start_d, K.end_d, ph.sb("start_d_sb", [HI, P]))
        rk = Ranks(nc, K, ph, hs, hd)
        ZW = 6272
        zero = ph.sb("zero", [P, ZW])
        s_z, s_zero = ph.sem("z"), ph.sem("zeroed")
        with nc.Block() as block:

            @block.gpsimd
            def _(g):
                G.gpsimd(g)

            @block.sync
            def _(sp):
                store_gathered(G, sp, K.rows0, K.a0)

            @block.vector
            def _(v):
                v.memset(zero[:], 0.0).then_inc(s_z, 1)
                hs.vector_start(v)
                hs.vector_rows(v)
                hs.vector_end(v)
                hd.vector_start(v)
                rk.vector(v)
                hd.vector_end(v)

            @block.tensor
            def _(pe):
                hs.tensor_start(pe)
                hs.tensor_rows(pe)
                hs.tensor_end(pe)
                hd.tensor_start(pe)
                rk.tensor(pe)
                hd.tensor_end(pe)

            @block.scalar
            def _(act):
                act.wait_ge(s_z, 1)
                k = 0
                for arr in K.zeroed:
                    at, total = 0, arr.shape[0]
                    while at < total:
                        w = min(ZW * P, total - at)
                        assert w % P == 0
                        act.dma_start(arr[at:at + w].rearrange("(p f) -> p f", p=P), zero[:, 0:w // P]).then_inc(s_zero, 16)
                        at += w
                        k += 16
                hs.store(act)
                rank_rows_and_counts(rk, act)
                hd.store(act)
                act.wait_ge(s_zero, k)


def rank_rows_and_counts(rk, act):
    S = rk

    def load(k, t):
        at = t * (RT * P)
        act.dma_start(S.krow[k][:], S.K.key_rows[bass.ds(at, RT * P)].partition_broadcast(P)).then_inc(S.s_rows[k], 16)
        act.dma_start(S.hrow[k][:], S.K.hi_rows[bass.ds(at, RT * P)].partition_broadcast(HI)).then_inc(S.s_rows[k], 16)

    def turn(i, last):
        for k in range(2):
            for j in range(RT):
                c = k * RT + j
                act.wait_ge(S.s_run, i * (2 * RT) + c + 1)
                act.copy(S.run_sb[j % 2][:], S.run[:]).then_inc(S.s_copied, 1)
            if not last:
                act.wait_ge(S.s_rows_used[k], i + 1)
                load(k, i * 2 + k + 2)

    load(0, 0)
    load(1, 1)
    steps = EC // RT // 2
    with act.Fori(0, steps - 1) as i:
        turn(i, False)
    turn(steps - 1, True)



def layernorm(v, act, ph, K, sems):
    s_own, s_var, s_std = sems
    mean, sq = ph.sb("mean", [P, NC_]), ph.sb("sq", [P, NC_, D])
    var, std, rstd, eps = (ph.sb(x, [P, NC_ if x != "eps" else 1]) for x in ("var", "std", "rstd", "eps"))
    X = K.X[:].rearrange("p (c d) -> p c d", d=D)
    H = K.H[:, 0:NC_, :]

    def wide(a):
        return a[:].unsqueeze(2).to_broadcast([P, NC_, D])

    def vector(v, st):
        st.did(v.memset(eps[:], LN_EPS))
        st.step(v.tensor_reduce(mean[:], X, AX.X, ALU.add))
        st.step(v.tensor_scalar(mean[:], mean[:], 1.0 / D, None, ALU.mult))
        st.step(v.tensor_tensor(H, X, wide(mean), ALU.subtract))
        st.step(v.tensor_tensor(sq[:], H, H, ALU.mult))
        st.step(v.tensor_reduce(var[:], sq[:], AX.X, ALU.add))
        v.sem_inc(s_var, 1)
        v.wait_ge(s_std, 1)
        st.step(v.reciprocal(rstd[:], std[:]))
        st.step(v.tensor_tensor(H, H, wide(rstd), ALU.mult))
        st.step(v.tensor_scalar(H, H, 0.0, None, ALU.max))

    def scalar(act):
        act.wait_ge(s_var, 1)
        act.activation(std[:], var[:], ACT.Sqrt, bias=eps[:, 0:1], scale=1.0 / D).then_inc(s_std, 1)

    return vector, scalar


def table0(nc, K):
    with phase(nc, "t0") as ph:
        aw = ph.sb("aw", [P, 2 * D])
        prod = ph.sb("prod", [P, NC_, D])
        tab = ph.sb("tab", [P, NC_, D + 1])
        s_w, s_tab, s_out = ph.sem("w"), ph.sem("tab"), ph.sem("out")
        sems = ph.sem("own"), ph.sem("var"), ph.sem("std")
        vec, sca = layernorm(None, None, ph, K, sems)
        with nc.Block() as block:

            @block.sync
            def _(sp):
                sp.dma_start(aw[:], K.in_aw.partition_broadcast(P)).then_inc(s_w, 16)
                sp.wait_ge(s_tab, 1)
                sp.dma_start(K.table0.rearrange("(p c) w -> p (c w)", p=P), tab[:].rearrange("p c w -> p (c w)")).then_inc(s_out, 16)
                sp.wait_ge(s_out, 16)

            @block.vector
            def _(v):
                st = Steps(v, sems[0])
                vec(v, st)
                v.wait_ge(s_w, 16)
                H = K.H[:, 0:NC_, :]
                st.did(v.tensor_copy(tab[:, :, 0:D], H))
                for s, out in ((0, tab[:, :, D]), (1, K.b0[:])):
                    w = aw[:, s * D:(s + 1) * D].unsqueeze(1).to_broadcast([P, NC_, D])
                    st.step(v.tensor_tensor(prod[:], H, w, ALU.mult))
                    st.step(v.tensor_reduce(out, prod[:], AX.X, ALU.add))
                v.sem_inc(s_tab, 1)

            @block.scalar
            def _(act):
                sca(act)




class Order:

    def __init__(self, sb, name, keep):
        self.name, self.keep = name, keep
        self.fill_i = sb(f"{name}_fill_i", [P, NC_], I32)
        self.last_i = sb(f"{name}_last_i", [P, NC_], I32)
        self.has = sb(f"{name}_has", [P, NC_])
        self.mend_i = sb(f"{name}_mend_i", [P, 1], I32)
        self.span = sb(f"{name}_span", [P, P])
        self.span_neg = sb(f"{name}_span_neg", [P, P])
        self.first_i = sb(f"{name}_first_i", [P, 1], I32)


def places(nc, K, O, start, end):
    with phase(nc, f"pl_{O.name}") as ph:
        a, b, t, spare = (ph.sb(x, [P, NC_]) for x in "abts")
        spare_i = ph.sb("spare_i", [P, NC_], I32)
        s_in, s_own, s_io = ph.sem("in"), ph.sem("own"), ph.sem("io")
        with nc.Block() as block:

            @block.gpsimd
            def _(g):
                g.iota(spare_i[:], [[1, NC_]], EP, NC_).then_inc(s_io, 1)

            @block.sync
            def _(sp):
                sp.dma_start(a[:], start.rearrange("(p c) -> p c", p=P)).then_inc(s_in, 16)
                sp.dma_start(b[:], end.rearrange("(p c) -> p c", p=P)).then_inc(s_in, 16)

            @block.vector
            def _(v):
                st = Steps(v, s_own)
                v.wait_ge(s_in, 32)
                v.wait_ge(s_io, 1)
                st.did(v.tensor_copy(spare[:], spare_i[:]))
                st.did(v.tensor_tensor(O.has[:], b[:], a[:], ALU.is_gt))
                st.step(v.tensor_scalar(t[:], b[:], -1.0, 0.0, ALU.add, ALU.max))
                st.step(v.tensor_copy(O.last_i[:], t[:]))
                st.step(v.tensor_tensor(a[:], a[:], spare[:], ALU.subtract))
                st.step(v.tensor_tensor(a[:], a[:], O.has[:], ALU.mult))
                st.step(v.tensor_tensor(a[:], a[:], spare[:], ALU.add))
                st.step(v.tensor_copy(O.fill_i[:], a[:]))


def carries(nc, K, O):
    with phase(nc, f"ca_{O.name}") as ph:
        lead = ph.sb("lead", [P, EC])
        f, m, base, spare, r = (ph.sb(x, [P, 1]) for x in ("f", "m", "base", "spare", "r"))
        wide = ph.sb("wide", [P, P])
        pt = ph.ps("pt", [P, P])
        s_own, s_wide, s_t = ph.sem("own"), ph.sem("wide"), ph.sem("t")
        with nc.Block() as block:

            @block.vector
            def _(v):
                st = Steps(v, s_own)
                st.step(v.tensor_tensor_scan(lead[:], O.keep[:], O.keep[:], 1.0, ALU.mult, ALU.mult))
                st.step(v.tensor_reduce(f[:], lead[:], AX.X, ALU.add))
                st.did(v.tensor_scalar(m[:], f[:], 0.5, None, ALU.is_gt))
                st.did(v.tensor_scalar(base[:], K.pcol[:], float(EC), -1.0, ALU.mult, ALU.add))
                st.step(v.tensor_scalar(spare[:], K.pcol[:], float(EP), None, ALU.add))
                st.step(v.tensor_tensor(r[:], f[:], base[:], ALU.add))
                st.step(v.tensor_tensor(r[:], r[:], spare[:], ALU.subtract))
                st.step(v.tensor_tensor(r[:], r[:], m[:], ALU.mult))
                st.step(v.tensor_tensor(r[:], r[:], spare[:], ALU.add))
                st.did(v.tensor_copy(O.mend_i[:], r[:]))
                v.tensor_copy(wide[:], lead[:, EC - 1:EC].to_broadcast([P, P])).then_inc(s_wide, 1)
                v.wait_ge(s_t, 1)
                st.step(v.tensor_copy(O.span[:], pt[:]))
                st.did(v.tensor_scalar(O.span_neg[:], O.span[:], 1.0, -NEG, ALU.subtract, ALU.mult))
                st.settle()

            @block.tensor
            def _(pe):
                pe.wait_ge(s_wide, 1)
                pe.transpose(pt[:], wide[:], K.ident[:]).then_inc(s_t, 1)


def mend_and_read(nc, K, name, O, rows, W, ends, op, out):
    pieces = [(a, min(a + 64, W)) for a in range(0, W, 64)]
    with phase(nc, name) as ph:
        full = [ph.sb(f"full{a}", [b - a, P + 1]) for a, b in pieces]
        carry, row = ph.sb("carry", [P, W]), ph.sb("row", [P, W])
        pt = ph.ps("pt", [64, P])
        pc = ph.ps("pc", [P, W])
        s_t, s_own, s_full, s_c, s_row, s_mended, s_back, s_out = (
            ph.sem(x) for x in ("t", "own", "full", "c", "row", "mended", "back", "out"))
        with nc.Block() as block:

            @block.tensor
            def _(pe):
                for n, (a, b) in enumerate(pieces):
                    if n:
                        pe.wait_ge(s_full, n)
                    pe.transpose(pt[0:b - a, :], ends[:, a:b], K.ident[:]).then_inc(s_t, 1)
                for n, (a, b) in enumerate(pieces):
                    pe.wait_ge(s_full, n + 1)
                    mm = pe.matmul(pc[:, a:b], full[n][:, 0:P], K.ident[0:b - a, 0:b - a], start=True, stop=True)
                    mm.then_inc(s_c, 1)

            @block.vector
            def _(v):
                st = Steps(v, s_own)
                for n, (a, b) in enumerate(pieces):
                    st.step(v.memset(full[n][:, 0:1], 0.0))
                    v.wait_ge(s_t, n + 1)
                    if op == ALU.add:
                        ins = v.tensor_tensor_scan(full[n][:, 1:P + 1], O.span[0:b - a, :], pt[0:b - a, :], 0.0, ALU.mult, ALU.add)
                    else:
                        ins = v.tensor_tensor_scan(full[n][:, 1:P + 1], O.span_neg[0:b - a, :], pt[0:b - a, :], NEG, ALU.add, ALU.max)
                    ins.then_inc(s_full, 1)
                v.wait_ge(s_c, len(pieces))
                st.step(v.tensor_copy(carry[:], pc[:]))
                v.wait_ge(s_row, 16)
                v.tensor_tensor(row[:], row[:], carry[:], op).then_inc(s_mended, 1)

            @block.gpsimd
            def _(g):
                g.indirect_dma_start(row[:], None, rows, bass.IndirectOffsetOnAxis(ap=O.mend_i[:], axis=0)).then_inc(s_row, 16)
                g.wait_ge(s_mended, 1)
                g.indirect_dma_start(rows, bass.IndirectOffsetOnAxis(ap=O.mend_i[:], axis=0), row[:], None).then_inc(s_back, 16)
                g.wait_ge(s_back, 16)
                for c in range(NC_):
                    g.indirect_dma_start(out[:, c, :], None, rows,
                                         bass.IndirectOffsetOnAxis(ap=O.last_i[:, c:c + 1], axis=0)).then_inc(s_out, 16)
                g.wait_ge(s_out, 16 * NC_)


def put_starts(nc, K, name, O, tile, W, fill, table, init):
    with phase(nc, name) as ph:
        s_put, s_tab, s_init = ph.sem("put"), ph.sem("tab"), ph.sem("init")
        with nc.Block() as block:

            @block.sync
            def _(sp):
                sp.dma_start(table.rearrange("(p c) w -> p (c w)", p=P), tile.rearrange("p c w -> p (c w)")).then_inc(s_tab, 16)
                sp.wait_ge(s_tab, 16)

            @block.gpsimd
            def _(g):
                for c in range(NC_):
                    g.indirect_dma_start(fill, bass.IndirectOffsetOnAxis(ap=O.fill_i[:, c:c + 1], axis=0),
                                         tile[:, c, :], None).then_inc(s_put, 16)
                g.wait_ge(s_tab, 16)
                g.indirect_dma_start(init, None, table, bass.IndirectOffsetOnAxis(ap=O.first_i[:], axis=0)).then_inc(s_init, 16)
                g.wait_ge(s_put, 16 * NC_)
                g.wait_ge(s_init, 16)


def max_scan(nc, K, name, O, vals, rows, W, ends):
    with phase(nc, name) as ph:
        neg = ph.sb("neg", [P, EC])
        m = ph.sb("m", [P, EC, W])
        s_own, s_m, s_out = ph.sem("own"), ph.sem("m"), ph.sem("out")
        with nc.Block() as block:

            @block.vector
            def _(v):
                st = Steps(v, s_own)
                st.step(v.tensor_scalar(neg[:], O.keep[:], 1.0, -NEG, ALU.subtract, ALU.mult))
                for w in range(W):
                    st.did(v.tensor_tensor_scan(m[:, :, w], neg[:], vals[:, w, :], NEG, ALU.add, ALU.max))
                st.settle()
                v.tensor_copy(ends, m[:, EC - 1, :]).then_inc(s_m, 1)
                v.wait_ge(s_m, 1)

            @block.sync
            def _(sp):
                sp.wait_ge(s_m, 1)
                sp.dma_start(rows[0:EP, :].rearrange("(p c) w -> p (c w)", p=P), m[:].rearrange("p c w -> p (c w)")).then_inc(s_out, 16)
                sp.wait_ge(s_out, 16)


def bound(nc, K, name, b, top, out, W, slope):
    with phase(nc, name) as ph:
        t = ph.sb("t", [P, NC_, W])
        s_own = ph.sem("own")
        with nc.Block() as block:

            @block.vector
            def _(v):
                st = Steps(v, s_own)
                st.did(v.tensor_copy(out[:, :, 0:W], b))
                st.step(v.tensor_tensor(t[:], top, b, ALU.add))
                st.step(v.scalar_tensor_tensor(out=out[:, :, W:2 * W], in0=t[:], scalar=slope, in1=t[:],
                                               op0=ALU.mult, op1=ALU.max))


def exponentials(nc, K, name, O, vals, fill, init, W, slope, ex):
    HC = EC // 2
    with phase(nc, name) as ph:
        f = ph.sb("f", [P, HC, 2 * W])
        last = ph.sb("last", [P, 2 * W])
        e = [ph.sb(f"e{k}", [P, HC]) for k in range(2)]
        s_in, s_own, s_e, s_ex, s_f = (ph.sem(x) for x in ("in", "own", "e", "ex", "f"))
        with nc.Block() as block:

            @block.sync
            def _(sp):
                for half in range(2):
                    if half:
                        sp.wait_ge(s_f, 1)
                    sp.dma_start(f[:].rearrange("p c w -> p (c w)"),
                                 fill[0:EP, :].rearrange("(p c) w -> p (c w)", p=P)[:, half * HC * 2 * W:(half + 1) * HC * 2 * W]).then_inc(s_in, 16)

            @block.vector
            def _(v):
                st = Steps(v, s_own)
                st.step(v.tensor_copy(last[:], init))
                for half in range(2):
                    c = slice(half * HC, (half + 1) * HC)
                    v.wait_ge(s_in, 16 * half + 16)
                    for w in range(2 * W):
                        st.did(v.tensor_tensor_scan(f[:, :, w], O.keep[:, c], f[:, :, w], last[:, w:w + 1], ALU.mult, ALU.add))
                    st.settle()
                    st.did(v.tensor_copy(last[:], f[:, HC - 1, :]))
                    for w in range(W):
                        n = half * W + w
                        if n >= 2:
                            v.wait_ge(s_ex, n - 1)
                        b = e[n % 2]
                        st.step(v.tensor_tensor(b[:], vals[:, w, c], f[:, :, w], ALU.add))
                        st.step(v.scalar_tensor_tensor(out=b[:], in0=b[:], scalar=slope, in1=b[:], op0=ALU.mult, op1=ALU.max))
                        v.tensor_tensor(b[:], b[:], f[:, :, W + w], ALU.subtract).then_inc(s_e, 1)
                    v.wait_ge(s_e, (half + 1) * W)
                    v.sem_inc(s_f, 1)
                    st.settle()

            @block.scalar
            def _(act):
                for half in range(2):
                    for w in range(W):
                        n = half * W + w
                        act.wait_ge(s_e, n + 1)
                        act.activation(ex[:, w, half * HC:(half + 1) * HC], e[n % 2][:], ACT.Exp).then_inc(s_ex, 1)
                act.wait_ge(s_ex, 2 * W)


def weighted_sums(nc, K, name, O, rows, Win, ex, W, out, CH):
    WO = W * (D + 1)
    with phase(nc, name) as ph:
        inp = [ph.sb(f"in{k}", [P, CH, Win]) for k in range(2)]
        acc = [ph.sb(f"acc{k}", [P, CH, WO]) for k in range(2)]
        state = ph.sb("state", [P, WO])
        s_in, s_used, s_terms, s_acc, s_out, s_free = (
            [ph.sem(f"{x}{k}") for k in range(2)] for x in ("in", "used", "terms", "acc", "out", "free"))
        s_own = ph.sem("own")
        pairs = EC // CH // 2
        with nc.Block() as block:

            @block.sync
            def _(sp):
                with sp.Fori(0, pairs) as i:
                    for k in range(2):
                        sp.wait_ge(s_used[k], i + 1)
                        sp.dma_start(inp[k][:].rearrange("p c w -> p (c w)"),
                                     rows.rearrange("(p c) -> p c", p=P)[:, bass.ds((i * 2 + k) * (CH * Win), CH * Win)]).then_inc(s_in[k], 16)

            @block.gpsimd
            def _(g):
                for k in range(2):
                    g.sem_inc(s_used[k], 1)
                with g.Fori(0, pairs) as i:
                    for k in range(2):
                        col = (i * 2 + k) * CH
                        g.wait_ge(s_in[k], 16 * i + 16)
                        g.wait_ge(s_free[k], i + 1)
                        for h in range(W):
                            x = ex[:, h, bass.ds(col, CH)]
                            g.tensor_tensor(acc[k][:, :, h * D:(h + 1) * D], inp[k][:, :, 0:D],
                                            x.unsqueeze(2).to_broadcast([P, CH, D]), ALU.mult).then_inc(s_terms[k], 1)
                            g.tensor_copy(acc[k][:, :, W * D + h], x).then_inc(s_terms[k], 1)
                        g.wait_ge(s_terms[k], 2 * W * i + 2 * W)
                        g.sem_inc(s_used[k], 1)

            @block.vector
            def _(v):
                st = Steps(v, s_own)
                st.step(v.memset(state[:], 0.0))
                with v.Fori(0, pairs) as i:
                    st.loop(i, 2 * (WO + 1))
                    for k in range(2):
                        for h in range(W):
                            v.wait_ge(s_terms[k], 2 * W * i + 2 * h + 2)
                            for c in [*range(h * D, h * D + D), W * D + h]:
                                st.did(v.tensor_tensor_scan(acc[k][:, :, c], O.keep[:, bass.ds((i * 2 + k) * CH, CH)], acc[k][:, :, c],
                                                            state[:, c:c + 1], ALU.mult, ALU.add))
                        st.settle()
                        st.step(v.tensor_copy(state[:], acc[k][:, CH - 1, :]))
                        v.sem_inc(s_acc[k], 1)
                    st.end_loop(pairs)
                st.step(v.tensor_copy(K.ends[:, 0:WO], state[:]))

            @block.scalar
            def _(act):
                for k in range(2):
                    act.sem_inc(s_free[k], 1)
                with act.Fori(0, pairs) as i:
                    for k in range(2):
                        act.wait_ge(s_acc[k], i + 1)
                        act.dma_start(out[0:EP, :].rearrange("(p c) w -> p (c w)", p=P)[:, bass.ds((i * 2 + k) * (CH * WO), CH * WO)],
                                      acc[k][:].rearrange("p c w -> p (c w)")).then_inc(s_out[k], 16)
                        act.wait_ge(s_out[k], 16 * i + 16)
                        act.sem_inc(s_free[k], 1)


def permute(nc, K, name, O, fill, init, W, WO, out):
    with phase(nc, name) as ph:
        inp = [ph.sb(f"in{k}", [P, SG, W]) for k in range(2)]
        buf = [ph.sb(f"buf{k}", [P, SG, WO]) for k in range(2)]
        ix = [ph.sb(f"ix{k}", [P, SG], I32) for k in range(2)]
        s_in, s_used, s_buf, s_put, s_free = ([ph.sem(f"{x}{k}") for k in range(2)] for x in ("in", "used", "buf", "put", "free"))
        s_own = ph.sem("own")
        pairs = STAGES // 2
        keyed = WO > W
        with nc.Block() as block:

            @block.sync
            def _(sp):
                with sp.Fori(0, pairs) as i:
                    for k in range(2):
                        t = i * 2 + k
                        sp.wait_ge(s_used[k], i + 1)
                        sp.wait_ge(s_free[k], i + 1)
                        sp.dma_start(inp[k][:].rearrange("p c w -> p (c w)"),
                                     fill[0:EP, :].rearrange("(p c) w -> p (c w)", p=P)[:, bass.ds(t * (SG * W), SG * W)]).then_inc(s_in[k], 16)
                        sp.dma_start(ix[k][:], K.pos_i.rearrange("(p c) -> p c", p=P)[:, bass.ds(t * SG, SG)]).then_inc(s_in[k], 16)

            @block.vector
            def _(v):
                st = Steps(v, s_own)
                for k in range(2):
                    v.sem_inc(s_used[k], 1)
                st.step(v.tensor_copy(buf[1][:, SG - 1, 0:W], init))
                with v.Fori(0, pairs) as i:
                    st.loop(i, 2 * WO)
                    for k in range(2):
                        col = (i * 2 + k) * SG
                        v.wait_ge(s_in[k], 32 * i + 32)
                        for c in range(W):
                            st.did(v.tensor_tensor_scan(buf[k][:, :, c], O.keep[:, bass.ds(col, SG)], inp[k][:, :, c],
                                                        buf[1 - k][:, SG - 1, c:c + 1], ALU.mult, ALU.add))
                        if keyed:
                            st.did(v.tensor_copy(buf[k][:, :, W], K.src_f[:, bass.ds(col, SG)]))
                        st.settle()
                        v.sem_inc(s_used[k], 1)
                        v.sem_inc(s_buf[k], 1)
                    st.end_loop(pairs)

            @block.gpsimd
            def _(g):
                with g.Fori(0, pairs) as i:
                    for k in range(2):
                        g.wait_ge(s_buf[k], i + 1)
                        g.wait_ge(s_in[k], 32 * i + 32)
                        g.nop(nofuse=True)
                        for j in range(SG):
                            g.indirect_dma_start(out, bass.IndirectOffsetOnAxis(ap=ix[k][:, j:j + 1], axis=0),
                                                 buf[k][:, j, :], None).then_inc(s_put[k], 16)

            @block.scalar
            def _(act):
                for k in range(2):
                    act.sem_inc(s_free[k], 1)
                with act.Fori(0, pairs) as i:
                    for k in range(2):
                        act.wait_ge(s_put[k], (16 * SG) * i + 16 * SG)
                        act.sem_inc(s_free[k], 1)


def store_pos(nc, K):
    with phase(nc, "pos") as ph:
        t = ph.sb("t", [P, EC], I32)
        s_t, s_out = ph.sem("t"), ph.sem("out")
        with nc.Block() as block:

            @block.vector
            def _(v):
                v.tensor_copy(t[:], K.pos[:]).then_inc(s_t, 1)

            @block.sync
            def _(sp):
                sp.wait_ge(s_t, 1)
                sp.dma_start(K.pos_i.rearrange("(p c) -> p c", p=P), t[:]).then_inc(s_out, 16)
                sp.wait_ge(s_out, 16)


def unpack(nc, K, rows, W, vals):
    CH = 196
    with phase(nc, "unpack") as ph:
        inp = [ph.sb(f"in{k}", [P, CH, W]) for k in range(2)]
        key = ph.sb("key", [P, EC])
        prev = ph.sb("prev", [P, 1])
        s_in, s_a, s_v = ([ph.sem(f"{x}{k}") for k in range(2)] for x in ("in", "a", "v"))
        s_own, s_prev, s_key = ph.sem("own"), ph.sem("prev"), ph.sem("key")
        pairs = EC // CH // 2
        with nc.Block() as block:

            @block.sync
            def _(sp):
                with sp.Fori(0, pairs) as i:
                    for k in range(2):
                        sp.wait_ge(s_a[k], i + 1)
                        sp.wait_ge(s_v[k], i + 1)
                        sp.dma_start(inp[k][:].rearrange("p c w -> p (c w)"),
                                     rows.rearrange("(p c) w -> p (c w)", p=P)[:, bass.ds((i * 2 + k) * (CH * W), CH * W)]).then_inc(s_in[k], 16)
                sp.wait_ge(s_key, 1)
                sp.dma_start(prev[1:P, :], key[0:P - 1, EC - 1:EC]).then_inc(s_prev, 16)

            @block.scalar
            def _(act):
                for k in range(2):
                    act.sem_inc(s_a[k], 1)
                with act.Fori(0, pairs) as i:
                    for k in range(2):
                        col = (i * 2 + k) * CH
                        act.wait_ge(s_in[k], 16 * i + 16)
                        for h in range(HEADS):
                            last = act.copy(vals[:, h, bass.ds(col, CH)], inp[k][:, :, D + h])
                        last.then_inc(s_a[k], 1)

            @block.vector
            def _(v):
                st = Steps(v, s_own)
                for k in range(2):
                    v.sem_inc(s_v[k], 1)
                st.step(v.memset(prev[:], -1.0))
                with v.Fori(0, pairs) as i:
                    for k in range(2):
                        v.wait_ge(s_in[k], 16 * i + 16)
                        v.tensor_copy(key[:, bass.ds((i * 2 + k) * CH, CH)], inp[k][:, :, W - 1]).then_inc(s_v[k], 1)
                v.wait_ge(s_v[1], pairs + 1)
                v.wait_ge(s_v[0], pairs + 1)
                v.sem_inc(s_key, 1)
                st.did(v.tensor_copy(K.o_s.first_i[:], key[:, 0:1]))
                st.did(v.tensor_tensor(K.keep_s[:, 1:EC], key[:, 1:EC], key[:, 0:EC - 1], ALU.is_equal))
                v.wait_ge(s_prev, 16)
                st.did(v.tensor_tensor(K.keep_s[:, 0:1], key[:, 0:1], prev[:], ALU.is_equal))
                st.settle()



MUL, MOUT, KH = 16, 8, 16
KD = 10
FW = 96
NOUT = 48
WA = NOUT * KD
WB = NOUT * KH
BANK = 512
AHEAD = 4
TANH_GAIN = 1.593
INV_SQRT3 = 0.5773502691896258
PW_S, PW_V = 0.17677669529663687, 0.25


def edge_weights(nc, K, wall):
    c0 = math.sqrt(2.0) / math.sqrt(10.0) / 4.0
    r32 = math.sqrt(1.5)
    with phase(nc, "wall") as ph:
        a = ph.sb("a", [32, 3, KH, MOUT])
        b = ph.sb("b", [48, 2, KH, MOUT])
        ao = ph.sb("ao", [32, 3, MOUT, KH])
        bo = ph.sb("bo", [48, MOUT, KH])
        cc = ph.sb("cc", [32, 1])
        s_z, s_in, s_own, s_done, s_out = (ph.sem(x) for x in ("z", "in", "own", "done", "out"))
        W2 = K.in_W2.rearrange("k (i u w) -> i u k w", i=7, u=MUL)
        with nc.Block() as block:

            @block.sync
            def _(sp):
                for r, parts in enumerate(((0, 2, 4), (1, 3, 6))):
                    for n, i in enumerate(parts):
                        sp.dma_start(a[16 * r:16 * r + 16, n, :, :], W2[i]).then_inc(s_in, 16)
                for r in range(3):
                    for n, i in enumerate((5, 6)):
                        sp.dma_start(b[16 * r:16 * r + 16, n, :, :], W2[i]).then_inc(s_in, 16)
                sp.wait_ge(s_z, 1)
                sp.wait_ge(s_done, 1)
                for k0, k1, c in ((0, KD, 0), (KD, KH, WA)):
                    out = wall[:, c:c + NOUT * (k1 - k0)].rearrange("p (o k) -> p o k", k=k1 - k0)
                    sp.dma_start(out[0:32, 0:24, :], ao[:, :, :, k0:k1].rearrange("p n w k -> p (n w) k")).then_inc(s_out, 16)
                    v = out[:, 24:48, :].rearrange("p (w i) k -> p w i k", i=3)
                    for i in range(3):
                        sp.dma_start(v[32 + 16 * i:48 + 16 * i, :, i, :], bo[16 * i:16 * i + 16, :, k0:k1]).then_inc(s_out, 16)
                sp.dma_start(wall[80:90, WB:], K.in_W1).then_inc(s_out, 16)
                sp.wait_ge(s_out, 16 * 9)

            @block.vector
            def _(v):
                st = Steps(v, s_own)
                v.memset(wall[:], 0.0).then_inc(s_z, 1)
                st.step(v.memset(cc[:], r32 * PW_V * c0))
                st.step(v.memset(cc[0:16, :], PW_V * c0))
                v.wait_ge(s_in, 16 * 12)
                st.did(v.tensor_scalar(ao[:, 0:2, :, :], a[:, 0:2, :, :].rearrange("p n k w -> p n w k"), PW_S * c0, None, ALU.mult))
                st.did(v.tensor_scalar(ao[:, 2, :, :], a[:, 2, :, :].rearrange("p k w -> p w k"), cc[:, 0:1], None, ALU.mult))
                st.did(v.tensor_scalar(b[:, 0, :, :], b[:, 0, :, :], INV_SQRT3 * PW_V * c0, None, ALU.mult))
                st.step(v.tensor_scalar(b[:, 1, :, :], b[:, 1, :, :], r32 / 3 * PW_V * c0, None, ALU.mult))
                st.step(v.tensor_tensor(bo[:], b[:, 0, :, :].rearrange("p k w -> p w k"), b[:, 1, :, :].rearrange("p k w -> p w k"), ALU.subtract))
                v.sem_inc(s_done, 1)


def unit_vectors(nc, K, n, gain):
    with phase(nc, "unit") as ph:
        sq = ph.sb("sq", [P, EC, 3])
        ln, zero = ph.sb("ln", [P, EC]), ph.sb("zero", [P, 1])
        s_in, s_own, s_a, s_b = (ph.sem(x) for x in ("in", "own", "a", "b"))
        with nc.Block() as block:

            @block.sync
            def _(sp):
                sp.dma_start(n.rearrange("p c w -> p (c w)"), K.vec.rearrange("(p c) -> p c", p=P)).then_inc(s_in, 16)
                sp.dma_start(gain, K.nrm.rearrange("(p c) -> p c", p=P)).then_inc(s_in, 16)

            @block.vector
            def _(v):
                st = Steps(v, s_own)
                st.did(v.memset(zero[:], 0.0))
                v.wait_ge(s_in, 32)
                st.step(v.tensor_tensor(sq[:], n, n, ALU.mult))
                st.step(v.tensor_reduce(ln[:], sq[:], AX.X, ALU.add))
                v.sem_inc(s_a, 1)
                st.did(v.tensor_scalar(gain, gain, TANH_GAIN, None, ALU.mult))
                v.wait_ge(s_b, 1)
                st.step(v.reciprocal(ln[:], ln[:]))
                st.step(v.tensor_tensor(n, n, ln[:].unsqueeze(2).to_broadcast([P, EC, 3]), ALU.mult))

            @block.scalar
            def _(act):
                act.wait_ge(s_a, 1)
                act.activation(ln[:], ln[:], ACT.Sqrt, bias=zero[:, 0:1]).then_inc(s_b, 1)


def edge_network(nc, K, O, table, fill, init, wall, n, gain, out):
    with phase(nc, "net") as ph:
        G = Gather(nc, K, ph, table, D, K.src)
        hd = [ph.sb(f"hd{k}", [P, SG, D]) for k in range(2)]
        F = [ph.sb(f"F{k}", [P, SG, FW]) for k in range(2)]
        t3 = ph.sb("t3", [P, SG, 16, 3])
        fT = [ph.sb(f"fT{k}", [FW, P]) for k in range(2)]
        hk = [ph.sb(f"hk{k}", [P, KH]) for k in range(AHEAD)]
        pr = [ph.sb(f"pr{k}", [P, 2, NOUT, KH]) for k in range(2)]
        o = [ph.sb(f"o{k}", [P, SG, NOUT]) for k in range(2)]
        u3 = ph.sb("u3", [P, SG, MOUT, 3])
        res = [ph.sb(f"res{k}", [P, SG, D]) for k in range(2)]
        last = ph.sb("last", [P, D])
        pA = [ph.ps(f"pA{k}", [P, BANK]) for k in range(AHEAD)]
        pB = [ph.ps(f"pB{k}", [P, BANK]) for k in range(AHEAD)]
        pf = [b[0:FW, BANK - P:BANK] for b in pB]
        names = ("in", "xs", "cp", "emb", "F", "Fused", "res", "out", "free")
        s_in, s_xs, s_cp, s_emb, s_F, s_Fu, s_res, s_out, s_free = ([ph.sem(f"{x}{k}") for k in range(2)] for x in names)
        (s_own, s_tr, s_fT, s_P, s_B, s_h, s_pr, s_pa, s_red, s_tanh_in, s_tanh, s_z) = (
            ph.sem(x) for x in ("own", "tr", "fT", "P", "B", "h", "pr", "pa", "red", "tanh_in", "tanh", "z"))
        pairs = STAGES // 2
        per = 2 * SG
        PAIRS = SG // 2
        assert SG % AHEAD == 0 and WB - WA + KH <= BANK - P

        def following(i, k):
            return (i, 1) if k == 0 else (i + 1, 0)

        def prior(i, k):
            return (i, 0) if k == 1 else (i - 1, 1)

        with nc.Block() as block:

            @block.gpsimd
            def _(g):
                G.gpsimd(g)

            @block.sync
            def _(sp):
                def load_rows(i, k):
                    t = i * 2 + k
                    sp.wait_ge(s_cp[k], i + 1)
                    sp.dma_start(hd[k][:].rearrange("p c w -> p (c w)"),
                                 fill[0:EP, :].rearrange("(p c) w -> p (c w)", p=P)[:, bass.ds(t * (SG * D), SG * D)]).then_inc(s_in[k], 16)
                    G.load_index(sp, k, t)
                    sp.sem_inc(G.s_free[k], 1)

                def load_emb(i, k):
                    sp.wait_ge(s_Fu[k], i + 1)
                    sp.dma_start(F[k][:, :, 80:90],
                                 K.emb.rearrange("(p c w) -> p c w", p=P, w=10)[:, bass.ds((i * 2 + k) * SG, SG), :]).then_inc(s_emb[k], 16)

                def store(i, k):
                    sp.wait_ge(s_res[k], i + 1)
                    sp.dma_start(out[0:EP, :].rearrange("(p c) w -> p (c w)", p=P)[:, bass.ds((i * 2 + k) * (SG * D), SG * D)],
                                 res[k][:].rearrange("p c w -> p (c w)")).then_inc(s_out[k], 16)
                    sp.wait_ge(s_out[k], 16 * i + 16)
                    sp.sem_inc(s_free[k], 1)

                def turn(i, first=False, left=3):
                    if left > 1:
                        load_rows(i + 1, 1)
                    if not first:
                        store(i - 1, 1)
                    if left > 1:
                        load_emb(i + 1, 0)
                    if left > 2:
                        load_rows(i + 2, 0)
                    store(i, 0)
                    if left > 1:
                        load_emb(i + 1, 1)

                sp.wait_ge(s_z, 1)
                for k in range(2):
                    load_rows(0, k)
                    load_emb(0, k)
                load_rows(1, 0)
                turn(0, first=True)
                with sp.Fori(0, pairs - 3) as i:
                    turn(i + 1)
                turn(pairs - 2, left=2)
                turn(pairs - 1, left=1)
                store(pairs - 1, 1)

            @block.vector
            def _(v):
                st = Steps(v, s_own)
                for k in range(2):
                    st.did(v.memset(F[k][:], 0.0))
                st.step(v.tensor_copy(last[:], init))
                v.sem_inc(s_z, 1)
                st.step(v.memset(res[1][:, SG - 1, :], 0.0))

                def hold(i, k, c0, c1):
                    if c0 == 0:
                        v.wait_ge(s_in[k], 16 * i + 16)
                    for c in range(c0, min(c1, D)):
                        st.did(v.tensor_tensor_scan(hd[k][:, :, c], O.keep[:, bass.ds((i * 2 + k) * SG, SG)], hd[k][:, :, c],
                                                    last[:, c:c + 1], ALU.mult, ALU.add))

                def held(i, k):
                    st.settle()
                    st.step(v.tensor_copy(last[:], hd[k][:, SG - 1, :]))
                    v.sem_inc(s_xs[k], 1)

                def dots(i, k, part):
                    if part == 0:
                        v.wait_ge(s_cp[k], i + 2)
                        nn = n[:, bass.ds((i * 2 + k) * SG, SG), :].unsqueeze(2).to_broadcast([P, SG, 16, 3])
                        st.did(v.tensor_tensor(t3[:], F[k][:, :, 32:80].rearrange("p c (i u) -> p c u i", i=3), nn, ALU.mult))
                    else:
                        st.settle()
                        st.step(v.tensor_reduce(F[k][:, :, 16:32], t3[:], AX.X, ALU.add))
                        v.sem_inc(s_F[k], 1)

                def products(i, k, m):
                    v.wait_ge(s_red, i * SG + k * PAIRS + m + 1)
                    for c in range(2):
                        a = (2 * m + c) % AHEAD
                        v.wait_ge(s_h, i * per + k * SG + 2 * m + c + 1)
                        v.wait_ge(s_P, i * per + k * SG + 2 * m + c + 1)
                        v.tensor_tensor(pr[m % 2][:, c, :, 0:KD], pA[a][:, 0:WA].rearrange("p (o k) -> p o k", k=KD),
                                        hk[a][:, 0:KD].unsqueeze(1).to_broadcast([P, NOUT, KD]), ALU.mult).then_inc(s_pr, 1)

                def sums(i, k, m):
                    v.wait_ge(s_pr, i * per + k * SG + 2 * m + 2 + AHEAD)
                    v.wait_ge(s_pa, i * per + k * SG + 2 * m + 2 + AHEAD)
                    v.tensor_reduce(o[k][:, 2 * m:2 * m + 2, :], pr[m % 2][:], AX.X, ALU.add).then_inc(s_red, 1)

                def summed(i, k):
                    v.wait_ge(s_red, i * SG + (k + 1) * PAIRS + 2)
                    v.sem_inc(s_tanh_in, 1)

                def outputs(i, k, part):
                    t = i * 2 + k
                    ok = o[k]
                    nn = n[:, bass.ds(t * SG, SG), :].unsqueeze(2).to_broadcast([P, SG, MOUT, 3])
                    gg = gain[:, bass.ds(t * SG, SG)].unsqueeze(2).to_broadcast([P, SG, 8])
                    cw = ok[:, :, 16:24].unsqueeze(3).to_broadcast([P, SG, MOUT, 3])
                    gt = ok[:, :, 8:16].unsqueeze(3).to_broadcast([P, SG, MOUT, 3])
                    vv = ok[:, :, 24:48].rearrange("p c (w i) -> p c w i", i=3)
                    if part == 0:
                        st.did(v.tensor_tensor(u3[:], cw, nn, ALU.mult))
                    elif part == 1:
                        st.settle()
                        st.did(v.tensor_tensor(vv, vv, u3[:], ALU.add))
                    elif part == 2:
                        v.wait_ge(s_tanh, t + 1)
                        v.wait_ge(s_free[k], i + 1)
                        st.did(v.tensor_tensor(res[k][:, :, 0:8], ok[:, :, 0:8], gg, ALU.mult))
                        st.did(v.tensor_tensor(ok[:, :, 8:16], ok[:, :, 8:16], gg, ALU.mult))
                    else:
                        st.settle()
                        st.did(v.tensor_tensor(res[k][:, :, 8:32].rearrange("p c (w i) -> p c w i", i=3), vv, gt, ALU.mult))

                def run_sums(i, k, c0, c1):
                    if c0 == 0:
                        st.settle()
                    for c in range(c0, min(c1, D)):
                        st.did(v.tensor_tensor_scan(res[k][:, :, c], O.keep[:, bass.ds((i * 2 + k) * SG, SG)], res[k][:, :, c],
                                                    res[1 - k][:, SG - 1, c:c + 1], ALU.mult, ALU.add))

                def run_summed(i, k):
                    st.settle()
                    v.sem_inc(s_res[k], 1)

                def turn(i, k, less, more):
                    was, to = prior(i, k), following(i, k)
                    for m in range(PAIRS):
                        products(i, k, m)
                        if m >= 1:
                            sums(i, k, m - 1)
                        elif less:
                            sums(*was, PAIRS - 1)
                        if more:
                            if m < 5:
                                hold(*to, 7 * m, 7 * m + 7)
                            elif m == 5:
                                held(*to)
                            elif m in (10, 11):
                                dots(*to, m - 10)
                        if less:
                            if m == 1:
                                summed(*was)
                            if 1 <= m <= 4:
                                outputs(*was, m - 1)
                            elif 6 <= m <= 10:
                                run_sums(*was, 7 * (m - 6), 7 * (m - 5))
                            elif m == 11:
                                run_summed(*was)

                hold(0, 0, 0, D)
                held(0, 0)
                dots(0, 0, 0)
                dots(0, 0, 1)
                turn(0, 0, False, True)
                turn(0, 1, True, True)
                with v.Fori(0, pairs - 2) as i:
                    st.loop(i, 2 * (D + 1 + 2 + 5 + D))
                    turn(i + 1, 0, True, True)
                    turn(i + 1, 1, True, True)
                st.end_loop(pairs - 2)
                turn(pairs - 1, 0, True, True)
                turn(pairs - 1, 1, True, False)
                sums(pairs - 1, 1, PAIRS - 1)
                summed(pairs - 1, 1)
                for part in range(4):
                    outputs(pairs - 1, 1, part)
                run_sums(pairs - 1, 1, 0, D)
                run_summed(pairs - 1, 1)
                st.step(v.tensor_copy(K.ends[:, 0:D], res[1][:, SG - 1, :]))

            @block.tensor
            def _(pe):
                pe.sem_inc(s_Fu[0], 1)
                pe.sem_inc(s_Fu[1], 1)
                pe.sem_inc(s_pr, AHEAD)
                pe.sem_inc(s_pa, AHEAD)

                def transpose(i, k, j):
                    if j == 0:
                        pe.wait_ge(s_F[k], i + 1)
                        pe.wait_ge(s_emb[k], 16 * i + 16)
                    pe.wait_ge(s_pa, i * per + k * SG + j + 1)
                    pe.transpose(pf[j % AHEAD], F[k][:, j, :], K.ident[:]).then_inc(s_tr, 1)

                def turn(i, k, more):
                    for j in range(SG):
                        a, q = j % AHEAD, i * per + k * SG + j
                        if j + 1 < SG:
                            transpose(i, k, j + 1)
                        elif more:
                            transpose(*following(i, k), 0)
                        pe.wait_ge(s_fT, q + 3)
                        pe.matmul(pB[a][:, 0:WB - WA + KH], fT[j % 2][:], wall[:, WA:], start=True, stop=True).then_inc(s_B, 1)
                        pe.wait_ge(s_pr, q + 1)
                        pe.matmul(pA[a][:, 0:WA], fT[j % 2][:], wall[:, 0:WA], start=True, stop=True).then_inc(s_P, 1)
                        if j == SG - 2:
                            pe.wait_ge(s_tr, q + 2)
                            pe.sem_inc(s_Fu[k], 1)

                transpose(0, 0, 0)
                with pe.Fori(0, pairs - 1) as i:
                    turn(i, 0, True)
                    turn(i, 1, True)
                turn(pairs - 1, 0, True)
                turn(pairs - 1, 1, False)

            @block.scalar
            def _(act):
                act.sem_inc(s_fT, 2)
                act.sem_inc(s_red, 2)
                for k in range(2):
                    act.sem_inc(s_free[k], 1)
                    act.sem_inc(s_cp[k], 1)

                def place(i, k, part):
                    e, c = part // 4, part % 4
                    x = (G.st[k], hd[k])[e]
                    if part == 0:
                        act.wait_ge(G.s_rows[k], (16 * SG) * i + 16 * SG)
                        act.wait_ge(s_emb[k], 16 * i + 16)
                    if part == 4:
                        act.wait_ge(s_xs[k], i + 1)
                    if c == 0:
                        act.copy(F[k][:, :, 8 * e:8 * e + 8], x[:, :, 0:8])
                    else:
                        ins = act.copy(F[k][:, :, 16 + 16 * c + 8 * e:24 + 16 * c + 8 * e],
                                       x[:, :, 8:32].rearrange("p c (u i) -> p c u i", i=3)[:, :, :, c - 1])
                        if part == 7:
                            ins.then_inc(s_cp[k], 1)

                def copy_features(q, j):
                    act.wait_ge(s_tr, q + 1)
                    act.copy(fT[j % 2][:], pf[j % AHEAD]).then_inc(s_fT, 1)

                def squash(i, k):
                    act.wait_ge(s_tanh_in, i * 2 + k + 1)
                    act.activation(o[k][:, :, 0:16], o[k][:, :, 0:16], ACT.Tanh).then_inc(s_tanh, 1)

                def turn(i, k, less, more):
                    for j in range(SG):
                        a, c, b = j % AHEAD, j % 2, j // 2 % 2
                        q = i * per + k * SG + j
                        if j + 1 < SG or more:
                            copy_features(q + 1, j + 1)
                        act.wait_ge(s_B, q + 1)
                        act.wait_ge(s_pr, q + 1)
                        act.activation(hk[a][:], pB[a][:, WB - WA:WB - WA + KH], ACT.Relu).then_inc(s_h, 1)
                        act.wait_ge(s_h, q + 1)
                        act.wait_ge(s_red, i * SG + k * PAIRS + j // 2 + 1)
                        for u in range(KD, KH):
                            ins = act.activation(pr[b][:, c, :, u], pB[a][:, 0:WB - WA].rearrange("p (o k) -> p o k", k=KH - KD)[:, :, u - KD],
                                                 ACT.Copy, scale=hk[a][:, u:u + 1])
                        ins.then_inc(s_pa, 1)
                        if more and 11 <= j < 19:
                            place(*following(i, k), j - 11)
                        if less and j == 4:
                            squash(*prior(i, k))

                for part in range(8):
                    place(0, 0, part)
                copy_features(0, 0)
                turn(0, 0, False, True)
                turn(0, 1, True, True)
                with act.Fori(0, pairs - 2) as i:
                    turn(i + 1, 0, True, True)
                    turn(i + 1, 1, True, True)
                turn(pairs - 1, 0, True, True)
                turn(pairs - 1, 1, True, False)
                squash(pairs - 1, 1)



BN_EPS = 1e-5
CB = 112


def first_sums(nc, K, O, fill, init, rows, out, stats):
    CH = CB
    with phase(nc, "z") as ph:
        a = [ph.sb(f"a{k}", [P, CH, D]) for k in range(2)]
        b = [ph.sb(f"b{k}", [P, CH, D]) for k in range(2)]
        sq = ph.sb("sq", [P, CH, D])
        last = ph.sb("last", [P, D])
        one = ph.sb("one", [P, 1])
        zz = ph.sb("zz", [P, 448])
        p1, p2 = ph.ps("p1", [1, 448]), ph.ps("p2", [1, 448])
        s_in_a, s_in_b, s_z, s_out, s_free, s_added = (
            [ph.sem(f"{x}{k}") for k in range(2)] for x in ("in_a", "in_b", "z", "out", "free", "added"))
        s_own, s_sq, s_pe, s_one, s_fin = (ph.sem(x) for x in ("own", "sq", "pe", "one", "fin"))
        pairs = EC // CH // 2
        with nc.Block() as block:

            @block.sync
            def _(sp):
                with sp.Fori(0, pairs) as i:
                    for k in range(2):
                        t = i * 2 + k
                        for x, src, s_freed, s_in in ((a, fill[0:EP, :], s_added, s_in_a), (b, rows, s_free, s_in_b)):
                            sp.wait_ge(s_freed[k], i + 1)
                            sp.dma_start(x[k][:].rearrange("p c w -> p (c w)"),
                                         src.rearrange("(p c) w -> p (c w)", p=P)[:, bass.ds(t * (CH * D), CH * D)]).then_inc(s_in[k], 16)

            @block.vector
            def _(v):
                st = Steps(v, s_own)
                st.did(v.memset(one[:], 1.0))
                st.did(v.memset(zz[:], 0.0))
                st.step(v.tensor_copy(last[:], init))
                v.sem_inc(s_one, 1)
                for k in range(2):
                    v.sem_inc(s_added[k], 1)
                with v.Fori(0, pairs) as i:
                    st.loop(i, 2 * (D + 2))
                    for k in range(2):
                        col = (i * 2 + k) * CH
                        v.wait_ge(s_in_a[k], 16 * i + 16)
                        for c in range(D):
                            st.did(v.tensor_tensor_scan(a[k][:, :, c], O.keep[:, bass.ds(col, CH)], a[k][:, :, c],
                                                        last[:, c:c + 1], ALU.mult, ALU.add))
                        st.settle()
                        v.wait_ge(s_in_b[k], 16 * i + 16)
                        st.did(v.tensor_copy(last[:], a[k][:, CH - 1, :]))
                        st.step(v.tensor_tensor(b[k][:], a[k][:], b[k][:], ALU.add))
                        v.sem_inc(s_z[k], 1)
                        v.sem_inc(s_added[k], 1)
                    st.end_loop(pairs)
                v.wait_ge(s_fin, 1)
                st.did(v.tensor_copy(stats[:, 0, :], p1[:]))
                st.did(v.tensor_copy(stats[:, 1, :], p2[:]))
                st.settle()

            @block.scalar
            def _(act):
                for k in range(2):
                    act.sem_inc(s_free[k], 1)
                act.sem_inc(s_pe, 1)
                with act.Fori(0, pairs) as i:
                    for k in range(2):
                        t = i * 2 + k
                        act.wait_ge(s_z[k], i + 1)
                        act.dma_start(out.rearrange("(p c) w -> p (c w)", p=P)[:, bass.ds(t * (CH * D), CH * D)],
                                      b[k][:].rearrange("p c w -> p (c w)")).then_inc(s_out[k], 16)
                        act.wait_ge(s_pe, t + 1)
                        act.activation(sq[:], b[k][:], ACT.Square).then_inc(s_sq, 1)
                        act.wait_ge(s_pe, t + 2)
                        act.wait_ge(s_out[k], 16 * i + 16)
                        act.sem_inc(s_free[k], 1)

            @block.tensor
            def _(pe):
                pe.wait_ge(s_one, 1)
                pe.matmul(p1[:], one[:], zz[:], start=True, stop=False, skip_group_check=True)
                pe.matmul(p2[:], one[:], zz[:], start=True, stop=False, skip_group_check=True)
                with pe.Fori(0, pairs) as i:
                    for k in range(2):
                        t = i * 2 + k
                        pe.wait_ge(s_z[k], i + 1)
                        bf, sf = b[k][:].rearrange("p c w -> p (c w)"), sq[:].rearrange("p c w -> p (c w)")
                        for m in range(CH * D // 448):
                            pe.matmul(p1[:], one[:], bf[:, 448 * m:448 * m + 448], start=False, stop=False, skip_group_check=True)
                        pe.wait_ge(s_sq, t + 1)
                        for m in range(CH * D // 448):
                            mm = pe.matmul(p2[:], one[:], sf[:, 448 * m:448 * m + 448], start=False, stop=False, skip_group_check=True)
                        mm.then_inc(s_pe, 1)
                pe.matmul(p1[:], one[:], zz[:], start=False, stop=True, skip_group_check=True)
                pe.matmul(p2[:], one[:], zz[:], start=False, stop=True, skip_group_check=True).then_inc(s_fin, 1)


def bn_coefficients(v, st, s_a, s_b, total, total_sq, pad, gamma, beta, scale, shift, t, eps):
    st.step(v.tensor_tensor(t, pad, pad, ALU.mult))
    st.step(v.scalar_tensor_tensor(out=total, in0=pad, scalar=-float(NPAD), in1=total, op0=ALU.mult, op1=ALU.add))
    st.step(v.scalar_tensor_tensor(out=total_sq, in0=t, scalar=-float(NPAD), in1=total_sq, op0=ALU.mult, op1=ALU.add))
    st.did(v.tensor_scalar(total, total, 1.0 / E, None, ALU.mult))
    st.step(v.tensor_scalar(total_sq, total_sq, 1.0 / E, None, ALU.mult))
    st.step(v.tensor_tensor(t, total, total, ALU.mult))
    st.step(v.tensor_tensor(t, total_sq, t, ALU.subtract))
    st.step(v.tensor_scalar(t, t, 0.0, None, ALU.max))
    v.sem_inc(s_a, 1)
    v.wait_ge(s_b, 1)
    st.step(v.reciprocal(t, t))
    st.step(v.tensor_tensor(scale, t, gamma, ALU.mult))
    st.step(v.tensor_tensor(t, total, scale, ALU.mult))
    st.step(v.tensor_tensor(shift, beta, t, ALU.subtract))


def norm1(nc, K, stats, z, coef):
    with phase(nc, "bn1") as ph:
        r = ph.sb("r", [1, 8, D])
        eps = ph.sb("eps", [1, 1])
        row = ph.sb("row", [1, 2, 4, D])
        pt = ph.ps("pt", [P, 2])
        s_in, s_own, s_a, s_b, s_row, s_t = (ph.sem(x) for x in ("in", "own", "a", "b", "row", "t"))
        with nc.Block() as block:

            @block.sync
            def _(sp):
                for n, x in enumerate((K.in_g1, K.in_be1)):
                    sp.dma_start(r[:, n, :], x.unsqueeze(0)).then_inc(s_in, 16)
                sp.dma_start(r[:, 2, :], z[EP - 1:EP, :]).then_inc(s_in, 16)

            @block.vector
            def _(v):
                st = Steps(v, s_own)
                st.step(v.memset(eps[:], BN_EPS))
                for n in range(2):
                    st.step(v.tensor_reduce(r[:, 3 + n, :], stats[:, n, :].rearrange("p (j d) -> p d j", d=D), AX.X, ALU.add))
                v.wait_ge(s_in, 48)
                bn_coefficients(v, st, s_a, s_b, r[:, 3, :], r[:, 4, :], r[:, 2, :], r[:, 0, :], r[:, 1, :], r[:, 5, :], r[:, 6, :], r[:, 7, :], eps)
                for n in range(2):
                    st.step(v.tensor_copy(row[:, n, :, :], r[:, 5 + n, :].unsqueeze(1).to_broadcast([1, 4, D])))
                v.sem_inc(s_row, 1)
                v.wait_ge(s_t, 1)
                st.step(v.tensor_copy(coef, pt[:]))

            @block.scalar
            def _(act):
                act.wait_ge(s_a, 1)
                act.activation(r[:, 7, :], r[:, 7, :], ACT.Sqrt, bias=eps[:, 0:1]).then_inc(s_b, 1)

            @block.tensor
            def _(pe):
                pe.wait_ge(s_row, 1)
                for n in range(2):
                    mm = pe.matmul(pt[:, n:n + 1], row[:, n, :, :].rearrange("p c d -> p (c d)"), K.ident[0:1, 0:1], start=True, stop=True)
                mm.then_inc(s_t, 1)


def second_product(nc, K, z, coef, out, sums):
    G7, NCH = CB // 16, EC // CB
    with phase(nc, "y") as ph:
        zi = [ph.sb(f"zi{k}", [P, CB, D]) for k in range(2)]
        rT = [ph.sb(f"rT{k}", [P, 512]) for k in range(2)]
        yT = [ph.sb(f"yT{k}", [P, 28 * P]) for k in range(2)]
        junk = [ph.sb(f"junk{k}", [P, 512]) for k in range(2)]
        m2 = ph.sb("m2", [P, P])
        b2 = ph.sb("b2", [P, 1])
        part = ph.sb("part", [P, 2, 2 * G7])
        pt = [ph.ps(f"pt{k}", [P, 512]) for k in range(2)]
        py = [ph.ps(f"py{k}", [P, 512]) for k in range(2)]
        s_in, s_used, s_y, s_out, s_free = ([ph.sem(f"{x}{k}") for k in range(2)] for x in ("in", "used", "y", "out", "free"))
        s_z, s_w, s_t, s_r, s_p, s_e, s_q, s_own, s_sum = (ph.sem(x) for x in ("z", "w", "t", "r", "p", "e", "q", "own", "sum"))
        pairs = NCH // 2
        with nc.Block() as block:

            @block.sync
            def _(sp):
                sp.wait_ge(s_z, 1)
                for c in range(4):
                    sp.dma_start(m2[c * D:(c + 1) * D, c * D:(c + 1) * D], K.in_M2).then_inc(s_w, 16)
                    sp.dma_start(b2[c * D:(c + 1) * D, :], K.in_b2.unsqueeze(1)).then_inc(s_w, 16)
                with sp.Fori(0, pairs) as i:
                    for k in range(2):
                        t = i * 2 + k
                        sp.wait_ge(s_used[k], i + 1)
                        sp.dma_start(zi[k][:].rearrange("p c w -> p (c w)"),
                                     z.rearrange("(p c) w -> p (c w)", p=P)[:, bass.ds(t * (CB * D), CB * D)]).then_inc(s_in[k], 16)

            @block.tensor
            def _(pe):
                pe.wait_ge(s_w, 128)
                for k in range(2):
                    pe.sem_inc(s_used[k], 1)
                with pe.Fori(0, pairs) as i:
                    for k in range(2):
                        zf = zi[k][:].rearrange("p c w -> p (c w)")
                        pe.wait_ge(s_in[k], 16 * i + 16)
                        for g in range(G7 + 1):
                            if g < G7:
                                n = i * (2 * G7) + k * G7 + g
                                b = (k * G7 + g) % 2
                                pe.wait_ge(s_r, n + 1)
                                for m in range(4):
                                    mm = pe.transpose(pt[b][:, m * P:(m + 1) * P], zf[:, (4 * g + m) * P:(4 * g + m + 1) * P], K.ident[:])
                                mm.then_inc(s_t, 1)
                            if g >= 1:
                                n = i * (2 * G7) + k * G7 + g - 1
                                b = (k * G7 + g - 1) % 2
                                pe.wait_ge(s_r, n + 3)
                                pe.wait_ge(s_e, n + 1)
                                pe.matmul(py[b][:], m2[:], rT[b][:], start=True, stop=True).then_inc(s_p, 1)
                        pe.sem_inc(s_used[k], 1)

            @block.scalar
            def _(act):
                act.sem_inc(s_r, 2)
                with act.Fori(0, pairs) as i:
                    for k in range(2):
                        for g in range(G7 + 1):
                            if g < G7:
                                b = (k * G7 + g) % 2
                                act.wait_ge(s_t, i * (2 * G7) + k * G7 + g + 1)
                                act.activation(rT[b][:], pt[b][:], ACT.Relu, bias=coef[:, 1:2], scale=coef[:, 0:1]).then_inc(s_r, 1)
                            if g >= 1:
                                n = i * (2 * G7) + k * G7 + g - 1
                                act.wait_ge(s_q, n + 1)
                                act.wait_ge(s_e, n + 3)
                                act.activation(junk[(k * G7 + g - 1) % 2][:], yT[k][:, (g - 1) * 512:g * 512], ACT.Square,
                                               accum_out=part[:, 1, k * G7 + g - 1:k * G7 + g]).then_inc(s_q, 1)
                        act.wait_ge(s_q, i * (2 * G7) + (k + 1) * G7 + 2)
                        act.sem_inc(s_y[k], 1)

            @block.vector
            def _(v):
                st = Steps(v, s_own)
                v.memset(m2[:], 0.0).then_inc(s_z, 1)
                v.sem_inc(s_e, 2)
                v.sem_inc(s_q, 2)
                v.wait_ge(s_w, 128)
                with v.Fori(0, pairs) as i:
                    st.loop(i, 2 + 2)
                    for k in range(2):
                        v.wait_ge(s_free[k], i + 1)
                        for g in range(G7):
                            n = i * (2 * G7) + k * G7 + g
                            b = (k * G7 + g) % 2
                            v.wait_ge(s_p, n + 1)
                            v.tensor_scalar(yT[k][:, g * 512:(g + 1) * 512], py[b][:], b2[:, 0:1], None, ALU.add).then_inc(s_e, 1)
                        v.wait_ge(s_e, i * (2 * G7) + (k + 1) * G7 + 2)
                        st.step(v.tensor_reduce(sums[:, 0, bass.ds((i * 2 + k) * G7, 1)], yT[k][:], AX.X, ALU.add))
                        v.wait_ge(s_q, i * (2 * G7) + (k + 1) * G7 + 2)
                        st.step(v.tensor_reduce(sums[:, 1, bass.ds((i * 2 + k) * G7, 1)], part[:, 1, k * G7:(k + 1) * G7], AX.X, ALU.add))
                        v.sem_inc(s_y[k], 1)
                    st.end_loop(pairs)

            @block.gpsimd
            def _(g_):
                for k in range(2):
                    g_.sem_inc(s_free[k], 1)
                with g_.Fori(0, pairs) as i:
                    for k in range(2):
                        t = i * 2 + k
                        g_.wait_ge(s_y[k], 2 * i + 2)
                        g_.nop(nofuse=True)
                        g_.dma_start(out[bass.ds(t * P, P), :], yT[k][:]).then_inc(s_out[k], 16)
                        g_.wait_ge(s_out[k], 16 * i + 16)
                        g_.sem_inc(s_free[k], 1)


def norm2(nc, K, sums, yT, coef):
    NCH, G7 = EC // CB, CB // 16
    with phase(nc, "bn2") as ph:
        c = ph.sb("c", [P, 10])
        eps = ph.sb("eps", [P, 1])
        gath = ph.sb("gath", [P, P])
        row, col = ph.sb("row", [P, 2]), ph.sb("col", [P, 2])
        ps = ph.ps("ps", [P, 2])
        s_in, s_own, s_a, s_b, s_g, s_t = (ph.sem(x) for x in ("in", "own", "a", "b", "g", "t"))
        with nc.Block() as block:

            @block.sync
            def _(sp):
                for q in range(4):
                    sp.dma_start(c[q * D:(q + 1) * D, 0:1], K.in_g2.unsqueeze(1)).then_inc(s_in, 16)
                    sp.dma_start(c[q * D:(q + 1) * D, 1:2], K.in_be2.unsqueeze(1)).then_inc(s_in, 16)
                    sp.dma_start(c[q * D:(q + 1) * D, 2:3],
                                 yT[(NCH - 1) * P + 96:(NCH - 1) * P + P, 28 * P - 1:28 * P], allow_slow_non_contiguous=True).then_inc(s_in, 16)

            @block.vector
            def _(v):
                st = Steps(v, s_own)
                st.did(v.memset(eps[:], BN_EPS))
                for a in range(4):
                    for b in range(4):
                        st.did(v.tensor_copy(gath[a * D:(a + 1) * D, b * D:(b + 1) * D], K.ident[a * D:(a + 1) * D, a * D:(a + 1) * D]))
                for n in range(2):
                    st.did(v.tensor_reduce(row[:, n:n + 1], sums[:, n, :].rearrange("p (t g) -> p g t", g=G7)[:, 0, :], AX.X, ALU.add))
                st.settle()
                v.sem_inc(s_g, 1)
                v.wait_ge(s_t, 1)
                st.step(v.tensor_copy(col[:], ps[:]))
                v.wait_ge(s_in, 192)
                bn_coefficients(v, st, s_a, s_b, col[:, 0:1], col[:, 1:2], c[:, 2:3], c[:, 0:1], c[:, 1:2], coef[:, 0:1], coef[:, 1:2], c[:, 3:4], eps)

            @block.tensor
            def _(pe):
                pe.wait_ge(s_g, 1)
                pe.matmul(ps[:], gath[:], row[:], start=True, stop=True).then_inc(s_t, 1)

            @block.scalar
            def _(act):
                act.wait_ge(s_a, 1)
                act.activation(c[:, 3:4], c[:, 3:4], ACT.Sqrt, bias=eps[:, 0:1]).then_inc(s_b, 1)


def last_sums(nc, K, O, yT, coef, out):
    G7, NCH = CB // 16, EC // CB
    with phase(nc, "r") as ph:
        yi = [ph.sb(f"yi{k}", [P, 28 * P]) for k in range(2)]
        acc = [ph.sb(f"acc{k}", [P, CB, D]) for k in range(2)]
        pt = [ph.ps(f"pt{k}", [P, 512]) for k in range(2)]
        s_in, s_used, s_r, s_acc, s_out, s_free = ([ph.sem(f"{x}{k}") for k in range(2)] for x in ("in", "used", "r", "acc", "out", "free"))
        s_t, s_c, s_own = ph.sem("t"), ph.sem("c"), ph.sem("own")
        pairs = NCH // 2
        with nc.Block() as block:

            @block.sync
            def _(sp):
                with sp.Fori(0, pairs) as i:
                    for k in range(2):
                        sp.wait_ge(s_used[k], i + 1)
                        sp.dma_start(yi[k][:], yT[bass.ds((i * 2 + k) * P, P), :]).then_inc(s_in[k], 16)

            @block.scalar
            def _(act):
                with act.Fori(0, pairs) as i:
                    for k in range(2):
                        act.wait_ge(s_in[k], 16 * i + 16)
                        act.activation(yi[k][:], yi[k][:], ACT.Relu, bias=coef[:, 1:2], scale=coef[:, 0:1]).then_inc(s_r[k], 1)

            @block.tensor
            def _(pe):
                for k in range(2):
                    pe.sem_inc(s_used[k], 1)
                with pe.Fori(0, pairs) as i:
                    for k in range(2):
                        pe.wait_ge(s_r[k], i + 1)
                        for g in range(G7):
                            n = i * (2 * G7) + k * G7 + g
                            b = (k * G7 + g) % 2
                            pe.wait_ge(s_c, n + 1)
                            for m in range(4):
                                mm = pe.transpose(pt[b][:, m * P:(m + 1) * P], yi[k][:, (4 * g + m) * P:(4 * g + m + 1) * P], K.ident[:])
                            mm.then_inc(s_t, 1)
                        pe.wait_ge(s_t, i * (2 * G7) + (k + 1) * G7)
                        pe.sem_inc(s_used[k], 1)

            @block.vector
            def _(v):
                st = Steps(v, s_own)
                v.sem_inc(s_c, 2)
                st.step(v.memset(acc[1][:, CB - 1, :], 0.0))
                with v.Fori(0, pairs) as i:
                    st.loop(i, 2 * D)
                    for k in range(2):
                        v.wait_ge(s_free[k], i + 1)
                        af = acc[k][:].rearrange("p c w -> p (c w)")
                        for g in range(G7):
                            v.wait_ge(s_t, i * (2 * G7) + k * G7 + g + 1)
                            v.tensor_copy(af[:, g * 512:(g + 1) * 512], pt[(k * G7 + g) % 2][:]).then_inc(s_c, 1)
                        v.wait_ge(s_c, i * (2 * G7) + (k + 1) * G7 + 2)
                        for c in range(D):
                            st.did(v.tensor_tensor_scan(acc[k][:, :, c], O.keep[:, bass.ds((i * 2 + k) * CB, CB)], acc[k][:, :, c],
                                                        acc[1 - k][:, CB - 1, c:c + 1], ALU.mult, ALU.add))
                        st.settle()
                        v.sem_inc(s_acc[k], 1)
                    st.end_loop(pairs)
                st.step(v.tensor_copy(K.ends[:, 0:D], acc[1][:, CB - 1, :]))

            @block.gpsimd
            def _(g_):
                for k in range(2):
                    g_.sem_inc(s_free[k], 1)
                with g_.Fori(0, pairs) as i:
                    for k in range(2):
                        g_.wait_ge(s_acc[k], i + 1)
                        g_.nop(nofuse=True)
                        g_.dma_start(out[0:EP, :].rearrange("(p c) w -> p (c w)", p=P)[:, bass.ds((i * 2 + k) * (CB * D), CB * D)],
                                     acc[k][:].rearrange("p c w -> p (c w)")).then_inc(s_out[k], 16)
                        g_.wait_ge(s_out[k], 16 * i + 16)
                        g_.sem_inc(s_free[k], 1)



def safe_reciprocal(v, st, O, den, out, W):
    has = O.has[:].unsqueeze(2).to_broadcast([P, NC_, W])
    st.step(v.tensor_tensor(out, den, has, ALU.mult))
    st.step(v.tensor_tensor(out, out, has, ALU.subtract))
    st.step(v.tensor_scalar(out, out, 1.0, None, ALU.add))
    st.step(v.reciprocal(out, out))
    st.step(v.tensor_tensor(out, out, has, ALU.mult))


class BlockProduct:

    def __init__(self, ph, K, wide, M, out_fn):
        self.ph, self.K, self.wide, self.M, self.out_fn = ph, K, wide, M, out_fn
        self.pt = [ph.ps(f"bp_pt{k}", [P, P]) for k in range(2)]
        self.po = [ph.ps(f"bp_po{k}", [P, 4 * M]) for k in range(2)]
        self.hT = [ph.sb(f"bp_hT{k}", [P, P]) for k in range(2)]
        self.s_t, self.s_c, self.s_o, self.s_e = (ph.sem(f"bp_{x}") for x in "tcoe")

    def tensor(self, pe):
        S = self
        H = S.K.H[:].rearrange("p c d -> p (c d)")
        for b in range(NB + 1):
            if b < NB:
                if b >= 2:
                    pe.wait_ge(S.s_c, b - 1)
                pe.transpose(S.pt[b % 2][:], H[:, b * P:(b + 1) * P], S.K.ident[:]).then_inc(S.s_t, 1)
            if b >= 1:
                pe.wait_ge(S.s_c, b)
                if b >= 3:
                    pe.wait_ge(S.s_e, b - 2)
                pe.matmul(S.po[(b - 1) % 2][:], S.hT[(b - 1) % 2][:], S.wide[:], start=True, stop=True).then_inc(S.s_o, 1)

    def scalar(self, act):
        S = self
        for b in range(NB):
            act.wait_ge(S.s_t, b + 1)
            if b >= 2:
                act.wait_ge(S.s_o, b - 1)
            act.copy(S.hT[b % 2][:], S.pt[b % 2][:]).then_inc(S.s_c, 1)

    def vector(self, v):
        S = self
        for b in range(NB):
            v.wait_ge(S.s_o, b + 1)
            n = min(4, NC_ - 4 * b)
            S.out_fn(v, b, n, S.po[b % 2][:].rearrange("p (c m) -> p c m", m=S.M)[:, 0:n, :]).then_inc(S.s_e, 1)
        v.wait_ge(S.s_e, NB)


def node1(nc, K, R):
    with phase(nc, "n1") as ph:
        rec = ph.sb("rec", [P, NC_, 1])
        w = ph.sb("w", [P, HEADS, D])
        fw, fb = ph.sb("fw", [P, 2 * D]), ph.sb("fb", [P, 1])
        prod = ph.sb("prod", [P, HEADS, D])
        V = ph.sb("V", [P, 2, HEADS])
        wide = ph.sb("wide", [P, 4 * 8])
        s_w, s_h, s_wide = ph.sem("w"), ph.sem("h"), ph.sem("wide")
        sems = ph.sem("own"), ph.sem("var"), ph.sem("std")
        vec, sca = layernorm(None, None, ph, K, sems)

        def out_fn(v, b, n, po):
            v.tensor_scalar(K.b1[:, 4 * b:4 * b + n, :], po[:, :, 0:HEADS], fb[:, 0:1], None, ALU.add).then_inc(s_h, 1)
            return v.tensor_copy(K.t1[:, 4 * b:4 * b + n, D:D + HEADS], po[:, :, HEADS:8])

        bp = BlockProduct(ph, K, wide, 8, out_fn)
        with nc.Block() as block:

            @block.sync
            def _(sp):
                for c in range(4):
                    sp.dma_start(w[c * D:(c + 1) * D, :, :], K.in_w.rearrange("h f o -> f h o")).then_inc(s_w, 16)
                sp.dma_start(fw[:], K.in_fw.rearrange("a b -> (a b)").partition_broadcast(P)).then_inc(s_w, 16)
                sp.dma_start(fb[:], K.in_fb.partition_broadcast(P)).then_inc(s_w, 16)

            @block.vector
            def _(v):
                st = Steps(v, sems[0])
                st.did(v.memset(wide[:], 0.0))
                v.wait_ge(s_w, 96)
                for s in range(2):
                    f = fw[:, s * D:(s + 1) * D].unsqueeze(1).to_broadcast([P, HEADS, D])
                    st.step(v.tensor_tensor(prod[:], w[:], f, ALU.mult))
                    st.step(v.tensor_reduce(V[:, s, :], prod[:], AX.X, ALU.add))
                for c in range(4):
                    st.step(v.tensor_copy(wide[c * D:(c + 1) * D, c * 8:(c + 1) * 8], V[c * D:(c + 1) * D, :, :].rearrange("p s h -> p (s h)")))
                safe_reciprocal(v, st, K.o_d, R[:, :, D:D + 1], rec[:], 1)
                st.step(v.tensor_tensor(R[:, :, 0:D], R[:, :, 0:D], rec[:].to_broadcast([P, NC_, D]), ALU.mult))
                X = K.X[:].rearrange("p (c d) -> p c d", d=D)
                st.step(v.tensor_tensor(X, X, R[:, :, 0:D], ALU.add))
                vec(v, st)
                v.sem_inc(s_wide, 1)
                st.did(v.tensor_copy(K.t1[:, :, 0:D], K.H[:, 0:NC_, :]))
                bp.vector(v)
                v.wait_ge(s_h, NB)
                st.settle()

            @block.scalar
            def _(act):
                sca(act)
                bp.scalar(act)

            @block.tensor
            def _(pe):
                pe.wait_ge(s_wide, 1)
                bp.tensor(pe)


def node2(nc, K, R):
    with phase(nc, "n2") as ph:
        rec = ph.sb("rec", [P, NC_, HEADS])
        w = ph.sb("w", [P, D])
        bias = ph.sb("bias", [P, D])
        nq = -(-NC_ // 4)
        sT = [ph.sb(f"sT{k}", [P, 4, P]) for k in range(2)]
        pt = [ph.ps(f"pt{k}", [P, 4, P]) for k in range(2)]
        po = [ph.ps(f"po{k}", [P, 4, D]) for k in range(2)]
        s_w, s_r, s_t, s_c, s_o, s_x = (ph.sem(x) for x in ("w", "r", "t", "c", "o", "x"))
        sems = ph.sem("own"), ph.sem("var"), ph.sem("std")
        vec, sca = layernorm(None, None, ph, K, sems)
        with nc.Block() as block:

            @block.sync
            def _(sp):
                sp.dma_start(w[:], K.in_w.rearrange("h f o -> (h f) o")).then_inc(s_w, 16)
                sp.dma_start(bias[:], K.in_bias.partition_broadcast(P)).then_inc(s_w, 16)

            @block.vector
            def _(v):
                st = Steps(v, sems[0])
                safe_reciprocal(v, st, K.o_s, R[:, :, HEADS * D:], rec[:], HEADS)
                st.step(v.tensor_scalar(rec[:], rec[:], 1.0 / HEADS, None, ALU.mult))
                for h in range(HEADS):
                    st.did(v.tensor_tensor(R[:, :, h * D:(h + 1) * D], R[:, :, h * D:(h + 1) * D],
                                           rec[:, :, h:h + 1].to_broadcast([P, NC_, D]), ALU.mult))
                v.wait_ge(s_w, 32)
                X = K.X[:].rearrange("p (c d) -> p c d", d=D)
                st.did(v.tensor_tensor(X, X, bias[:].unsqueeze(1).to_broadcast([P, NC_, D]), ALU.add))
                st.settle()
                v.sem_inc(s_r, 1)
                for q in range(nq):
                    n = min(4, NC_ - 4 * q)
                    v.wait_ge(s_o, q + 1)
                    v.tensor_tensor(X[:, 4 * q:4 * q + n, :], X[:, 4 * q:4 * q + n, :], po[q % 2][:, 0:n, :], ALU.add).then_inc(s_x, 1)
                v.wait_ge(s_x, nq)
                vec(v, st)

            @block.tensor
            def _(pe):
                pe.wait_ge(s_r, 1)
                pe.wait_ge(s_w, 32)
                for q in range(nq + 1):
                    if q < nq:
                        if q >= 2:
                            pe.wait_ge(s_c, q - 1)
                        for c in range(min(4, NC_ - 4 * q)):
                            t = pe.transpose(pt[q % 2][:, c, :], R[:, 4 * q + c, 0:P], K.ident[:])
                        t.then_inc(s_t, 1)
                    if q >= 1:
                        pe.wait_ge(s_c, q)
                        if q >= 3:
                            pe.wait_ge(s_x, q - 2)
                        for c in range(min(4, NC_ - 4 * (q - 1))):
                            t = pe.matmul(po[(q - 1) % 2][:, c, :], sT[(q - 1) % 2][:, c, :], w[:], start=True, stop=True)
                        t.then_inc(s_o, 1)

            @block.scalar
            def _(act):
                for q in range(nq):
                    n = min(4, NC_ - 4 * q)
                    act.wait_ge(s_t, q + 1)
                    if q >= 2:
                        act.wait_ge(s_o, q - 1)
                    act.copy(sT[q % 2][:, 0:n, :], pt[q % 2][:, 0:n, :]).then_inc(s_c, 1)
                sca(act)


def add_sums(v, st, K, O, R):
    X = K.X[:].rearrange("p (c d) -> p c d", d=D)
    st.step(v.tensor_tensor(R, R, O.has[:].unsqueeze(2).to_broadcast([P, NC_, D]), ALU.mult))
    st.step(v.tensor_tensor(X, X, R, ALU.add))


def node3(nc, K, R):
    with phase(nc, "n3") as ph:
        b1 = ph.sb("b1", [P, D])
        wide = ph.sb("wide", [P, 4 * 2 * D])
        s_w, s_h, s_wide, s_z = ph.sem("w"), ph.sem("h"), ph.sem("wide"), ph.sem("z")
        sems = ph.sem("own"), ph.sem("var"), ph.sem("std")
        vec, sca = layernorm(None, None, ph, K, sems)

        def out_fn(v, b, n, po):
            v.tensor_copy(K.tA[:, 4 * b:4 * b + n, :], po[:, :, 0:D]).then_inc(s_h, 1)
            return v.tensor_tensor(K.tB[:, 4 * b:4 * b + n, :], po[:, :, D:2 * D],
                                   b1[:].unsqueeze(1).to_broadcast([P, n, D]), ALU.add)

        bp = BlockProduct(ph, K, wide, 2 * D, out_fn)
        with nc.Block() as block:

            @block.sync
            def _(sp):
                sp.wait_ge(s_z, 1)
                for c in range(4):
                    for s in range(2):
                        sp.dma_start(wide[c * D:(c + 1) * D, (2 * c + s) * D:(2 * c + s + 1) * D],
                                     K.in_M1[s * D:(s + 1) * D, :]).then_inc(s_w, 16)
                sp.dma_start(b1[:], K.in_b1.partition_broadcast(P)).then_inc(s_w, 16)

            @block.vector
            def _(v):
                st = Steps(v, sems[0])
                v.memset(wide[:], 0.0).then_inc(s_z, 1)
                add_sums(v, st, K, K.o_d, R)
                vec(v, st)
                v.sem_inc(s_wide, 1)
                v.wait_ge(s_w, 144)
                bp.vector(v)
                v.wait_ge(s_h, NB)

            @block.scalar
            def _(act):
                sca(act)
                bp.scalar(act)

            @block.tensor
            def _(pe):
                pe.wait_ge(s_wide, 1)
                pe.wait_ge(s_w, 144)
                bp.tensor(pe)


def finish(nc, K, R):
    with phase(nc, "fin") as ph:
        s_own, s_x, s_out = ph.sem("own"), ph.sem("x"), ph.sem("out")
        with nc.Block() as block:

            @block.vector
            def _(v):
                st = Steps(v, s_own)
                add_sums(v, st, K, K.o_s, R)
                v.sem_inc(s_x, 1)

            @block.sync
            def _(sp):
                sp.wait_ge(s_x, 1)
                rows = N // NC_
                of = K.out.rearrange("n d -> (n d)")
                for a, b in ((0, 112), (112, rows)):
                    sp.dma_start(of[a * NC_ * D:b * NC_ * D].rearrange("(p f) -> p f", p=b - a), K.X[a:b, :]).then_inc(s_out, 16)
                sp.dma_start(of[rows * NC_ * D:N * D].rearrange("(p f) -> p f", p=1),
                             K.X[rows:rows + 1, 0:(N - rows * NC_) * D]).then_inc(s_out, 16)
                sp.wait_ge(s_out, 48)


def program(nc, args, out, stop=99):
    K = Kit()
    (K.in_x, K.in_src, K.in_dst, K.in_emb, K.in_vec, K.in_nrm, K.in_aw, K.in_w, K.in_fw, K.in_fb, K.in_bias,
     K.in_W1, K.in_W2, K.in_M1, K.in_b1, K.in_g1, K.in_be1, K.in_M2, K.in_b2, K.in_g2, K.in_be2) = args
    K.out = out

    def dram(name, shape, dt=F32):
        return nc.dram_tensor(name, shape, dt).ap()

    K.src, K.dst = dram("src_pad", (EP,), I32), dram("dst_pad", (EP,), I32)
    K.emb, K.vec, K.nrm = dram("emb_pad", (EP * 10,)), dram("vec_pad", (EP * 3,)), dram("nrm_pad", (EP,))
    K.key_rows, K.hi_rows = dram("key_rows", (EP,)), dram("hi_rows", (EP,), BF16)
    K.start_s, K.end_s, K.start_d, K.end_d = (dram(x, (NN,)) for x in ("start_s", "end_s", "start_d", "end_d"))
    K.table0 = dram("table0_rows", (NN, 33))
    K.rows0 = dram("rows0", (EP * 33,))
    K.zeroed = []
    with ExitStack() as res:
        def sb(name, shape, dt=F32):
            return res.enter_context(nc.sbuf_tensor(name, shape, dt))

        K.ident, K.tri, K.lane = sb("ident", [P, P]), sb("tri", [P, P]), sb("lane", [P, P])
        K.lane_b, K.lane_i = sb("lane_b", [P, P], BF16), sb("lane_i", [P, P], I32)
        K.pcol, K.pcol_i = sb("pcol", [P, 1]), sb("pcol_i", [P, 1], I32)
        K.X, K.H = sb("X", [P, NC_ * D]), sb("H", [P, 4 * NB, D])
        K.b0 = sb("b0", [P, NC_])
        K.b1 = sb("b1", [P, NC_, HEADS])
        K.keep_d, K.keep_s = sb("keep_d", [P, EC]), sb("keep_s", [P, EC])
        K.src_f = sb("src_f", [P, EC])
        K.ends = sb("ends", [P, 33 * HEADS])
        K.init = sb("init", [P, 36])
        K.o_d, K.o_s = Order(sb, "od", K.keep_d), Order(sb, "os", K.keep_s)
        rowsM1, rowsM4 = dram("rowsM1", (EP + P, 1)), dram("rowsM4", (EP + P, HEADS))
        rowsS1, rowsS4 = dram("rowsS1", (EP + P, 33)), dram("rowsS4", (EP + P, 33 * HEADS))
        rowsS2 = dram("rowsS2", (EP + P, D))
        fill_d2, fill_d36, fill_d32 = dram("fill_d2", (EP + NN, 2)), dram("fill_d36", (EP + NN, D + HEADS)), dram("fill_d32", (EP + NN, D))
        fill_s8, fill_s32 = dram("fill_s8", (EP + NN, 2 * HEADS)), dram("fill_s32", (EP + NN, D))
        tab2, tab36, tab32, tab8 = dram("tab2", (NN, 2)), dram("tab36", (NN, D + HEADS)), dram("tab32", (NN, D)), dram("tab8", (NN, 2 * HEADS))
        tabA = dram("tabA", (NN, D))
        perm1, perm3 = dram("perm1", (EP, D + HEADS + 1)), dram("perm3", (EP, D))
        K.pos_i = dram("pos_i", (EP,), I32)
        tabB, zrows, yrows = dram("tabB", (NN, D)), dram("zrows", (EP, D)), dram("yrows", (EC // CB * P, 28 * P))
        rowsS3 = dram("rowsS3", (EP + P, D))
        flat = lambda a: a.rearrange("a b -> (a b)")
        K.zeroed = [flat(a) for a in (fill_d2, fill_d36, fill_d32, fill_s8, fill_s32)]
        K.zeroed += [flat(a[EP:EP + P, :]) for a in (rowsM1, rowsM4, rowsS1, rowsS4, rowsS2, rowsS3)]

        with ExitStack() as lay:
            def lsb(name, shape, dt=F32):
                return lay.enter_context(nc.sbuf_tensor(name, shape, dt))

            K.a0 = lsb("a0", [P, EC])
            with ExitStack() as srt:
                def ssb(name, shape, dt=F32):
                    return srt.enter_context(nc.sbuf_tensor(name, shape, dt))

                K.pos, K.dst_f, K.start_s_sb = ssb("pos", [P, EC]), ssb("dst_f", [P, EC]), ssb("start_s_sb", [HI, P])
                K.src_hi, K.src_lo, K.dst_hi, K.dst_lo = (ssb(x, [P, EC], BF16) for x in ("src_hi", "src_lo", "dst_hi", "dst_lo"))
                setup(nc, K)
                load_keys(nc, K)
                table0(nc, K)
                sort_and_gather(nc, K)
                store_pos(nc, K)
            places(nc, K, K.o_d, K.start_d, K.end_d)
            places(nc, K, K.o_s, K.start_s, K.end_s)
            carries(nc, K, K.o_d)

            ex, top, f2, R = lsb("l0_ex", [P, 1, EC]), lsb("l0_top", [P, NC_, 1]), lsb("l0_f2", [P, NC_, 2]), lsb("l0_R", [P, NC_, 33])
            a0 = K.a0[:].unsqueeze(1)
            max_scan(nc, K, "mx0", K.o_d, a0, rowsM1, 1, K.ends[:, 0:1])
            mend_and_read(nc, K, "mr0", K.o_d, rowsM1, 1, K.ends[:, 0:1], ALU.max, top[:])
            bound(nc, K, "bd0", K.b0[:].unsqueeze(2), top[:], f2[:], 1, 0.01)
            put_starts(nc, K, "ps0", K.o_d, f2[:], 2, fill_d2, tab2, K.init[:, 0:2])
            exponentials(nc, K, "ex0", K.o_d, a0, fill_d2, K.init[:, 0:2], 1, 0.01, ex[:])
            weighted_sums(nc, K, "ws0", K.o_d, K.rows0, 33, ex[:], 1, rowsS1, 196)
            mend_and_read(nc, K, "ms0", K.o_d, rowsS1, 33, K.ends[:, 0:33], ALU.add, R[:])
            with ExitStack() as two:
                K.t1 = two.enter_context(nc.sbuf_tensor("t1", [P, NC_, D + HEADS], F32))
                node1(nc, K, R)
                put_starts(nc, K, "ps1", K.o_d, K.t1[:], D + HEADS, fill_d36, tab36, K.init[:])
        if stop < 1:
            return K
        permute(nc, K, "pm1", K.o_d, fill_d36, K.init[:], D + HEADS, D + HEADS + 1, perm1)
        with ExitStack() as lay:
            def lsb(name, shape, dt=F32):
                return lay.enter_context(nc.sbuf_tensor(name, shape, dt))
            vals = lsb("l1_vals", [P, HEADS, EC])
            unpack(nc, K, perm1, D + HEADS + 1, vals[:])
            carries(nc, K, K.o_s)
            with ExitStack() as two:
                top = two.enter_context(nc.sbuf_tensor("l1_top", [P, NC_, HEADS], F32))
                f8 = two.enter_context(nc.sbuf_tensor("l1_f8", [P, NC_, 2 * HEADS], F32))
                max_scan(nc, K, "mx1", K.o_s, vals[:], rowsM4, HEADS, K.ends[:, 0:HEADS])
                mend_and_read(nc, K, "mr1", K.o_s, rowsM4, HEADS, K.ends[:, 0:HEADS], ALU.max, top[:])
                bound(nc, K, "bd1", K.b1[:], top[:], f8[:], HEADS, 0.2)
                put_starts(nc, K, "ps1b", K.o_s, f8[:], 2 * HEADS, fill_s8, tab8, K.init[:, 0:2 * HEADS])
            exponentials(nc, K, "ex1", K.o_s, vals[:], fill_s8, K.init[:, 0:2 * HEADS], HEADS, 0.2, vals[:])
            weighted_sums(nc, K, "ws1", K.o_s, flat(perm1), D + HEADS + 1, vals[:], HEADS, rowsS4, 98)
        with ExitStack() as lay:
            R = lay.enter_context(nc.sbuf_tensor("l1_R", [P, NC_, 33 * HEADS], F32))
            mend_and_read(nc, K, "ms1", K.o_s, rowsS4, 33 * HEADS, K.ends[:], ALU.add, R[:])
            node2(nc, K, R)
        if stop < 2:
            return K
        with ExitStack() as lay:
            def lsb(name, shape, dt=F32):
                return lay.enter_context(nc.sbuf_tensor(name, shape, dt))
            put_starts(nc, K, "ps2", K.o_d, K.H[:, 0:NC_, :], D, fill_d32, tab32, K.init[:, 0:D])
            wall, nv, gain = lsb("wall", [FW, NOUT * KH + KH]), lsb("nv", [P, EC, 3]), lsb("gain", [P, EC])
            edge_weights(nc, K, wall)
            unit_vectors(nc, K, nv[:], gain[:])
            edge_network(nc, K, K.o_d, tab32, fill_d32, K.init[:, 0:D], wall, nv[:], gain[:], rowsS2)
        with ExitStack() as lay:
            def lsb(name, shape, dt=F32):
                return lay.enter_context(nc.sbuf_tensor(name, shape, dt))
            R = lsb("l2_R", [P, NC_, D])
            mend_and_read(nc, K, "ms2", K.o_d, rowsS2, D, K.ends[:, 0:D], ALU.add, R[:])
            K.tA, K.tB = lsb("tA", [P, NC_, D]), lsb("tB", [P, NC_, D])
            node3(nc, K, R[:])
            put_starts(nc, K, "psB", K.o_d, K.tB[:], D, fill_d32, tabB, K.init[:, 0:D])
            permute(nc, K, "pm3", K.o_d, fill_d32, K.init[:, 0:D], D, D, perm3)
            put_starts(nc, K, "psA", K.o_s, K.tA[:], D, fill_s32, tabA, K.init[:, 0:D])
        if stop < 3:
            return K
        with ExitStack() as lay:
            def lsb(name, shape, dt=F32):
                return lay.enter_context(nc.sbuf_tensor(name, shape, dt))
            stats, coef, sums = lsb("stats", [1, 2, 448]), lsb("coef", [P, 4]), lsb("sums", [P, 2, EC // 16])
            first_sums(nc, K, K.o_s, fill_s32, K.init[:, 0:D], perm3, zrows, stats[:])
            norm1(nc, K, stats[:], zrows, coef[:, 0:2])
            second_product(nc, K, zrows, coef[:, 0:2], yrows, sums[:])
            norm2(nc, K, sums[:], yrows, coef[:, 2:4])
            last_sums(nc, K, K.o_s, yrows, coef[:, 2:4], rowsS3)
            R = lsb("l3_R", [P, NC_, D])
            mend_and_read(nc, K, "ms3", K.o_s, rowsS3, D, K.ends[:, 0:D], ALU.add, R[:])
            finish(nc, K, R[:])
    return K


_INS = ["x", "src", "dst", "edge_attr_10", "edge_attr_3", "edge_weight", "L0_gnn_attn_w", "L1_gnn_w", "L1_gnn_fc_w",
        "L1_gnn_fc_b", "L1_gnn_bias", "L2_gnn_W1", "L2_gnn_W2", "L3_gnn_W1", "L3_gnn_b1", "L3_gnn_gamma1",
        "L3_gnn_beta1", "L3_gnn_W2", "L3_gnn_b2", "L3_gnn_gamma2", "L3_gnn_beta2"]


def kernel(**inputs):
    import numpy as _np
    import concourse.bacc as _bacc
    from concourse import mybir as _mybir
    from concourse.bass_utils import run_bass_kernel_spmd as _run

    nc = _bacc.Bacc("TRN2", target_bir_lowering=False, num_devices=1)
    arrays, args = {}, []
    for name in _INS:
        a = _np.ascontiguousarray(inputs[name])
        arrays[f"in_{name}_dram"] = a
        args.append(nc.dram_tensor(f"in_{name}_dram", a.shape, _mybir.dt.from_np(a.dtype), kind="ExternalInput").ap())
    out = nc.dram_tensor("out_0_dram", (N, D), F32, kind="ExternalOutput").ap()
    program(nc, args, out)
    r = _run(nc, [arrays], core_ids=[0])
    return r.results[0]["out_0_dram"]
```
